# Optimizing a Trainium2 kernel written in Bass

```python
import numpy as np
import jax
import jax.numpy as jnp

def _softmax(x, axis=-1):
    return jax.nn.softmax(x, axis=axis)

def _gelu(x):
    return jax.nn.gelu(x, approximate=True)

def _silu(x):
    return jax.nn.silu(x)

def _sigmoid(x):
    return jax.nn.sigmoid(x)

def _layernorm(x, axis=-1, eps=1e-05):
    m = jnp.mean(x, axis=axis, keepdims=True)
    v = jnp.var(x, axis=axis, keepdims=True)
    return (x - m) / jnp.sqrt(v + eps)

def _scatter_add(tgt, idx, src, axis=0):
    return tgt.at[idx].add(src)

def _segment_sum(src, seg, n):
    return jax.ops.segment_sum(src, seg, n)
kernel_name = 'mk_gnn_preln_d4_gnn_r32_9d2876'

def setup_inputs(seed: int=0):
    np.random.seed(seed)
    _w = jnp.asarray

    def _rec_inputs():
        import jax
        import jax.numpy as jnp
        _gk = jax.random.key(seed)
        x = -0.0009044 + 1 * jax.random.normal(jax.random.fold_in(_gk, 1), (3125, 16), jnp.float32)
        _s = jax.random.randint(jax.random.fold_in(_gk, 2), (50000,), 0, 3125, jnp.int32)
        _d = jax.random.randint(jax.random.fold_in(_gk, 3), (50000,), 0, 3125, jnp.int32)
        _loop = jnp.arange(3125, dtype=jnp.int32)
        src = jnp.concatenate([_s, _d, _loop])
        dst = jnp.concatenate([_d, _s, _loop])
        _o = jnp.argsort(dst, stable=True)
        src = src[_o]
        dst = dst[_o]
        edge_attr_16 = -0.00010739 + 0.99994 * jax.random.normal(jax.random.fold_in(_gk, 12), (103125, 16), jnp.float32)
        edge_attr_2 = -0.000290007 + 0.69988 * jax.random.normal(jax.random.fold_in(_gk, 13), (103125, 2), jnp.float32)
        edge_attr_8 = -5.3897e-05 + 0.999841 * jax.random.normal(jax.random.fold_in(_gk, 14), (103125, 8), jnp.float32)
        edge_type_90 = jax.random.randint(jax.random.fold_in(_gk, 16), (103125,), 0, 90, jnp.int32)
        node_vec1 = -0.00472126 + 0.997171 * jax.random.normal(jax.random.fold_in(_gk, 17), (3125, 1), jnp.float32)
        return (x, src, dst, edge_attr_16, edge_attr_2, edge_attr_8, edge_type_90, node_vec1)
    x, src, dst, edge_attr_16, edge_attr_2, edge_attr_8, edge_type_90, node_vec1 = _rec_inputs()

    def _L0_gnn_setup():
        import jax, jax.numpy as jnp
        import numpy as np
        N_NODES = 3125
        N_EDGES = 25000
        F_IN = 16
        F_OUT = 16
        NB = 4
        OUTPUT_SCALING = 1.0 / 128.0

        def hat_basis(u, n):
            centers = jnp.linspace(-1.0, 1.0, n, dtype=u.dtype)
            width = 2.0 / (n - 1)
            return jnp.maximum(0.0, 1.0 - jnp.abs(u[:, None] - centers[None, :]) / width)
        key = jax.random.key(seed)
        k1, k2, k3, k4, k5 = jax.random.split(key, 5)
        x = jax.random.normal(k1, (N_NODES, F_IN), dtype=jnp.float32)
        edge_attr = jax.random.normal(k2, (N_EDGES, 2), dtype=jnp.float32) * 0.7
        W = jax.random.normal(k3, (NB * NB, F_IN, F_OUT), dtype=jnp.float32) * (1.0 / np.sqrt(34.0) * np.sqrt(2.0 / (F_IN + F_OUT)))
        edge_index_i = jax.random.randint(k4, (N_EDGES,), 0, N_NODES, dtype=jnp.int64)
        edge_index_j = jax.random.randint(k5, (N_EDGES,), 0, N_NODES, dtype=jnp.int64)
        return {'x': x, 'edge_attr': edge_attr, 'W': W, 'edge_index_i': edge_index_i, 'edge_index_j': edge_index_j}
    _L0_gnn_all = _L0_gnn_setup()
    _L0_gnn_in = {k: v for k, v in _L0_gnn_all.items() if k in ('W',)}
    del _L0_gnn_all

    def _L1_gnn_setup():
        import jax, jax.numpy as jnp
        import numpy as np
        N = 3125
        E = 100000
        F = 16

        def _gcn(x, W, b, src, dst, norm, n):
            h = x @ W
            msg = h[src] * norm[:, None]
            out = jax.ops.segment_sum(msg, dst, num_segments=n)
            return out + b
        key = jax.random.key(seed)
        ks = jax.random.split(key, 5)
        x = jax.random.normal(ks[0], (N, F), dtype=jnp.float32)
        edge_index = jax.random.randint(ks[1], (2, E), 0, N)
        W1 = jax.random.normal(ks[2], (5, F, 64), dtype=jnp.float32) * (1.0 / np.sqrt(F))
        W2 = jax.random.normal(ks[3], (5, 64, 32), dtype=jnp.float32) * (1.0 / np.sqrt(64))
        W3 = jax.random.normal(ks[4], (5, 32, F), dtype=jnp.float32) * (1.0 / np.sqrt(32))
        b1 = jnp.zeros((5, 64), dtype=jnp.float32)
        b2 = jnp.zeros((5, 32), dtype=jnp.float32)
        b3 = jnp.zeros((5, F), dtype=jnp.float32)
        return {'x': x, 'edge_index': edge_index, 'W1': W1, 'b1': b1, 'W2': W2, 'b2': b2, 'W3': W3, 'b3': b3}
    _L1_gnn_all = _L1_gnn_setup()
    _L1_gnn_in = {k: v for k, v in _L1_gnn_all.items() if k in ('W1', 'b1', 'W2', 'b2', 'W3', 'b3')}
    del _L1_gnn_all

    def _L2_gnn_setup():
        import jax, jax.numpy as jnp
        import numpy as np
        N_NODES = 3125
        N_EDGES = 100000
        D_NODE = 16
        D_EDGE = 8
        D_HIDDEN = 16
        key = jax.random.key(seed)
        ks = jax.random.split(key, 8)
        node_features = jax.random.normal(ks[0], (N_NODES, D_NODE), dtype=jnp.float32)
        edge_attr_e3nn = jax.random.normal(ks[1], (N_EDGES, D_EDGE), dtype=jnp.float32)
        node_attr_scalar_raw = jax.random.normal(ks[2], (N_NODES, 1), dtype=jnp.float32)
        W_msg_tp = jax.random.normal(ks[3], (D_NODE, D_EDGE, D_HIDDEN), dtype=jnp.float32)
        W_msg_lin = jax.random.normal(ks[4], (D_HIDDEN, D_HIDDEN), dtype=jnp.float32)
        W_upd_tp = jax.random.normal(ks[5], (D_NODE, D_HIDDEN, D_HIDDEN), dtype=jnp.float32)
        W_upd_lin = jax.random.normal(ks[6], (D_HIDDEN, D_NODE), dtype=jnp.float32)
        edge_index = jax.random.randint(ks[7], (2, N_EDGES), 0, N_NODES, dtype=jnp.int64)
        return {'node_features': node_features, 'edge_attr_e3nn': edge_attr_e3nn, 'node_attr_scalar_raw': node_attr_scalar_raw, 'W_msg_tp': W_msg_tp, 'W_msg_lin': W_msg_lin, 'W_upd_tp': W_upd_tp, 'W_upd_lin': W_upd_lin, 'edge_index': edge_index}
    _L2_gnn_all = _L2_gnn_setup()
    _L2_gnn_in = {k: v for k, v in _L2_gnn_all.items() if k in ('W_msg_tp', 'W_msg_lin', 'W_upd_tp', 'W_upd_lin')}
    del _L2_gnn_all

    def _L3_gnn_setup():
        import jax, jax.numpy as jnp
        import numpy as np
        N, E, IN, OUT, R, B = (50000, 25000, 16, 16, 90, 30)
        key = jax.random.key(seed)
        ks = jax.random.split(key, 9)
        h = jax.random.normal(ks[0], (N, IN), dtype=jnp.float32)
        he = jax.random.normal(ks[1], (E, IN), dtype=jnp.float32)
        Ws = jax.random.normal(ks[2], (OUT, IN), dtype=jnp.float32) * 0.1
        Wa = jax.random.normal(ks[3], (1, 3 * OUT), dtype=jnp.float32) * 0.1
        weight = jax.random.normal(ks[4], (B, IN, OUT), dtype=jnp.float32) * 0.1
        w_comp = jax.random.normal(ks[5], (R, B), dtype=jnp.float32) * 0.1
        src = jax.random.randint(ks[6], (E,), 0, N)
        dst = jax.random.randint(ks[7], (E,), 0, N)
        rel_type = jax.random.randint(ks[8], (E,), 0, R)
        return {'h': h, 'he': he, 'Ws': Ws, 'Wa': Wa, 'weight': weight, 'w_comp': w_comp, 'src': src, 'dst': dst, 'rel_type': rel_type}
    _L3_gnn_all = _L3_gnn_setup()
    _L3_gnn_in = {k: v for k, v in _L3_gnn_all.items() if k in ('Ws', 'Wa', 'weight', 'w_comp')}
    del _L3_gnn_all
    return {'x': x, 'src': src, 'dst': dst, 'edge_attr_16': edge_attr_16, 'edge_attr_2': edge_attr_2, 'edge_attr_8': edge_attr_8, 'edge_type_90': edge_type_90, 'node_vec1': node_vec1, 'L0_gnn_W': _L0_gnn_in['W'], 'L1_gnn_W1': _L1_gnn_in['W1'], 'L1_gnn_b1': _L1_gnn_in['b1'], 'L1_gnn_W2': _L1_gnn_in['W2'], 'L1_gnn_b2': _L1_gnn_in['b2'], 'L1_gnn_W3': _L1_gnn_in['W3'], 'L1_gnn_b3': _L1_gnn_in['b3'], 'L2_gnn_W_msg_tp': _L2_gnn_in['W_msg_tp'], 'L2_gnn_W_msg_lin': _L2_gnn_in['W_msg_lin'], 'L2_gnn_W_upd_tp': _L2_gnn_in['W_upd_tp'], 'L2_gnn_W_upd_lin': _L2_gnn_in['W_upd_lin'], 'L3_gnn_Ws': _L3_gnn_in['Ws'], 'L3_gnn_Wa': _L3_gnn_in['Wa'], 'L3_gnn_weight': _L3_gnn_in['weight'], 'L3_gnn_w_comp': _L3_gnn_in['w_comp']}

def reference(x, src, dst, edge_attr_16, edge_attr_2, edge_attr_8, edge_type_90, node_vec1, L0_gnn_W, L1_gnn_W1, L1_gnn_b1, L1_gnn_W2, L1_gnn_b2, L1_gnn_W3, L1_gnn_b3, L2_gnn_W_msg_tp, L2_gnn_W_msg_lin, L2_gnn_W_upd_tp, L2_gnn_W_upd_lin, L3_gnn_Ws, L3_gnn_Wa, L3_gnn_weight, L3_gnn_w_comp):
    import jax
    import jax.numpy as jnp

    def _L0_gnn_ref(x, edge_attr, W, edge_index_i, edge_index_j):
        import jax, jax.numpy as jnp
        import numpy as np
        N_NODES = 3125
        N_EDGES = 25000
        F_IN = 16
        F_OUT = 16
        NB = 4
        OUTPUT_SCALING = 1.0 / 128.0

        def hat_basis(u, n):
            centers = jnp.linspace(-1.0, 1.0, n, dtype=u.dtype)
            width = 2.0 / (n - 1)
            return jnp.maximum(0.0, 1.0 - jnp.abs(u[:, None] - centers[None, :]) / width)
        mask = edge_index_i != edge_index_j
        mapped = jnp.clip(edge_attr, -1.0, 1.0)
        bx = hat_basis(mapped[:, 0], NB)
        by = hat_basis(mapped[:, 1], NB)
        basis = (bx[:, :, None] * by[:, None, :]).reshape(mapped.shape[0], NB * NB)
        xj = x[edge_index_j]
        u = jnp.einsum('ei,kio->eko', xj, W)
        msg = jnp.einsum('ek,eko->eo', basis, u)
        msg = jnp.where(mask[:, None], msg, jnp.zeros((), msg.dtype))
        out = jax.ops.segment_sum(msg, edge_index_i, num_segments=x.shape[0])
        return out * OUTPUT_SCALING

    def _L1_gnn_ref(x, edge_index, W1, b1, W2, b2, W3, b3):
        import jax, jax.numpy as jnp
        import numpy as np
        N = 3125
        E = 100000
        F = 16

        def _gcn(x, W, b, src, dst, norm, n):
            h = x @ W
            msg = h[src] * norm[:, None]
            out = jax.ops.segment_sum(msg, dst, num_segments=n)
            return out + b
        n = x.shape[0]
        loops = jnp.arange(n)
        src = jnp.concatenate([edge_index[0], loops])
        dst = jnp.concatenate([edge_index[1], loops])
        deg = jax.ops.segment_sum(jnp.ones(src.shape[0], jnp.float32), dst, num_segments=n)
        dis = jax.lax.rsqrt(jnp.maximum(deg, 1.0))
        norm = dis[src] * dis[dst]
        for i in range(5):
            x = jax.nn.relu(_gcn(x, W1[i], b1[i], src, dst, norm, n))
            x = jax.nn.relu(_gcn(x, W2[i], b2[i], src, dst, norm, n))
            x = jax.nn.softmax(_gcn(x, W3[i], b3[i], src, dst, norm, n), axis=1)
        return x

    def _L2_gnn_ref(node_features, edge_attr_e3nn, node_attr_scalar_raw, W_msg_tp, W_msg_lin, W_upd_tp, W_upd_lin, edge_index):
        import jax, jax.numpy as jnp
        import numpy as np
        N_NODES = 3125
        N_EDGES = 100000
        D_NODE = 16
        D_EDGE = 8
        D_HIDDEN = 16
        n_nodes = node_features.shape[0]
        row = edge_index[0]
        col = edge_index[1]
        norm_msg_tp = 1.0 / np.float32(np.sqrt(D_NODE * D_EDGE))
        norm_upd_tp = 1.0 / np.float32(np.sqrt(D_NODE * D_HIDDEN))
        norm_lin = 1.0 / np.float32(np.sqrt(D_HIDDEN))
        x_j = node_features[col]
        m = jnp.einsum('ei,ej,ijh->eh', x_j, edge_attr_e3nn, W_msg_tp) * norm_msg_tp
        m = jax.nn.silu(m)
        m = m @ W_msg_lin * norm_lin
        agg = jax.ops.segment_sum(m, row, num_segments=n_nodes)
        u = jnp.einsum('ni,nh,ihk->nk', node_features, agg, W_upd_tp) * norm_upd_tp
        u = jax.nn.silu(u)
        u = u @ W_upd_lin * norm_lin
        return node_features + u

    def _L3_gnn_ref(h, he, Ws, Wa, weight, w_comp, src, dst, rel_type):
        import jax, jax.numpy as jnp
        import numpy as np
        N, E, IN, OUT, R, B = (50000, 25000, 16, 16, 90, 30)
        n_nodes, in_dim = h.shape
        num_bases, _, out_dim = weight.shape
        num_rels = w_comp.shape[0]
        V = weight.reshape(in_dim, num_bases, out_dim)
        W_rel = jnp.matmul(w_comp, V).reshape(num_rels, in_dim, out_dim)
        h_src = h[src]
        z_src = h_src @ Ws.T
        z_dst = h[dst] @ Ws.T
        z_e = he @ Ws.T
        e = jnp.concatenate([z_src, z_e, z_dst], axis=1) @ Wa.T
        msg = jnp.einsum('ei,eio->eo', h_src, W_rel[rel_type]) * e
        h_out = jax.ops.segment_sum(msg, dst, num_segments=n_nodes)
        return h_out
    edge_index = jnp.stack([src, dst])
    h = jnp.maximum(_layernorm(x, axis=-1), 0.0)
    x = x + _L0_gnn_ref(h, edge_attr_2, L0_gnn_W, src, dst)
    h = jnp.maximum(_layernorm(x, axis=-1), 0.0)
    x = x + _L1_gnn_ref(h, edge_index, L1_gnn_W1, L1_gnn_b1, L1_gnn_W2, L1_gnn_b2, L1_gnn_W3, L1_gnn_b3)
    h = jnp.maximum(_layernorm(x, axis=-1), 0.0)
    x = x + _L2_gnn_ref(h, edge_attr_8, node_vec1, L2_gnn_W_msg_tp, L2_gnn_W_msg_lin, L2_gnn_W_upd_tp, L2_gnn_W_upd_lin, edge_index)
    h = jnp.maximum(_layernorm(x, axis=-1), 0.0)
    x = x + _L3_gnn_ref(h, edge_attr_16, L3_gnn_Ws, L3_gnn_Wa, L3_gnn_weight, L3_gnn_w_comp, src, dst, edge_type_90)
    return x

_drawn_inputs = setup_inputs


def setup_inputs(seed=0):
    import zlib

    import numpy as np

    out = dict(_drawn_inputs(seed))
    spreads = {'L1_gnn_b1': (0.0, 0.8), 'L1_gnn_b2': (0.0, 0.8), 'L1_gnn_b3': (0.0, 0.8)}
    factors = {'edge_attr_2': 8.0, 'L0_gnn_W': 8.0, 'L1_gnn_W1': 8.0, 'L1_gnn_W2': 8.0, 'L1_gnn_W3': 8.0}
    for name, (base, spread) in spreads.items():
        noise = np.random.default_rng([zlib.crc32(name.encode()), seed]).standard_normal(out[name].shape)
        drawn = base * np.exp(spread * noise) if base else spread * noise
        out[name] = jnp.asarray(drawn.astype(out[name].dtype))
    for name, factor in factors.items():
        out[name] = (out[name] * factor).astype(out[name].dtype)
    return out
```

```python
from contextlib import ExitStack

import numpy as np

import concourse.bass as bass
import concourse.mybir as mybir
from concourse.alu_op_type import AluOpType as ALU

ACT = mybir.ActivationFunctionType
AX = mybir.AxisListType
F32, BF16, F16, I32 = mybir.dt.float32, mybir.dt.bfloat16, mybir.dt.float16, mybir.dt.int32
BYTES = {F32: 4, I32: 4, BF16: 2, F16: 2}

P = 128
N, E, F = 3125, 103125, 16
NB = -(-N // P)
NP = NB * P
QS = 4
STEP = P * QS
NS = -(-E // STEP)
NC = NS * QS
HI, LO = 8, NP // 8
HALF = NP // 2
NR, NBASE = 90, 30
LAYERS, F1, F2 = 5, 64, 32
BANK = 512
CHUNKS = [(j * BANK, min(BANK, NP - j * BANK)) for j in range(-(-NP // BANK))]
NCH = len(CHUNKS)
EPS = 1e-5
GROW = F + 1
ENGINES = 5
TPP = NS // 2


def gnn(nc, x_in, src_in, dst_in, dstrow_in, type_in, attr2_in, attr8_in, attr16_in, w0_in,
        w1_in, b1_in, w2_in, b2_in, w3_in, b3_in, wmt_in, wml_in, wut_in, wul_in, ws_in, wa_in,
        wv_in, wct_in, out):
    range_dram = nc.dram_tensor("step_range", (2, NS), F32, kind="Internal").ap()
    table_dram = nc.dram_tensor("block_steps", (NB, 4), I32, kind="Internal").ap()
    rel_dram = nc.dram_tensor("relation_weights", (F * NR * F,), F32, kind="Internal").ap()
    node_dram = nc.dram_tensor("node_rows", (NP, GROW), F32, kind="Internal").ap()

    with ExitStack() as ctx:
        def sb(name, shape, dt):
            return ctx.enter_context(nc.sbuf_tensor(name, shape, dt))

        def sem(name):
            return ctx.enter_context(nc.semaphore(name))

        def shaped(ap, shape):
            names = "abcd"[:len(shape)]
            if len(shape) == 1:
                return ap
            return ap.rearrange(f"p ({' '.join(names)}) -> p {' '.join(names)}",
                                **{k: d for k, d in zip(names, shape)})

        x = sb("x", [P, NB, F], F32)
        ident = sb("ident", [P, P], F32)
        ident_bf = sb("ident_bf", [P, P], BF16)
        ident_h = sb("ident_h", [P, P], F16)
        iota = sb("iota", [P, NP], F16)
        iota128, iotaLO, iotaNR = iota[:, HALF:HALF + P], iota[:, HALF:HALF + LO], iota[:, HALF:HALF + 96]
        steps_row = sb("steps_row", [1, NB * 4], I32)
        block_lo = sb("block_lo", [P, 1], F32)
        node_no = sb("node_no", [P, 1], F32)
        dst_rel = sb("dst_rel", [P, QS], F32)
        cur = sb("cur", [P, QS], F32)
        stat = sb("stat", [P, NB, 4], F32)
        eps_t = sb("eps_t", [P, 1], F32)

        big = sb("big", [P, NB * NP], F16)
        work = sb("work", [P, 19700], F16)

        class Region:
            def __init__(self, tensor, size):
                self.tensor, self.size, self.at = tensor, size, 0

            def take(self, shape, dt, parts=P):
                n = int(np.prod(shape)) * BYTES[dt] // 2
                ap = self.tensor[0:parts, self.at:self.at + n]
                self.at += n + (-n) % 2
                assert self.at <= self.size, (self.at, self.size)
                return shaped(ap if dt == F16 else ap.bitcast(dt), list(shape))

        def regions():
            return Region(big, NB * NP), Region(work, 19700)

        psum = ctx.enter_context(nc.psum_tensor("psum", [P, 8, BANK], F32))

        def bank(i, shape, dt=F32, parts=P, count=1):
            n = int(np.prod(shape)) * BYTES[dt] // 4
            ap = psum[0:parts, i:i + count, :].rearrange("p a b -> p (a b)")[:, 0:n]
            return shaped(ap if dt == F32 else ap.bitcast(dt), list(shape))

        phase_done = sem("phase_done")
        phase_no = {}

        def phase_end(eng):
            phase_no[eng] = phase_no.get(eng, 0) + 1
            eng.drain().then_inc(phase_done, 1)
            eng.wait_ge(phase_done, ENGINES * phase_no[eng])

        def block_table(eng, b):
            def entry(k, least, most):
                return eng.value_load(steps_row[0:1, bass.ds(b * 4 + k, 1)], min_val=least, max_val=most)
            return entry(0, 0, NS - 1), entry(1, 1, NS), entry(2, 0, NB * NS)

        def total_steps(eng):
            return eng.value_load(steps_row[0:1, 3:4], min_val=1, max_val=NB * NS)

        def block_steps(eng, table):
            first, count, base = table
            with eng.Fori(0, count) as i:
                s = nc.s_assert_within(first + i, 0, NS - 1,
                                       skip_runtime_bounds_check_because="first + count is at most NS")
                yield s, base + i

        def split3(v, parts, src, rest):
            v.tensor_copy(parts[0], src)
            v.drain()
            v.tensor_tensor(rest, src, parts[0], ALU.subtract)
            v.drain()
            v.tensor_copy(parts[1], rest)
            v.drain()
            v.tensor_tensor(rest, rest, parts[1], ALU.subtract)
            v.drain()
            return v.tensor_copy(parts[2], rest)

        def wide(ap, n):
            return ap.unsqueeze(2).to_broadcast([ap.shape[0], ap.shape[1], n])

        ln_var = sem("ln_var")
        ln_std = sem("ln_std")
        ln_done = sem("ln_done")

        def dve_layernorm(v, h, tmp, k):
            mean, var, rstd = stat[:, :, 0], stat[:, :, 1], stat[:, :, 3]
            v.tensor_reduce(mean, x[:], AX.X, ALU.add)
            v.drain()
            v.tensor_scalar(mean, mean, 1.0 / F, None, ALU.mult)
            v.drain()
            v.tensor_tensor(h, x[:], wide(mean, F), ALU.subtract)
            v.drain()
            v.tensor_tensor(tmp, h, h, ALU.mult)
            v.drain()
            v.tensor_reduce(var, tmp, AX.X, ALU.add)
            v.drain()
            v.tensor_scalar(var, var, 1.0 / F, EPS, ALU.mult, ALU.add).then_inc(ln_var, 1)
            v.wait_ge(ln_std, k)
            v.reciprocal(rstd, stat[:, :, 2])
            v.drain()
            v.tensor_tensor(h, h, wide(rstd, F), ALU.mult)
            v.drain()
            v.tensor_scalar(h, h, 0.0, None, ALU.max).then_inc(ln_done, 1)

        def act_layernorm(a, k):
            a.wait_ge(ln_var, k)
            a.activation(stat[:, :, 2], stat[:, :, 1], ACT.Sqrt).then_inc(ln_std, 1)

        hT_psum = sem("hT_psum")
        hT_done = sem("hT_done")

        def pe_transpose_nodes(pe, h, k):
            for b in range(NB):
                mm = pe.transpose(bank(0, [NP], parts=F, count=7)[:, b * P:(b + 1) * P], h[:, b, :], ident[:])
            mm.then_inc(hT_psum, 1)

        def act_copy_nodes(a, hT, k):
            a.wait_ge(hT_psum, k)
            a.activation(hT, bank(0, [NP], parts=F, count=7), ACT.Copy).then_inc(hT_done, 1)

        GROUPS = [(g, min(2, NB - 2 * g)) for g in range(-(-NB // 2))]
        tab_psum = sem("tab_psum")
        tab_free = sem("tab_free")

        def pe_table(pe, hT, w, width, k):
            pe.wait_ge(hT_done, k)
            for g, m in GROUPS:
                if g >= 7:
                    pe.wait_ge(tab_free, len(GROUPS) * (k - 1) + g - 6)
                for t in range(m):
                    b = 2 * g + t
                    mm = pe.matmul(bank(g % 7, [2, 256])[:, t, 0:width], hT[:, b * P:(b + 1) * P], w,
                                   start=True, stop=True)
                mm.then_inc(tab_psum, 1)

        def dve_table(v, table, rest, width, k):
            for g, m in GROUPS:
                v.wait_ge(tab_psum, len(GROUPS) * (k - 1) + g + 1)
                split3(v, [table[:, 2 * g:2 * g + m, i, :] for i in range(3)],
                       bank(g % 7, [2, 256])[:, 0:m, 0:width], rest[:, 0:m, 0:width]).then_inc(tab_free, 1)
                v.drain()

        class Sweep:

            def __init__(self, tag, silu, K):
                self.silu, self.K, self.width = silu, K, K * F
                self.onehot_ready = sem(f"{tag}_onehot_ready")
                self.onehotT_psum = sem(f"{tag}_onehotT_psum")
                self.onehotT_ready = sem(f"{tag}_onehotT_ready")
                self.products_ready = sem(f"{tag}_products_ready")
                self.products_used = sem(f"{tag}_products_used")
                self.msg_ready = sem(f"{tag}_msg_ready")
                self.msg_spread = sem(f"{tag}_msg_spread")
                self.silu_done = sem(f"{tag}_silu_done")
                self.lo_ready = sem(f"{tag}_lo_ready")
                self.scatter_done = sem(f"{tag}_scatter_done")

            def place(self, dst_f, lo_f, onehot_hi, coef, table, W):
                self.dst_f, self.lo_f, self.onehot_hi, self.coef, self.table = dst_f, lo_f, onehot_hi, coef, table
                self.onehot = W.take([QS, P], BF16)
                self.onehotT = W.take([QS, P], BF16)
                self.prod = W.take([QS, 256], F32)
                self.msg = W.take([QS, F], F32)
                self.smsg = W.take([QS, F], F32)
                self.spread = W.take([QS, HI, F], F32)
                self.onehot_lo = W.take([QS, LO], F32)
                self.psT = bank(0, [QS, P], BF16)
                self.products = [bank(1 + r, [2, 256])[:, :, 0:self.width] for r in range(2)]
                self.agg = bank(3, [LO])

            def onehots_lo(self, v):
                for q in range(QS):
                    op = v.tensor_scalar(self.onehot_lo[:, q, :], iotaLO, cur[:, q:q + 1], None, ALU.is_equal)
                return op

            def dve(self, v):
                prev = self.silu_done if self.silu else self.msg_spread
                v.memset(block_lo[:], 0.0)
                v.memset(cur[:], -1.0)
                v.memset(self.onehot_lo, 0.0)
                v.drain()
                v.sem_inc(self.products_used, 2)
                with v.Fori(0, NB) as b:
                    for s, n in block_steps(v, block_table(v, b)):
                        v.tensor_scalar(dst_rel[:], self.dst_f[:, bass.ds(s * QS, QS)], block_lo[:], None, ALU.subtract)
                        v.drain()
                        for q in range(QS):
                            op = v.tensor_scalar(self.onehot[:, q, :], iota128, dst_rel[:, q:q + 1], None, ALU.is_equal)
                        op.then_inc(self.onehot_ready, 1)
                        v.wait_ge(self.scatter_done, n + 1)
                        self.onehots_lo(v).then_inc(self.lo_ready, 1)
                        v.drain()
                        v.tensor_copy(cur[:], self.lo_f[:, bass.ds(s * QS, QS)])
                        for r in range(2):
                            half = slice(2 * r, 2 * r + 2)
                            prod = self.prod[:, half, 0:self.width].rearrange("p q (k o) -> p q k o", o=F)
                            coef = self.coef[:, bass.ds(s * QS + 2 * r, 2), :]
                            v.wait_ge(self.products_ready, n * 2 + (r + 1))
                            v.tensor_tensor(prod, self.products[r].rearrange("p q (k o) -> p q k o", o=F),
                                            coef.unsqueeze(3).to_broadcast([P, 2, self.K, F]),
                                            ALU.mult).then_inc(self.products_used, 1)
                            v.drain()
                            v.wait_ge(prev, n * 2 + (r + 1))
                            v.tensor_reduce(self.msg[:, half, :], prod.rearrange("p q k o -> p q o k"),
                                            AX.X, ALU.add).then_inc(self.msg_ready, 1)
                    v.drain()
                    v.tensor_scalar(block_lo[:], block_lo[:], float(P), None, ALU.add)
                    v.drain()
                total = total_steps(v)
                v.wait_ge(self.scatter_done, total + 1)
                self.onehots_lo(v).then_inc(self.lo_ready, 1)

            def act(self, a):
                if self.silu:
                    a.sem_inc(self.silu_done, 2)
                with a.Fori(0, NB) as b:
                    for s, n in block_steps(a, block_table(a, b)):
                        a.wait_ge(self.onehotT_psum, n + 1)
                        a.activation(self.onehotT, self.psT, ACT.Copy).then_inc(self.onehotT_ready, 1)
                        if self.silu:
                            for r in range(2):
                                half = slice(2 * r, 2 * r + 2)
                                a.wait_ge(self.msg_ready, n * 2 + (r + 1))
                                a.wait_ge(self.msg_spread, n * 2 + (r + 1))
                                a.activation(self.smsg[:, half, :], self.msg[:, half, :], ACT.Silu,
                                             scale=1.0 / float(np.sqrt(F * self.K))).then_inc(self.silu_done, 1)
                        a.wait_ge(self.products_ready, n * 2 + 2)

            def pool(self, g):
                g.memset(self.spread, 0.0)
                g.drain()
                g.sem_inc(self.msg_spread, 2)
                with g.Fori(0, NB) as b:
                    for s, n in block_steps(g, block_table(g, b)):
                        g.wait_ge(self.scatter_done, n + 2)
                        for r in range(2):
                            half = slice(2 * r, 2 * r + 2)
                            if self.silu:
                                g.wait_ge(self.silu_done, n * 2 + (r + 3))
                            else:
                                g.wait_ge(self.msg_ready, n * 2 + (r + 1))
                            msg = (self.smsg if self.silu else self.msg)[:, half, :]
                            hi = self.onehot_hi[:, bass.ds(s * QS + 2 * r, 2), :]
                            g.tensor_tensor(self.spread[:, half, :, :],
                                            msg.unsqueeze(2).to_broadcast([P, 2, HI, F]),
                                            hi.unsqueeze(3).to_broadcast([P, 2, HI, F]),
                                            ALU.mult).then_inc(self.msg_spread, 1)

            def scatter(self, pe, qs=range(QS), start=False):
                for q in qs:
                    mm = pe.matmul(self.agg, self.spread[:, q, :, :].rearrange("p h o -> p (h o)"),
                                   self.onehot_lo[:, q, :], start=start, stop=True, skip_group_check=True)
                return mm

            def zero(self, pe):
                return self.scatter(pe, [0], True)

            def pe(self, pe):
                pe.wait_ge(self.msg_spread, 2)
                pe.wait_ge(self.products_used, 2)
                self.zero(pe).then_inc(self.scatter_done, 1)
                with pe.Fori(0, NB) as b:
                    for s, n in block_steps(pe, block_table(pe, b)):
                        pe.wait_ge(self.onehot_ready, n + 1)
                        for q in range(QS):
                            mm = pe.transpose(self.psT[:, q, :], self.onehot[:, q, :], ident_bf[:])
                        mm.then_inc(self.onehotT_psum, 1)
                        pe.wait_ge(self.onehotT_ready, n + 1)
                        for r in range(2):
                            pe.wait_ge(self.products_used, n * 2 + (r + 1))
                            for t in range(2):
                                for i in range(3):
                                    row = self.table[:, bass.ds(b, 1), i, :].rearrange("p a w -> p (a w)")
                                    mm = pe.matmul(self.products[r][:, t, :], self.onehotT[:, 2 * r + t, :],
                                                   row, start=(i == 0), stop=(i == 2))
                            mm.then_inc(self.products_ready, 1)
                        pe.wait_ge(self.lo_ready, n + 1)
                        pe.wait_ge(self.msg_spread, n * 2 + 2)
                        self.scatter(pe).then_inc(self.scatter_done, 1)
                total = total_steps(pe)
                pe.wait_ge(self.lo_ready, total + 1)
                pe.wait_ge(self.msg_spread, total * 2 + 2)
                self.scatter(pe)

        sweep0 = Sweep("spline", False, 16)
        sweep2 = Sweep("tensor", True, 8)

        agg_copied = sem("agg_copied")
        agg_moved = sem("agg_moved")

        def sync_regroup(sp, agg_sb, aggT, k):
            sp.wait_ge(agg_copied, k)
            for h in range(HI):
                sp.dma_start(aggT[0:F, h * LO:(h + 1) * LO], agg_sb[h * F:(h + 1) * F, :]).then_inc(agg_moved, 16)

        B1, W1 = regions()
        hT = B1.take([NP], F32, parts=F)
        attr2 = B1.take([NC, 2], F32)
        hats = B1.take([NC, 2, 4], F32)
        basis = B1.take([NC, 4, 4], F32)
        table0 = B1.take([NB, 3, 256], BF16)
        dst_i = B1.take([NC], I32)
        src_i = B1.take([NC], I32)
        h0 = W1.take([NB, F], F32)
        lntmp = W1.take([NB, F], F32)
        dst_f = W1.take([NC], F32)
        src_c = W1.take([NC], F32)
        W1_keep = W1.at
        lo_f = W1.take([NC], F32)
        mark = W1.at
        rest = W1.take([2, 256], F32)
        hi_f = W1.take([NC], F32)
        tmp_c = W1.take([NC], F32)
        w0 = W1.take([256], F32, parts=F)
        centers = W1.take([4], F32)
        W1b = Region(work, 19700)
        W1b.at = mark
        dst_rows = hats.rearrange("p a b c -> p (a b c)")[0:TPP, 0:2 * STEP]
        dst_rows_i = basis.rearrange("p a b c -> p (a b c)").bitcast(I32)[0:TPP, 0:2 * STEP]
        bx = table0.rearrange("p a b c -> p (a b c)").bitcast(F32)
        step_mm = bx[0:TPP, 0:4].rearrange("p (k t) -> p k t", k=2)
        step_rng = bx[0:NB, 8:8 + 2 * NS].rearrange("p (k t) -> p k t", k=2)
        step_no = bx[0:NB, 1000:1000 + NS]
        step_left = bx[0:NB, 1500:1500 + NS]
        flags = bx[0:NB, 2000:2000 + NS]
        thr = bx[0:NB, 2500:2502]
        bounds = bx[0:NB, 2510:2518]
        before = bx[0:NB, 2600:2600 + NB]
        ones25 = bx[0:NB, 2700:2700 + NB]
        bounds_i = bx[0:NB, 2800:2804].bitcast(I32)

        loaded = sem("loaded")
        consts = sem("consts")
        rng_copied = sem("rng_copied")
        rng_out = sem("rng_out")
        rng_in = sem("rng_in")
        count_ready = sem("count_ready")
        base_ready = sem("base_ready")
        bounds_ready = sem("bounds_ready")
        bounds_out = sem("bounds_out")
        bounds_in = sem("bounds_in")
        LOADS1 = 7

        onehot_hi = B1.take([NC, HI], BF16)

        sweep0.place(dst_f, lo_f, onehot_hi, basis.rearrange("p c a b -> p c (a b)"), table0, W1b)

        B2, W2 = regions()
        A = B2.take([NB, NP], F16)
        W2.at = W1_keep
        onehot_src = W2.take([2, NP], BF16)
        onehot_dst = W2.take([2, P], BF16)
        onehot_own = W2.take([NP], BF16)
        counts = W2.take([NP], F16)
        own_ready = sem("a_own_ready")
        a_ready = sem("a_onehots_ready")
        a_used = sem("a_onehots_used")
        a_block = sem("a_block_done")
        a_counts = sem("a_counts_copied")
        a_turned = sem("a_turned")
        a_stored_v = sem("a_stored_dve")
        a_stored_a = sem("a_stored_act")
        TURN = [(g * 8, min(8, NB - g * 8)) for g in range(-(-NB // 8))]

        B3, W3 = regions()
        W3.at = 2 * NB * F * 2
        hn = Region(work, 19700).take([NB, F], F32)
        disB = W3.take([NP], F32, parts=96)
        scaled = [W3.take([BANK], F32, parts=96) for _ in range(3)]
        xT = W3.take([BANK], F32, parts=F1)
        Hin = W3.take([NB, 3, F], BF16)
        Hmid = W3.take([NB, 3, F2], BF16)
        Hout = W3.take([NB, 3, F], BF16)
        dis = W3.take([NB], F32)
        W1s = W3.take([96], F32, parts=3 * F)
        S2 = W3.take([F2], F32, parts=96)
        S3 = W3.take([F], F32, parts=3 * F)
        W2w = W3.take([F2], F32, parts=F1)
        W3w = W3.take([F], F32, parts=F2)
        b1t = W3.take([1], F32, parts=F1)
        b2t = W3.take([1], F32, parts=F2)
        b3t = W3.take([F], F32)
        gtmp = W3.take([4, F2], F32)
        grest = W3.take([4, F2], F32)
        z = W3.take([4, F], F32)
        zs = W3.take([4, 4], F32)
        x3 = lntmp
        ones96 = W3.take([96], BF16)

        l_w = sem("l_weights")
        l_wfree = sem("l_weights_free")
        l_main = sem("l_main")
        l_scaled = sem("l_scaled")
        l_z = sem("l_z")
        l_relu = sem("l_relu")
        l_g = sem("l_g")
        l_h = sem("l_h")
        l_mx = sem("l_softmax_in")
        l_ex = sem("l_softmax_exp")
        d_ones = sem("d_ones")
        d_main = sem("d_main")
        d_deg = sem("d_deg")
        d_sqrt = sem("d_sqrt")
        d_inv = sem("d_inv")
        d_node = sem("d_node")
        h_in = sem("h_in")
        WDMAS = 8

        B4, W4 = regions()
        h2T = B4.take([NP], F32, parts=F)
        aggT = B4.take([NP], F32, parts=F)
        uT = B4.take([NP], F32, parts=F)
        attr8 = B4.take([NC, 8], F32)
        table2 = B4.take([NB, 3, 128], BF16)
        onehot_hi2 = B4.take([NC, HI], BF16)
        src_i2 = B4.take([NC], I32)
        agg_sb = B4.take([LO], F32)
        aggn = B4.take([NB, F], F32)
        u = B4.take([NB, F], F32)
        vprod = B4.take([2, 256], F32)
        wmt = B4.take([128], F32, parts=F)
        wml = B4.take([F], F32, parts=F)
        wut = B4.take([256], F32, parts=F)
        wul = B4.take([F], F32, parts=F)
        h2 = Region(work, 19700).take([NB, F], F32)
        W4.at = 2 * NB * F * 2
        dst_f4 = W4.take([NC], F32)
        lo_f4 = W4.take([NC], F32)
        mark4 = W4.at
        hi_f4 = W4.take([NC], F32)
        tmp_c4 = W4.take([NC], F32)
        rest4 = W4.take([2, 256], F32)
        dst_i4 = W4.take([NC], I32)
        tmp_src4 = W4.take([NC], F32)
        W4b = Region(work, 19700)
        W4b.at = mark4
        sweep2.place(dst_f4, lo_f4, onehot_hi2, attr8, table2, W4b)

        agg_sb0 = Region(big, NB * NP)
        agg_sb0.at = NP * 2
        agg0 = agg_sb0.take([LO], F32)
        aggT0 = agg_sb0.take([NP], F32, parts=F)

        B5, W5 = regions()
        h3T = B5.take([NP], F32, parts=F)
        attr16 = B5.take([NC, F], F32)
        gathered = B5.take([NC, GROW], F32)
        src_i5 = B5.take([NC + 2 * QS], I32)
        att_e = B5.take([NC], F32)
        type_f = B5.take([NC], F32)
        rel = B5.take([256], F32, parts=NR)
        relp = B5.take([3, 256], BF16, parts=NR)
        noderow = B5.take([NB, GROW], F32)
        pdst = B5.take([NB, 3], BF16)
        prest = B5.take([256], F32)
        wct = B5.take([NR], F32, parts=NBASE)
        wv = B5.take([256], F32, parts=NBASE)
        ws = B5.take([F], F32, parts=F)
        wa = B5.take([3], F32, parts=F)
        wab = B5.take([P], F32, parts=F)
        att = B5.take([3], F32, parts=F)
        a2b = B5.take([F], F32)
        pf = B5.take([NB, 3], F32)
        h3 = Region(work, 19700).take([NB, F], F32)
        W5.at = 2 * NB * F * 2
        dst_f5 = W5.take([NC], F32)
        mark5 = W5.at
        e_chunk = W5.take([101, F], F32)
        W5b = Region(work, 19700)
        W5b.at = mark5
        onehot5 = W5b.take([QS, P], F32)
        onehotT5 = W5b.take([QS, P], BF16)
        onehot_ty = W5b.take([QS, 96], BF16)
        onehotT_ty = W5b.take([QS, P], BF16, parts=96)
        prod5 = W5b.take([QS, 256], F32)
        red5 = W5b.take([QS, F], F32)
        msg5 = W5b.take([QS, F], F32)
        es5 = W5b.take([QS], F32)
        es5b = W5b.take([QS], F32)
        stage = [W5b.take([QS, GROW], F32) for _ in range(2)]
        stage_idx = [W5b.take([QS], I32) for _ in range(2)]
        zero5 = W5b.take([P], F32)
        r_onehots = sem("r_onehots_ready")
        r_turned = sem("r_turned")
        r_copied = sem("r_copied")
        r_pd = sem("r_pd_ready")
        r_prod = sem("r_products_ready")
        r_msg = sem("r_msg_ready")
        r_agg = sem("r_agg_done")
        r_out = sem("r_out_added")
        r_gath = [sem(f"r_gather_{i}") for i in range(2)]
        r_hg = sem("r_gathered")
        r_idx = sem("r_idx")
        load5 = sem("load5")
        rel_psum = sem("rel_psum")
        rel_sb = sem("rel_sb")
        rel_out = sem("rel_out")
        rel_in = sem("rel_in")
        att_psum = sem("att_psum")
        att_sb = sem("att_sb")
        pf_psum = sem("pf_psum")
        row_sb = sem("row_sb")
        row_out = sem("row_out")
        load4 = sem("load4")
        upd = sem("upd")
        updv = sem("updv")
        upda = sem("upda")
        out_sem = sem("out_sem")

        block = ctx.enter_context(nc.Block())

        @block.sync
        def _(sp):
            def ld(dst, src, s):
                sp.dma_start(dst, src).then_inc(s, 16)
            ld(dst_rows_i, dstrow_in, loaded)
            ld(x[:], x_in, loaded)
            ld(dst_i, dst_in, loaded)
            ld(src_i, src_in, loaded)
            ld(attr2, attr2_in, loaded)
            ld(w0.rearrange("i (k o) -> i k o", o=F), w0_in.rearrange("k i o -> i k o"), loaded)
            sp.wait_ge(rng_copied, 1)
            ld(range_dram.rearrange("k (p t) -> p k t", t=2), step_mm, rng_out)
            sp.wait_ge(rng_out, 16)
            ld(step_rng, range_dram.partition_broadcast(NB), rng_in)
            sp.wait_ge(bounds_ready, 1)
            ld(table_dram, bounds_i, bounds_out)
            sp.wait_ge(bounds_out, 16)
            ld(steps_row[0:1, :], table_dram.rearrange("(a b) k -> a (b k)", a=1), bounds_in)
            sp.wait_ge(bounds_in, 16)
            phase_end(sp)
            phase_end(sp)
            sync_regroup(sp, agg0, aggT0, 1)
            phase_end(sp)
            phase_end(sp)
            phase_end(sp)
            with sp.Fori(0, LAYERS) as l:
                one = bass.ds(l, 1)
                sp.wait_ge(l_wfree, l + 1)
                for i in range(3):
                    ld(W1s[i * F:(i + 1) * F, 0:F1], w1_in[one, :, :].rearrange("a i o -> (a i) o"), l_w)
                ld(W2w, w2_in[one, :, :].rearrange("a i o -> (a i) o"), l_w)
                ld(W3w, w3_in[one, :, :].rearrange("a i o -> (a i) o"), l_w)
                ld(b1t, b1_in[one, :].rearrange("a (i o) -> (a i) o", o=1), l_w)
                ld(b2t, b2_in[one, :].rearrange("a (i o) -> (a i) o", o=1), l_w)
                ld(b3t, b3_in[one, :].rearrange("a o -> (a o)").partition_broadcast(P), l_w)
            phase_end(sp)
            ld(dst_i4, dst_in, load4)
            ld(src_i2, src_in, load4)
            ld(attr8, attr8_in, load4)
            ld(wmt, wmt_in.rearrange("i j h -> i (j h)"), load4)
            ld(wml, wml_in, load4)
            ld(wut, wut_in.rearrange("i h k -> i (h k)"), load4)
            ld(wul, wul_in, load4)
            phase_end(sp)
            phase_end(sp)
            sync_regroup(sp, agg_sb, aggT, 2)
            phase_end(sp)
            ld(attr16, attr16_in, load5)
            ld(src_i5[:, 0:NC], src_in, load5)
            ld(type_f.bitcast(I32), type_in, load5)
            ld(wct, wct_in, load5)
            ld(wv.rearrange("b (i o) -> b i o", o=F), wv_in.rearrange("i b o -> b i o"), load5)
            ld(ws, ws_in, load5)
            ld(wa, wa_in, load5)
            sp.wait_ge(rel_sb, 1)
            ld(rel_dram.rearrange("(i r o) -> r i o", i=F, r=NR), rel.rearrange("r (i o) -> r i o", o=F), rel_out)
            sp.wait_ge(rel_out, 16)
            ld(rel, rel_dram.rearrange("(r c) -> r c", r=NR), rel_in)
            sp.wait_ge(row_sb, 1)
            ld(node_dram.rearrange("(b p) c -> p b c", p=P), noderow, row_out)
            sp.wait_ge(row_out, 16)
            phase_end(sp)
            phase_end(sp)
            full = N // P
            ld(out[0:full * P, :].rearrange("(b p) c -> p b c", p=P), x[:, 0:full, :], out_sem)
            ld(out[full * P:N, :], x[0:N - full * P, full, :], out_sem)
            sp.wait_ge(out_sem, 32)

        @block.gpsimd
        def _(g):
            g.iota(iota[:], [[1, NP]], base=-HALF, channel_multiplier=0, allow_small_or_imprecise_dtypes=True)
            g.iota(step_no, [[1, NS]], base=1, channel_multiplier=0, allow_small_or_imprecise_dtypes=True)
            g.iota(step_left, [[-1, NS]], base=NS, channel_multiplier=0, allow_small_or_imprecise_dtypes=True)
            g.iota(thr[:, 0:1], [[1, 1]], base=0, channel_multiplier=P, allow_small_or_imprecise_dtypes=True)
            g.iota(thr[:, 1:2], [[1, 1]], base=P - 1, channel_multiplier=P, allow_small_or_imprecise_dtypes=True)
            g.iota(node_no[:], [[1, 1]], base=-HALF, channel_multiplier=1, allow_small_or_imprecise_dtypes=True)
            g.memset(ident[:], 0.0)
            g.memset(before, 1.0)
            g.memset(ones25, 1.0)
            for j in range(4):
                g.memset(centers[:, j:j + 1], -1.0 + 2.0 * j / 3.0)
            g.drain()
            g.affine_select(out=ident[:], in_=ident[:], compare_op=ALU.not_equal, fill=1.0, base=0,
                            pattern=[[-1, P]], channel_multiplier=1)
            g.affine_select(out=before, in_=before, compare_op=ALU.is_gt, fill=0.0, base=0,
                            pattern=[[1, NB]], channel_multiplier=-1)
            g.drain()
            g.tensor_copy(ident_bf[:], ident[:])
            g.tensor_copy(ident_h[:], ident[:])
            g.drain().then_inc(consts, 1)
            phase_end(g)
            sweep0.pool(g)
            phase_end(g)
            phase_end(g)
            phase_end(g)
            phase_end(g)
            phase_end(g)
            phase_end(g)
            sweep2.pool(g)
            phase_end(g)
            phase_end(g)
            g.memset(src_i5[:, NC:NC + 2 * QS], 0)
            g.memset(zero5, 0.0)
            phase_end(g)

            def gather(i, s):
                g.tensor_copy(stage_idx[i], src_i5[:, bass.ds(s * QS, QS)])
                g.drain()
                for q in range(QS):
                    g.indirect_dma_start(out=stage[i][:, q, :], out_offset=None, in_=node_dram,
                                         in_offset=bass.IndirectOffsetOnAxis(ap=stage_idx[i][:, q:q + 1], axis=0)
                                         ).then_inc(r_gath[i], 16)

            def keep(i, s, done):
                g.wait_ge(r_gath[i], done)
                g.tensor_copy(gathered[:, bass.ds(s * QS, QS), :], stage[i]).then_inc(r_hg, 1)
                g.drain()

            gather(0, 0)
            with g.Fori(0, NS // 2) as k:
                gather(1, k * 2 + 1)
                keep(0, k * 2, k * (16 * QS) + 16 * QS)
                gather(0, k * 2 + 2)
                keep(1, k * 2 + 1, k * (16 * QS) + 16 * QS)
            g.wait_ge(r_gath[0], 16 * QS * (NS // 2 + 1))
            phase_end(g)

        @block.scalar
        def _(a):
            act_layernorm(a, 1)
            act_copy_nodes(a, hT, 1)
            phase_end(a)
            sweep0.act(a)
            phase_end(a)
            phase_end(a)
            with a.Fori(0, NB) as b:
                a.wait_ge(a_block, b + 1)
                for j, (c0, cn) in enumerate(CHUNKS):
                    a.activation(counts[:, c0:c0 + cn], bank(j, [cn]), ACT.Copy).then_inc(a_counts, 1)
                for g, (s0, sn) in enumerate(TURN):
                    if g % 2:
                        a.wait_ge(a_turned, b * len(TURN) + (g + 1))
                        a.activation(A[:, s0:s0 + sn, bass.ds(b * P, P)], bank(g, [sn, P], F16), ACT.Copy
                                     ).then_inc(a_stored_a, 1)
                a.wait_ge(a_turned, b * len(TURN) + len(TURN))
            phase_end(a)
            for j, (c0, cn) in enumerate(CHUNKS):
                a.wait_ge(d_deg, j + 1)
                a.activation(disB[:, c0:c0 + cn], disB[:, c0:c0 + cn], ACT.Sqrt).then_inc(d_sqrt, 1)
            act_layernorm(a, 2)
            phase_end(a)
            with a.Fori(0, LAYERS) as l:
                a.wait_ge(l_w, l * (16 * WDMAS) + 16 * WDMAS)
                for conv, (width, bias) in enumerate(((F1, b1t), (F2, b2t))):
                    for j, (c0, cn) in enumerate(CHUNKS):
                        k = conv * NCH + j
                        a.wait_ge(l_z, l * (2 * NCH) + (k + 1))
                        a.activation(xT[0:width, 0:cn], bank(3, [cn], parts=width), ACT.Relu,
                                     bias=bias[0:width, :]).then_inc(l_relu, 1)
                for j in range(NCH):
                    a.wait_ge(l_mx, l * NCH + (j + 1))
                    a.activation(z, z, ACT.Exp).then_inc(l_ex, 1)
            phase_end(a)
            act_layernorm(a, 3)
            act_copy_nodes(a, h2T, 2)
            phase_end(a)
            sweep2.act(a)
            phase_end(a)
            a.wait_ge(updv, 1 + len(GROUPS))
            a.activation(u, u, ACT.Silu, scale=1.0 / float(np.sqrt(F * F))).then_inc(upda, 1)
            a.wait_ge(upd, 3 + len(GROUPS))
            a.activation(uT, bank(0, [NP], parts=F, count=7), ACT.Copy).then_inc(upda, 1)
            phase_end(a)
            act_layernorm(a, 4)
            act_copy_nodes(a, h3T, 3)
            phase_end(a)
            with a.Fori(0, NB) as b:
                for s, n in block_steps(a, block_table(a, b)):
                    a.wait_ge(r_turned, n + 1)
                    a.activation(onehotT5, bank(0, [QS, P]), ACT.Copy).then_inc(r_copied, 1)
                    a.activation(onehotT_ty, bank(1, [QS, P], BF16, parts=96), ACT.Copy).then_inc(r_copied, 1)
                    a.wait_ge(r_prod, n * 2 + 2)
            phase_end(a)

        @block.tensor
        def _(pe):
            pe.wait_ge(consts, 1)
            pe.wait_ge(count_ready, 1)
            pe.matmul(bank(7, [2])[0:NB, 0:1], before, bounds[:, 1:2], start=True, stop=True)
            pe.matmul(bank(7, [2])[0:NB, 1:2], ones25, bounds[:, 1:2], start=True, stop=True).then_inc(base_ready, 1)
            pe.wait_ge(ln_done, 1)
            pe_transpose_nodes(pe, h0, 1)
            pe_table(pe, hT, w0, 256, 1)
            phase_end(pe)
            sweep0.pe(pe)
            phase_end(pe)
            pe.wait_ge(agg_moved, 16 * HI)
            for b in range(NB):
                mm = pe.matmul(bank(4, [NB, F])[:, b, :], aggT0[:, b * P:(b + 1) * P], ident[0:F, 0:F],
                               start=True, stop=True)
            mm.then_inc(upd, 1)
            phase_end(pe)
            pe.sem_inc(a_used, 2)
            with pe.Fori(0, NB) as b:
                pe.wait_ge(own_ready, b + 1)
                for j, (c0, cn) in enumerate(CHUNKS):
                    mm = pe.matmul(bank(j, [cn]), ident_bf[:], onehot_own[:, c0:c0 + cn], start=True, stop=True,
                                   skip_group_check=True)
                for s, n in block_steps(pe, block_table(pe, b)):
                    for q in range(QS):
                        pe.wait_ge(a_ready, n * QS + (q + 1))
                        for j, (c0, cn) in enumerate(CHUNKS):
                            mm = pe.matmul(bank(j, [cn]), onehot_dst[:, q % 2, :],
                                           onehot_src[:, q % 2, c0:c0 + cn], start=False, stop=True,
                                           skip_group_check=True)
                        mm.then_inc(a_used, 1)
                pe.drain().then_inc(a_block, 1)
                for g, (s0, sn) in enumerate(TURN):
                    if g == 0:
                        pe.wait_ge(a_counts, b * NCH + NCH)
                    for t in range(sn):
                        mm = pe.transpose(bank(g, [sn, P], F16)[:, t, :],
                                          counts[:, (s0 + t) * P:(s0 + t + 1) * P], ident_h[:])
                    mm.then_inc(a_turned, 1)
                pe.wait_ge(a_stored_v, b * 2 + 2)
                pe.wait_ge(a_stored_a, b * 2 + 2)
            phase_end(pe)
            pe.wait_ge(d_ones, 1)
            for j, (c0, cn) in enumerate(CHUNKS):
                for b in range(NB):
                    mm = pe.matmul(bank(j, [cn], parts=96), ones96, A[:, b, c0:c0 + cn],
                                   start=(b == 0), stop=(b == NB - 1))
                mm.then_inc(d_main, 1)
            pe.wait_ge(d_inv, NCH)
            for b in range(NB):
                mm = pe.matmul(bank(7, [NB])[:, b:b + 1], disB[0:1, b * P:(b + 1) * P], ident[0:1, 0:1],
                               start=True, stop=True)
            mm.then_inc(d_node, 1)
            phase_end(pe)
            with pe.Fori(0, LAYERS) as l:
                pe.wait_ge(l_w, l * (16 * WDMAS) + 16 * WDMAS)
                for conv, (H, width) in enumerate(((Hin, F), (Hmid, F2), (Hout, F))):
                    rows = 3 * width

                    def weigh(j):
                        c0, cn = CHUNKS[j]
                        k = conv * NCH + j
                        pe.wait_ge(l_scaled, l * (3 * NCH) + (k + 1))
                        if conv < 2:
                            w, m = ((W1s, 96), (S2, F2))[conv]
                            pe.matmul(bank(3, [cn], parts=m), w[0:rows, 0:m], scaled[k % 3][0:rows, 0:cn],
                                      start=True, stop=True).then_inc(l_z, 1)

                    def finish(j):
                        c0, cn = CHUNKS[j]
                        k = conv * NCH + j
                        if conv < 2:
                            pe.wait_ge(l_relu, l * (2 * NCH) + (k + 1))
                        pe.wait_ge(l_h, l * (3 * NCH) + (k + 1))
                        for t in range(cn // P):
                            cols = slice(t * P, (t + 1) * P)
                            if conv == 0:
                                mm = pe.matmul(bank(4, [4, F2])[:, t, :], xT[0:F1, cols], W2w, start=True, stop=True)
                            elif conv == 1:
                                mm = pe.matmul(bank(4, [4, F2])[:, t, 0:F], xT[0:F2, cols], W3w, start=True, stop=True)
                            else:
                                mm = pe.matmul(bank(4, [4, F2])[:, t, 0:F], scaled[k % 3][0:rows, cols],
                                               S3, start=True, stop=True)
                        mm.then_inc(l_g, 1)

                    for j, (c0, cn) in enumerate(CHUNKS):
                        k = conv * NCH + j
                        if k >= 3:
                            pe.wait_ge(l_scaled, l * (3 * NCH) + (k - 2))
                        for b in range(NB):
                            if j == 0 and b % 4 == 0:
                                if conv == 0:
                                    pe.wait_ge(l_h, l * (3 * NCH) + 1) if b == 0 else None
                                else:
                                    pe.wait_ge(l_h, l * (3 * NCH) + ((conv - 1) * NCH + b // 4 + 2))
                            mm = pe.matmul(bank(k % 3, [cn], parts=rows), H[:, b, :, :].rearrange("p a f -> p (a f)"),
                                           A[:, b, c0:c0 + cn], start=(b == 0), stop=(b == NB - 1))
                        mm.then_inc(l_main, 1)
                        if j >= 2:
                            finish(j - 2)
                        if j >= 1:
                            weigh(j - 1)
                    finish(NCH - 2)
                    weigh(NCH - 1)
                    finish(NCH - 1)
            phase_end(pe)
            pe.wait_ge(ln_done, 3)
            pe_transpose_nodes(pe, h2, 2)
            pe.wait_ge(load4, 16 * 7)
            pe_table(pe, h2T, wmt, 128, 2)
            phase_end(pe)
            sweep2.pe(pe)
            phase_end(pe)
            pe.wait_ge(agg_moved, 16 * 2 * HI)
            for b in range(NB):
                mm = pe.matmul(bank(7, [NB, F])[:, b, :], aggT[:, b * P:(b + 1) * P], wml, start=True, stop=True)
            mm.then_inc(upd, 1)
            for g, m in GROUPS:
                if g >= 7:
                    pe.wait_ge(updv, 1 + g - 6)
                for t in range(m):
                    b = 2 * g + t
                    mm = pe.matmul(bank(g % 7, [2, 256])[:, t, :], h2T[:, b * P:(b + 1) * P], wut, start=True, stop=True)
                mm.then_inc(upd, 1)
            pe.wait_ge(upda, 1)
            for b in range(NB):
                mm = pe.transpose(bank(0, [NP], parts=F, count=7)[:, b * P:(b + 1) * P], u[:, b, :], ident[:])
            mm.then_inc(upd, 1)
            pe.wait_ge(upda, 2)
            for b in range(NB):
                mm = pe.matmul(bank(7, [NB, F])[:, b, :], uT[:, b * P:(b + 1) * P], wul, start=True, stop=True)
            mm.then_inc(upd, 1)
            phase_end(pe)
            pe.wait_ge(load5, 16 * 7)
            pe.matmul(bank(7, [256], parts=NR), wct, wv, start=True, stop=True).then_inc(rel_psum, 1)
            pe.wait_ge(rel_sb, 1)
            pe.matmul(bank(7, [3], parts=F), ws, wa, start=True, stop=True)
            pe.wait_ge(att_sb, 1)
            pe.matmul(bank(7, [32])[:, 16:32], wab, ws, start=True, stop=True).then_inc(att_psum, 1)
            pe.wait_ge(ln_done, 4)
            pe_transpose_nodes(pe, h3, 3)
            pe.wait_ge(hT_done, 3)
            pe.wait_ge(att_sb, 2)
            for b in range(NB):
                mm = pe.matmul(bank(6, [NB, 3])[:, b, :], h3T[:, b * P:(b + 1) * P], att, start=True, stop=True)
            mm.then_inc(pf_psum, 1)
            phase_end(pe)
            pe.sem_inc(r_agg, 1)
            with pe.Fori(0, NB) as b:
                pe.wait_ge(r_out, b + 1)
                table = block_table(pe, b)
                pe.matmul(bank(5, [F]), zero5, zero5[:, 0:F], start=True, stop=True, skip_group_check=True)
                for s, n in block_steps(pe, table):
                    pe.wait_ge(r_onehots, n + 1)
                    for q in range(QS):
                        pe.transpose(bank(0, [QS, P])[:, q, :], onehot5[:, q, :], ident[:])
                    for q in range(QS):
                        mm = pe.transpose(bank(1, [QS, P], BF16, parts=96)[:, q, :], onehot_ty[:, q, :], ident_bf[:])
                    mm.then_inc(r_turned, 1)
                    pe.wait_ge(r_copied, n * 2 + 2)
                    for q in range(QS):
                        for i in range(3):
                            mm = pe.matmul(bank(4, [QS])[:, q:q + 1], onehotT5[:, q, :],
                                           pdst[:, bass.ds(b, 1), i], start=(i == 0), stop=(i == 2))
                    mm.then_inc(r_pd, 1)
                    for r in range(2):
                        for t in range(2):
                            for i in range(3):
                                mm = pe.matmul(bank(2 + r, [2, 256])[:, t, :], onehotT_ty[0:NR, 2 * r + t, :],
                                               relp[0:NR, i, :], start=(i == 0), stop=(i == 2))
                        mm.then_inc(r_prod, 1)
                    pe.wait_ge(r_msg, n + 1)
                    for q in range(QS):
                        mm = pe.matmul(bank(5, [F]), onehot5[:, q, :], msg5[:, q, :], start=False, stop=True,
                                       skip_group_check=True)
                    mm.then_inc(r_agg, 1)
            phase_end(pe)

        @block.vector
        def _(v):
            v.wait_ge(loaded, 16 * 6)
            v.wait_ge(consts, 1)
            v.tensor_copy(dst_rows, dst_rows_i)
            v.drain()
            rows2 = dst_rows.rearrange("p (t e) -> p t e", t=2)
            v.tensor_reduce(step_mm[:, 0, :], rows2, AX.X, ALU.max)
            v.tensor_reduce(step_mm[:, 1, :], rows2, AX.X, ALU.min)
            v.drain().then_inc(rng_copied, 1)
            dve_layernorm(v, h0, lntmp, 1)
            v.wait_ge(rng_in, 16)
            v.tensor_scalar(flags, step_rng[:, 0, :], thr[:, 0:1], None, ALU.is_ge)
            v.drain()
            v.tensor_tensor(flags, flags, step_left, ALU.mult)
            v.drain()
            v.tensor_reduce(bounds[:, 0:1], flags, AX.X, ALU.max)
            v.drain()
            v.tensor_scalar(bounds[:, 0:1], bounds[:, 0:1], -1.0, float(NS), ALU.mult, ALU.add)
            v.drain()
            v.tensor_scalar(bounds[:, 0:1], bounds[:, 0:1], float(NS - 1), None, ALU.min)
            v.tensor_scalar(flags, step_rng[:, 1, :], thr[:, 1:2], None, ALU.is_le)
            v.drain()
            v.tensor_tensor(flags, flags, step_no, ALU.mult)
            v.drain()
            v.tensor_reduce(bounds[:, 4:5], flags, AX.X, ALU.max)
            v.drain()
            v.tensor_tensor(bounds[:, 1:2], bounds[:, 4:5], bounds[:, 0:1], ALU.subtract)
            v.drain()
            v.tensor_scalar(bounds[:, 1:2], bounds[:, 1:2], 1.0, None, ALU.max)
            v.drain().then_inc(count_ready, 1)
            v.wait_ge(base_ready, 1)
            v.tensor_copy(bounds[:, 2:4], bank(7, [2])[0:NB, :])
            v.drain()
            v.tensor_copy(bounds_i, bounds[:, 0:4])
            v.drain().then_inc(bounds_ready, 1)
            v.tensor_copy(dst_f, dst_i)
            v.tensor_copy(src_c, src_i)
            v.drain()

            def split_src(src_f, hi, lo, hi_onehot, tmp):
                v.tensor_scalar(hi, src_f, float(LO), None, ALU.is_ge)
                for k in range(2, HI):
                    v.tensor_scalar(tmp, src_f, float(LO * k), None, ALU.is_ge)
                    v.drain()
                    v.tensor_tensor(hi, hi, tmp, ALU.add)
                    v.drain()
                v.tensor_scalar(tmp, hi, -float(LO), None, ALU.mult)
                v.drain()
                v.tensor_tensor(lo, src_f, tmp, ALU.add)
                for k in range(HI):
                    v.tensor_scalar(hi_onehot[:, :, k], hi, float(k), None, ALU.is_equal)
                v.drain()

            split_src(src_c, hi_f, lo_f, onehot_hi, tmp_c)
            v.tensor_scalar(attr2, attr2, -1.0, 1.0, ALU.max, ALU.min)
            v.tensor_tensor(tmp_c, src_c, dst_f, ALU.not_equal)
            v.drain()
            for j in range(4):
                v.tensor_scalar(hats[:, :, :, j], attr2, centers[:, j:j + 1], None, ALU.subtract)
            v.drain()
            rising = basis.rearrange("p c a b -> p (c a b)")[:, 0:NC * 8].rearrange("p (c a b) -> p c a b", a=2, b=4)
            v.tensor_scalar(rising, hats, 1.5, 1.0, ALU.mult, ALU.add)
            v.drain()
            v.tensor_scalar(hats, hats, -1.5, 1.0, ALU.mult, ALU.add)
            v.drain()
            v.tensor_tensor(hats, hats, rising, ALU.min)
            v.drain()
            v.tensor_scalar(hats, hats, 0.0, None, ALU.max)
            v.drain()
            v.tensor_tensor(hats[:, :, 1, :], hats[:, :, 1, :], wide(tmp_c, 4), ALU.mult)
            v.drain()
            v.tensor_tensor(basis, hats[:, :, 0, :].unsqueeze(3).to_broadcast([P, NC, 4, 4]),
                            hats[:, :, 1, :].unsqueeze(2).to_broadcast([P, NC, 4, 4]), ALU.mult)
            v.tensor_scalar(src_c, src_c, -float(HALF), None, ALU.add)
            v.wait_ge(bounds_out, 16)
            dve_table(v, table0, rest, 256, 1)
            phase_end(v)
            sweep0.dve(v)
            phase_end(v)
            v.tensor_copy(agg0, sweep0.agg)
            v.drain().then_inc(agg_copied, 1)
            v.wait_ge(upd, 1)
            v.scalar_tensor_tensor(x[:], bank(4, [NB, F]), 1.0 / 128.0, x[:], ALU.mult, ALU.add)
            v.drain()
            phase_end(v)
            v.memset(block_lo[:], 0.0)
            v.tensor_scalar(onehot_own, iota[:], node_no[:], None, ALU.is_equal).then_inc(own_ready, 1)
            v.drain()
            with v.Fori(0, NB) as b:
                for s, n in block_steps(v, block_table(v, b)):
                    v.tensor_scalar(dst_rel[:], dst_f[:, bass.ds(s * QS, QS)], block_lo[:], None, ALU.subtract)
                    v.tensor_copy(cur[:], src_c[:, bass.ds(s * QS, QS)])
                    v.drain()
                    for q in range(QS):
                        v.wait_ge(a_used, n * QS + (q + 1))
                        v.tensor_scalar(onehot_dst[:, q % 2, :], iota128, dst_rel[:, q:q + 1], None, ALU.is_equal)
                        v.tensor_scalar(onehot_src[:, q % 2, :], iota[:], cur[:, q:q + 1], None,
                                        ALU.is_equal).then_inc(a_ready, 1)
                    v.drain()
                for g, (s0, sn) in enumerate(TURN):
                    if g % 2 == 0:
                        v.wait_ge(a_turned, b * len(TURN) + (g + 1))
                        v.tensor_copy(A[:, s0:s0 + sn, bass.ds(b * P, P)], bank(g, [sn, P], F16)
                                      ).then_inc(a_stored_v, 1)
                v.tensor_scalar(block_lo[:], block_lo[:], float(P), None, ALU.add)
                v.tensor_scalar(node_no[:], node_no[:], float(P), None, ALU.add)
                v.drain()
                v.tensor_scalar(onehot_own, iota[:], node_no[:], None, ALU.is_equal).then_inc(own_ready, 1)
            phase_end(v)
            v.memset(ones96, 1.0).then_inc(d_ones, 1)
            v.memset(W1s, 0.0)
            for j, (c0, cn) in enumerate(CHUNKS):
                v.wait_ge(d_main, j + 1)
                v.tensor_scalar(disB[:, c0:c0 + cn], bank(j, [cn], parts=96), 1.0, None, ALU.max).then_inc(d_deg, 1)
            for j, (c0, cn) in enumerate(CHUNKS):
                v.wait_ge(d_sqrt, j + 1)
                v.reciprocal(disB[:, c0:c0 + cn], disB[:, c0:c0 + cn]).then_inc(d_inv, 1)
            dve_layernorm(v, hn, x3, 2)
            for i in range(3):
                v.tensor_copy(S2[i * F2:(i + 1) * F2, :], ident[i * F2:(i + 1) * F2, i * F2:(i + 1) * F2])
            v.tensor_tensor(S3, ident[0:3 * F, 0:F], ident[0:3 * F, F:2 * F], ALU.add)
            v.drain()
            v.tensor_tensor(S3, S3, ident[0:3 * F, 2 * F:3 * F], ALU.add)
            v.wait_ge(d_node, 1)
            v.tensor_copy(dis, bank(7, [NB]))
            v.drain()

            def parts_of(H, b0, m, src, width):
                t, r = gtmp[:, 0:m, 0:width], grest[:, 0:m, 0:width]
                v.tensor_tensor(t, src, wide(dis[:, b0:b0 + m], width), ALU.mult)
                v.drain()
                return split3(v, [H[:, b0:b0 + m, i, :] for i in range(3)], t, r)

            for j, (c0, cn) in enumerate(CHUNKS):
                b0, m = c0 // P, cn // P
                parts_of(Hin, b0, m, hn[:, b0:b0 + m, :], F)
                v.drain()
            v.sem_inc(l_wfree, 1)
            v.sem_inc(l_h, 1)
            phase_end(v)
            with v.Fori(0, LAYERS) as l:
                for conv, (H, width) in enumerate(((Hmid, F2), (Hout, F), (Hin, F))):
                    rows = 3 * (F, F2, F)[conv]

                    def scale(j):
                        c0, cn = CHUNKS[j]
                        k = conv * NCH + j
                        v.wait_ge(l_main, l * (3 * NCH) + (k + 1))
                        v.tensor_tensor(scaled[k % 3][0:rows, 0:cn], bank(k % 3, [cn], parts=rows),
                                        disB[0:rows, c0:c0 + cn], ALU.mult).then_inc(l_scaled, 1)

                    def store(j):
                        c0, cn = CHUNKS[j]
                        b0, m = c0 // P, cn // P
                        k = conv * NCH + j
                        v.wait_ge(l_g, l * (3 * NCH) + (k + 1))
                        got = bank(4, [4, F2])[:, 0:m, 0:width]
                        if conv < 2:
                            parts_of(H, b0, m, got, width).then_inc(l_h, 1)
                            v.drain()
                            return
                        mx, sm = zs[:, 0:m, 0], zs[:, 0:m, 1]
                        zz = z[:, 0:m, :]
                        v.tensor_tensor(zz, got, b3t.unsqueeze(1).to_broadcast([P, m, F]), ALU.add)
                        v.drain()
                        v.tensor_reduce(mx, zz, AX.X, ALU.max)
                        v.drain()
                        v.tensor_tensor(zz, zz, wide(mx, F), ALU.subtract).then_inc(l_mx, 1)
                        v.wait_ge(l_ex, l * NCH + (j + 1))
                        v.tensor_reduce(sm, zz, AX.X, ALU.add)
                        v.drain()
                        v.reciprocal(sm, sm)
                        v.drain()
                        v.tensor_tensor(x3[:, b0:b0 + m, :], zz, wide(sm, F), ALU.mult)
                        v.drain()
                        parts_of(H, b0, m, x3[:, b0:b0 + m, :], F).then_inc(l_h, 1)
                        v.drain()

                    if conv == 2:
                        v.wait_ge(l_w, l * (16 * WDMAS) + 16 * WDMAS)
                    for j in range(NCH):
                        scale(j)
                        if j >= 2:
                            store(j - 2)
                    store(NCH - 2)
                    store(NCH - 1)
                v.sem_inc(l_wfree, 1)
            v.tensor_tensor(x[:], x[:], x3, ALU.add)
            v.drain()
            phase_end(v)
            dve_layernorm(v, h2, lntmp, 3)
            v.wait_ge(load4, 16 * 7)
            v.tensor_copy(dst_f4, dst_i4)
            v.tensor_copy(tmp_src4, src_i2)
            v.drain()
            split_src(tmp_src4, hi_f4, lo_f4, onehot_hi2, tmp_c4)
            dve_table(v, table2, rest4, 128, 2)
            phase_end(v)
            sweep2.dve(v)
            phase_end(v)
            v.tensor_copy(agg_sb, sweep2.agg)
            v.drain().then_inc(agg_copied, 1)
            v.wait_ge(upd, 2)
            v.tensor_scalar(aggn, bank(7, [NB, F]), 1.0 / float(np.sqrt(F)), None, ALU.mult)
            v.drain().then_inc(updv, 1)
            for g, m in GROUPS:
                v.wait_ge(upd, 3 + g)
                prod = vprod[:, 0:m, :].rearrange("p t (h k) -> p t h k", k=F)
                v.tensor_tensor(prod, bank(g % 7, [2, 256])[:, 0:m, :].rearrange("p t (h k) -> p t h k", k=F),
                                aggn[:, 2 * g:2 * g + m, :].unsqueeze(3).to_broadcast([P, m, F, F]), ALU.mult)
                v.drain()
                v.tensor_reduce(u[:, 2 * g:2 * g + m, :], prod.rearrange("p t h k -> p t k h"), AX.X, ALU.add
                                ).then_inc(updv, 1)
                v.drain()
            v.tensor_tensor(x[:], x[:], h2, ALU.add)
            v.drain()
            v.wait_ge(upd, 4 + len(GROUPS))
            v.scalar_tensor_tensor(x[:], bank(7, [NB, F]), 1.0 / float(np.sqrt(F)), x[:], ALU.mult, ALU.add)
            v.drain()
            phase_end(v)
            dve_layernorm(v, h3, lntmp, 4)
            v.wait_ge(load5, 16 * 7)
            v.tensor_copy(type_f, type_f.bitcast(I32))
            v.tensor_copy(wab, wa[:, 1:2].to_broadcast([F, P]))
            v.wait_ge(rel_psum, 1)
            v.tensor_copy(rel, bank(7, [256], parts=NR))
            v.drain().then_inc(rel_sb, 1)
            v.sem_inc(att_sb, 1)
            v.wait_ge(att_psum, 1)
            v.tensor_copy(att, bank(7, [3], parts=F))
            v.tensor_copy(a2b, bank(7, [32])[:, 16:32])
            v.drain().then_inc(att_sb, 1)
            v.wait_ge(rel_in, 16)
            split3(v, [relp[:, i, :] for i in range(3)], rel, prest[0:NR, :])
            v.wait_ge(pf_psum, 1)
            v.tensor_copy(pf, bank(6, [NB, 3]))
            v.drain()
            v.tensor_copy(noderow[:, :, 0:F], h3)
            v.tensor_copy(noderow[:, :, F], pf[:, :, 0])
            v.drain().then_inc(row_sb, 1)
            split3(v, [pdst[:, :, i] for i in range(3)], pf[:, :, 2], prest[:, 0:NB])
            for c in range(NC // 101):
                cols = slice(c * 101, (c + 1) * 101)
                v.drain()
                v.tensor_tensor(e_chunk, attr16[:, cols, :], a2b.unsqueeze(1).to_broadcast([P, 101, F]), ALU.mult)
                v.drain()
                v.tensor_reduce(att_e[:, cols], e_chunk, AX.X, ALU.add)
            v.drain()
            phase_end(v)
            v.memset(block_lo[:], 0.0)
            v.drain()
            v.sem_inc(r_out, 1)
            with v.Fori(0, NB) as b:
                table = block_table(v, b)
                for s, n in block_steps(v, table):
                    v.tensor_scalar(dst_rel[:], dst_f5[:, bass.ds(s * QS, QS)], block_lo[:], None, ALU.subtract)
                    v.tensor_copy(cur[:], type_f[:, bass.ds(s * QS, QS)])
                    v.drain()
                    v.wait_ge(r_agg, n + 1)
                    for q in range(QS):
                        v.tensor_scalar(onehot5[:, q, :], iota128, dst_rel[:, q:q + 1], None, ALU.is_equal)
                    for q in range(QS):
                        op = v.tensor_scalar(onehot_ty[:, q, :], iotaNR, cur[:, q:q + 1], None, ALU.is_equal)
                    op.then_inc(r_onehots, 1)
                    v.wait_ge(r_hg, s + 1)
                    v.wait_ge(r_pd, n + 1)
                    v.tensor_tensor(es5, bank(4, [QS]), gathered[:, bass.ds(s * QS, QS), F], ALU.add)
                    v.drain()
                    v.tensor_tensor(es5b, es5, att_e[:, bass.ds(s * QS, QS)], ALU.add)
                    for r in range(2):
                        prod = prod5[:, 2 * r:2 * r + 2, :].rearrange("p q (i o) -> p q i o", o=F)
                        hs = gathered[:, bass.ds(s * QS + 2 * r, 2), 0:F]
                        v.wait_ge(r_prod, n * 2 + (r + 1))
                        v.tensor_tensor(prod, bank(2 + r, [2, 256]).rearrange("p q (i o) -> p q i o", o=F),
                                        hs.unsqueeze(3).to_broadcast([P, 2, F, F]), ALU.mult)
                        v.drain()
                        v.tensor_reduce(red5[:, 2 * r:2 * r + 2, :], prod.rearrange("p q i o -> p q o i"),
                                        AX.X, ALU.add)
                    v.drain()
                    v.tensor_tensor(msg5, red5, wide(es5b, F), ALU.mult).then_inc(r_msg, 1)
                v.wait_ge(r_agg, table[2] + table[1] + 1)
                xb = x[:, bass.ds(b, 1), :].rearrange("p a f -> p (a f)")
                v.tensor_tensor(xb, bank(5, [F]), xb, ALU.add).then_inc(r_out, 1)
                v.tensor_scalar(block_lo[:], block_lo[:], float(P), None, ALU.add)
                v.drain()
            phase_end(v)


_ORDER = ["x", "src", "dst", "dstrow", "type", "attr2", "attr8", "attr16", "w0", "w1", "b1", "w2", "b2",
          "w3", "b3", "wmt", "wml", "wut", "wul", "ws", "wa", "wv", "wct"]


def kernel(**inputs):
    import numpy as _np
    import concourse.bacc as _bacc
    from concourse import mybir as _mybir
    from concourse.bass_utils import run_bass_kernel_spmd as _run

    i = {k: _np.asarray(v) for k, v in inputs.items()}

    def edges(a, pad):
        full = _np.full((NS * STEP,) + a.shape[1:], pad, a.dtype)
        full[:E] = a
        full = full.reshape((NS, P, QS) + a.shape[1:])
        return _np.ascontiguousarray(_np.moveaxis(full, 1, 0).reshape((P, NC) + a.shape[1:]))

    nodes = _np.zeros((NP, F), i["x"].dtype)
    nodes[:N] = i["x"]
    absent = 2 * NP - 1
    dstrow = _np.full((NS * STEP,), absent, i["dst"].dtype)
    dstrow[:E] = i["dst"]
    a = {
        "x": nodes.reshape(NB, P, F).transpose(1, 0, 2), "src": edges(i["src"], 0),
        "dst": edges(i["dst"], absent), "dstrow": dstrow.reshape(TPP, 2 * STEP),
        "type": edges(i["edge_type_90"], 0), "attr2": edges(i["edge_attr_2"], 0),
        "attr8": edges(i["edge_attr_8"], 0), "attr16": edges(i["edge_attr_16"], 0),
        "w0": i["L0_gnn_W"], "w1": i["L1_gnn_W1"], "b1": i["L1_gnn_b1"], "w2": i["L1_gnn_W2"],
        "b2": i["L1_gnn_b2"], "w3": i["L1_gnn_W3"], "b3": i["L1_gnn_b3"], "wmt": i["L2_gnn_W_msg_tp"],
        "wml": i["L2_gnn_W_msg_lin"], "wut": i["L2_gnn_W_upd_tp"], "wul": i["L2_gnn_W_upd_lin"],
        "ws": i["L3_gnn_Ws"], "wa": i["L3_gnn_Wa"].reshape(3, F).T,
        "wv": i["L3_gnn_weight"].reshape(F, NBASE, F), "wct": i["L3_gnn_w_comp"].T,
    }
    a = {f"in_{k}": _np.ascontiguousarray(v) for k, v in a.items()}
    nc = _bacc.Bacc("TRN2", target_bir_lowering=False, num_devices=1)
    args = [nc.dram_tensor(f"in_{k}", a[f"in_{k}"].shape, _mybir.dt.from_np(a[f"in_{k}"].dtype),
                           kind="ExternalInput").ap() for k in _ORDER]
    result = nc.dram_tensor("result", (N, F), _mybir.dt.float32, kind="ExternalOutput").ap()
    gnn(nc, *args, result)
    r = _run(nc, [a], core_ids=[0])
    return r.results[0]["result"]
```

```python
from contextlib import ExitStack

import numpy as np

import concourse.bass as bass
import concourse.mybir as mybir
from concourse.alu_op_type import AluOpType as ALU

ACT = mybir.ActivationFunctionType
AX = mybir.AxisListType
F32, BF16, F16, I32 = mybir.dt.float32, mybir.dt.bfloat16, mybir.dt.float16, mybir.dt.int32
BYTES = {F32: 4, I32: 4, BF16: 2, F16: 2}

P = 128
N, E, F = 3125, 103125, 16
NB = -(-N // P)
NP = NB * P
QS = 4
STEP = P * QS
NS = -(-E // STEP)
NC = NS * QS
HI, LO = 8, NP // 8
HALF = NP // 2
NR, NBASE = 90, 30
WORK = 19760
LAYERS, F1, F2 = 5, 64, 32
BANK = 512
CHUNKS = [(j * BANK, min(BANK, NP - j * BANK)) for j in range(-(-NP // BANK))]
NCH = len(CHUNKS)
EPS = 1e-5
GROW = F + 1
RCHUNK = 30
GQ = 2 * QS
NG = NC // GQ
ROWBUFS = 6
ENGINES = 5
TPP = NS // 2


def gnn(nc, x_in, src_in, dst_in, dstrow_in, type_in, attr2_in, attr8_in, attr16_in, w0_in,
        w1_in, b1_in, w2_in, b2_in, w3_in, b3_in, wmt_in, wml_in, wut_in, wul_in, ws_in, wa_in,
        wv_in, wct_in, out):
    range_dram = nc.dram_tensor("step_range", (2, NS), F32, kind="Internal").ap()
    table_dram = nc.dram_tensor("block_steps", (NB, 4), I32, kind="Internal").ap()
    rel_dram = nc.dram_tensor("relation_weights", (F * NR * F,), F32, kind="Internal").ap()
    rows_dram = nc.dram_tensor("relation_rows", (NP * NR, GROW), F32, kind="Internal").ap()

    with ExitStack() as ctx:
        def sb(name, shape, dt):
            return ctx.enter_context(nc.sbuf_tensor(name, shape, dt))

        def sem(name):
            return ctx.enter_context(nc.semaphore(name))

        def shaped(ap, shape):
            names = "abcd"[:len(shape)]
            if len(shape) == 1:
                return ap
            return ap.rearrange(f"p ({' '.join(names)}) -> p {' '.join(names)}",
                                **{k: d for k, d in zip(names, shape)})

        x = sb("x", [P, NB, F], F32)
        ident = sb("ident", [P, P], F32)
        ident_bf = sb("ident_bf", [P, P], BF16)
        ident_h = sb("ident_h", [P, P], F16)
        iota = sb("iota", [P, NP], F16)
        iota128, iotaLO, iotaNR = iota[:, HALF:HALF + P], iota[:, HALF:HALF + LO], iota[:, HALF:HALF + 96]
        steps_row = sb("steps_row", [1, NB * 4], I32)
        block_lo = sb("block_lo", [P, 1], F32)
        prev_block = sb("prev_block", [1, NB], I32)
        dst_rel = sb("dst_rel", [P, QS], F32)
        cur = sb("cur", [P, QS], F32)
        stat = sb("stat", [P, NB, 4], F32)
        eps_t = sb("eps_t", [P, 1], F32)

        big = sb("big", [P, NB * NP], F16)
        work = sb("work", [P, WORK], F16)

        class Region:
            def __init__(self, tensor, size):
                self.tensor, self.size, self.at = tensor, size, 0

            def take(self, shape, dt, parts=P):
                n = int(np.prod(shape)) * BYTES[dt] // 2
                ap = self.tensor[0:parts, self.at:self.at + n]
                self.at += n + (-n) % 2
                assert self.at <= self.size, (self.at, self.size)
                return shaped(ap if dt == F16 else ap.bitcast(dt), list(shape))

        def regions():
            return Region(big, NB * NP), Region(work, WORK)

        psum = ctx.enter_context(nc.psum_tensor("psum", [P, 8, BANK], F32))

        def bank(i, shape, dt=F32, parts=P, count=1):
            n = int(np.prod(shape)) * BYTES[dt] // 4
            ap = psum[0:parts, i:i + count, :].rearrange("p a b -> p (a b)")[:, 0:n]
            return shaped(ap if dt == F32 else ap.bitcast(dt), list(shape))

        phase_done = sem("phase_done")
        phase_no = {}

        def phase_end(eng):
            phase_no[eng] = phase_no.get(eng, 0) + 1
            eng.drain().then_inc(phase_done, 1)
            eng.wait_ge(phase_done, ENGINES * phase_no[eng])

        def block_table(eng, b):
            def entry(k, least, most):
                return eng.value_load(steps_row[0:1, bass.ds(b * 4 + k, 1)], min_val=least, max_val=most)
            return entry(0, 0, NS - 2), entry(1, 2, NS), entry(2, 0, NB * NS)

        def total_steps(eng):
            return eng.value_load(steps_row[0:1, 3:4], min_val=1, max_val=NB * NS)

        def block_steps(eng, table, start=0):
            first, count, base = table
            with eng.Fori(start, count) as i:
                s = nc.s_assert_within(first + i, 0, NS - 1,
                                       skip_runtime_bounds_check_because="first + count is at most NS")
                yield s, base + i

        def split3(v, parts, src, rest):
            v.tensor_copy(parts[0], src)
            v.drain()
            v.tensor_tensor(rest, src, parts[0], ALU.subtract)
            v.drain()
            v.tensor_copy(parts[1], rest)
            v.drain()
            v.tensor_tensor(rest, rest, parts[1], ALU.subtract)
            v.drain()
            return v.tensor_copy(parts[2], rest)

        def wide(ap, n):
            return ap.unsqueeze(2).to_broadcast([ap.shape[0], ap.shape[1], n])

        ln_var = sem("ln_var")
        ln_std = sem("ln_std")
        ln_done = sem("ln_done")

        def dve_layernorm(v, h, tmp, k):
            mean, var, rstd = stat[:, :, 0], stat[:, :, 1], stat[:, :, 3]
            v.tensor_reduce(mean, x[:], AX.X, ALU.add)
            v.drain()
            v.tensor_scalar(mean, mean, 1.0 / F, None, ALU.mult)
            v.drain()
            v.tensor_tensor(h, x[:], wide(mean, F), ALU.subtract)
            v.drain()
            v.tensor_tensor(tmp, h, h, ALU.mult)
            v.drain()
            v.tensor_reduce(var, tmp, AX.X, ALU.add)
            v.drain()
            v.tensor_scalar(var, var, 1.0 / F, EPS, ALU.mult, ALU.add).then_inc(ln_var, 1)
            v.wait_ge(ln_std, k)
            v.reciprocal(rstd, stat[:, :, 2])
            v.drain()
            v.tensor_tensor(h, h, wide(rstd, F), ALU.mult)
            v.drain()
            v.tensor_scalar(h, h, 0.0, None, ALU.max).then_inc(ln_done, 1)

        def act_layernorm(a, k):
            a.wait_ge(ln_var, k)
            a.activation(stat[:, :, 2], stat[:, :, 1], ACT.Sqrt).then_inc(ln_std, 1)

        hT_psum = sem("hT_psum")
        hT_done = sem("hT_done")

        def pe_transpose_nodes(pe, h, k):
            for b in range(NB):
                mm = pe.transpose(bank(0, [NP], parts=F, count=7)[:, b * P:(b + 1) * P], h[:, b, :], ident[:])
            mm.then_inc(hT_psum, 1)

        def act_copy_nodes(a, hT, k):
            a.wait_ge(hT_psum, k)
            a.activation(hT, bank(0, [NP], parts=F, count=7), ACT.Copy).then_inc(hT_done, 1)

        GROUPS = [(g, min(2, NB - 2 * g)) for g in range(-(-NB // 2))]
        tab_psum = sem("tab_psum")
        tab_free = sem("tab_free")

        def pe_table(pe, hT, w, width, k):
            pe.wait_ge(hT_done, k)
            for g, m in GROUPS:
                if g >= 7:
                    pe.wait_ge(tab_free, len(GROUPS) * (k - 1) + g - 6)
                for t in range(m):
                    b = 2 * g + t
                    mm = pe.matmul(bank(g % 7, [2, 256])[:, t, 0:width], hT[:, b * P:(b + 1) * P], w,
                                   start=True, stop=True)
                mm.then_inc(tab_psum, 1)

        def dve_table(v, table, rest, width, k):
            for g, m in GROUPS:
                v.wait_ge(tab_psum, len(GROUPS) * (k - 1) + g + 1)
                split3(v, [table[:, 2 * g:2 * g + m, i, :] for i in range(3)],
                       bank(g % 7, [2, 256])[:, 0:m, 0:width], rest[:, 0:m, 0:width]).then_inc(tab_free, 1)
                v.drain()

        class Sweep:

            def __init__(self, tag, silu, K):
                self.silu, self.K, self.width = silu, K, K * F
                self.onehot_ready = sem(f"{tag}_onehot_ready")
                self.onehotT_psum = sem(f"{tag}_onehotT_psum")
                self.onehotT_ready = sem(f"{tag}_onehotT_ready")
                self.products_ready = sem(f"{tag}_products_ready")
                self.products_used = sem(f"{tag}_products_used")
                self.msg_ready = sem(f"{tag}_msg_ready")
                self.msg_spread = sem(f"{tag}_msg_spread")
                self.silu_done = sem(f"{tag}_silu_done")
                self.lo_ready = sem(f"{tag}_lo_ready")
                self.scatter_done = sem(f"{tag}_scatter_done")

            def place(self, dst_f, lo_f, onehot_hi, coef, table, W):
                self.dst_f, self.lo_f, self.onehot_hi, self.coef, self.table = dst_f, lo_f, onehot_hi, coef, table
                self.onehot = W.take([QS, P], BF16)
                self.onehotT = W.take([QS, P], BF16)
                self.prod = W.take([QS, 256], F32)
                self.msg = W.take([QS, F], F32)
                self.smsg = W.take([QS, F], F32)
                self.spread = W.take([QS, HI, F], F32)
                self.onehot_lo = W.take([QS, LO], F32)
                self.psT = bank(0, [QS, P], BF16)
                self.products = [bank(1 + r, [2, 256])[:, :, 0:self.width] for r in range(2)]
                self.agg = bank(3, [LO])

            def onehots_lo(self, v):
                for q in range(QS):
                    op = v.tensor_scalar(self.onehot_lo[:, q, :], iotaLO, cur[:, q:q + 1], None, ALU.is_equal)
                return op

            def dve(self, v):
                prev = self.silu_done if self.silu else self.msg_spread
                v.memset(block_lo[:], 0.0)
                v.memset(cur[:], -1.0)
                v.memset(self.onehot_lo, 0.0)
                v.drain()
                v.sem_inc(self.products_used, 2)
                with v.Fori(0, NB) as b:
                    for s, n in block_steps(v, block_table(v, b)):
                        v.tensor_scalar(dst_rel[:], self.dst_f[:, bass.ds(s * QS, QS)], block_lo[:], None, ALU.subtract)
                        v.drain()
                        for q in range(QS):
                            op = v.tensor_scalar(self.onehot[:, q, :], iota128, dst_rel[:, q:q + 1], None, ALU.is_equal)
                        op.then_inc(self.onehot_ready, 1)
                        v.wait_ge(self.scatter_done, n + 1)
                        self.onehots_lo(v).then_inc(self.lo_ready, 1)
                        v.drain()
                        v.tensor_copy(cur[:], self.lo_f[:, bass.ds(s * QS, QS)])
                        for r in range(2):
                            half = slice(2 * r, 2 * r + 2)
                            prod = self.prod[:, half, 0:self.width].rearrange("p q (k o) -> p q k o", o=F)
                            coef = self.coef[:, bass.ds(s * QS + 2 * r, 2), :]
                            v.wait_ge(self.products_ready, n * 2 + (r + 1))
                            v.tensor_tensor(prod, self.products[r].rearrange("p q (k o) -> p q k o", o=F),
                                            coef.unsqueeze(3).to_broadcast([P, 2, self.K, F]),
                                            ALU.mult).then_inc(self.products_used, 1)
                            v.drain()
                            v.wait_ge(prev, n * 2 + (r + 1))
                            v.tensor_reduce(self.msg[:, half, :], prod.rearrange("p q k o -> p q o k"),
                                            AX.X, ALU.add).then_inc(self.msg_ready, 1)
                    v.drain()
                    v.tensor_scalar(block_lo[:], block_lo[:], float(P), None, ALU.add)
                    v.drain()
                total = total_steps(v)
                v.wait_ge(self.scatter_done, total + 1)
                self.onehots_lo(v).then_inc(self.lo_ready, 1)

            def act(self, a):
                if self.silu:
                    a.sem_inc(self.silu_done, 2)
                with a.Fori(0, NB) as b:
                    for s, n in block_steps(a, block_table(a, b)):
                        a.wait_ge(self.onehotT_psum, n + 1)
                        a.activation(self.onehotT, self.psT, ACT.Copy).then_inc(self.onehotT_ready, 1)
                        if self.silu:
                            for r in range(2):
                                half = slice(2 * r, 2 * r + 2)
                                a.wait_ge(self.msg_ready, n * 2 + (r + 1))
                                a.wait_ge(self.msg_spread, n * 2 + (r + 1))
                                a.activation(self.smsg[:, half, :], self.msg[:, half, :], ACT.Silu,
                                             scale=1.0 / float(np.sqrt(F * self.K))).then_inc(self.silu_done, 1)
                        a.wait_ge(self.products_ready, n * 2 + 2)

            def pool(self, g):
                g.memset(self.spread, 0.0)
                g.drain()
                g.sem_inc(self.msg_spread, 2)
                with g.Fori(0, NB) as b:
                    for s, n in block_steps(g, block_table(g, b)):
                        g.wait_ge(self.scatter_done, n + 2)
                        for r in range(2):
                            half = slice(2 * r, 2 * r + 2)
                            if self.silu:
                                g.wait_ge(self.silu_done, n * 2 + (r + 3))
                            else:
                                g.wait_ge(self.msg_ready, n * 2 + (r + 1))
                            msg = (self.smsg if self.silu else self.msg)[:, half, :]
                            hi = self.onehot_hi[:, bass.ds(s * QS + 2 * r, 2), :]
                            g.tensor_tensor(self.spread[:, half, :, :],
                                            msg.unsqueeze(2).to_broadcast([P, 2, HI, F]),
                                            hi.unsqueeze(3).to_broadcast([P, 2, HI, F]),
                                            ALU.mult).then_inc(self.msg_spread, 1)

            def scatter(self, pe, qs=range(QS), start=False):
                for q in qs:
                    mm = pe.matmul(self.agg, self.spread[:, q, :, :].rearrange("p h o -> p (h o)"),
                                   self.onehot_lo[:, q, :], start=start, stop=True, skip_group_check=True)
                return mm

            def zero(self, pe):
                return self.scatter(pe, [0], True)

            def pe(self, pe):
                pe.wait_ge(self.msg_spread, 2)
                pe.wait_ge(self.products_used, 2)
                self.zero(pe).then_inc(self.scatter_done, 1)
                with pe.Fori(0, NB) as b:
                    for s, n in block_steps(pe, block_table(pe, b)):
                        pe.wait_ge(self.onehot_ready, n + 1)
                        for q in range(QS):
                            mm = pe.transpose(self.psT[:, q, :], self.onehot[:, q, :], ident_bf[:])
                        mm.then_inc(self.onehotT_psum, 1)
                        pe.wait_ge(self.onehotT_ready, n + 1)
                        for r in range(2):
                            pe.wait_ge(self.products_used, n * 2 + (r + 1))
                            for t in range(2):
                                for i in range(3):
                                    row = self.table[:, bass.ds(b, 1), i, :].rearrange("p a w -> p (a w)")
                                    mm = pe.matmul(self.products[r][:, t, :], self.onehotT[:, 2 * r + t, :],
                                                   row, start=(i == 0), stop=(i == 2))
                            mm.then_inc(self.products_ready, 1)
                        pe.wait_ge(self.lo_ready, n + 1)
                        pe.wait_ge(self.msg_spread, n * 2 + 2)
                        self.scatter(pe).then_inc(self.scatter_done, 1)
                total = total_steps(pe)
                pe.wait_ge(self.lo_ready, total + 1)
                pe.wait_ge(self.msg_spread, total * 2 + 2)
                self.scatter(pe)

        sweep0 = Sweep("spline", False, 16)
        sweep2 = Sweep("tensor", True, 8)

        agg_copied = sem("agg_copied")
        agg_moved = sem("agg_moved")

        def sync_regroup(sp, agg_sb, aggT, k):
            sp.wait_ge(agg_copied, k)
            for h in range(HI):
                sp.dma_start(aggT[0:F, h * LO:(h + 1) * LO], agg_sb[h * F:(h + 1) * F, :]).then_inc(agg_moved, 16)

        B1, W1 = regions()
        hT = B1.take([NP], F32, parts=F)
        attr2 = B1.take([NC, 2], F32)
        hats = B1.take([NC, 2, 4], F32)
        basis = B1.take([NC, 4, 4], F32)
        table0 = B1.take([NB, 3, 256], BF16)
        dst_i = B1.take([NC], I32)
        src_i = B1.take([NC], I32)
        dst_f = W1.take([NC], F32)
        src_c = W1.take([NC], F32)
        W1_keep = W1.at
        h0 = B1.take([NB, F], F32)
        lntmp0 = B1.take([NB, F], F32)
        lnwork = Region(work, WORK)
        lnwork.at = 2 * NB * F
        lntmp = lnwork.take([NB, F], F32)
        lo_f = W1.take([NC], F32)
        mark = W1.at
        rest = W1.take([2, 256], F32)
        hi_f = W1.take([NC], F32)
        tmp_c = W1.take([NC], F32)
        w0 = W1.take([256], F32, parts=F)
        centers = W1.take([4], F32)
        W1b = Region(work, WORK)
        W1b.at = mark
        dst_rows = hats.rearrange("p a b c -> p (a b c)")[0:TPP, 0:2 * STEP]
        dst_rows_i = basis.rearrange("p a b c -> p (a b c)").bitcast(I32)[0:TPP, 0:2 * STEP]
        bx = table0.rearrange("p a b c -> p (a b c)").bitcast(F32)
        step_mm = bx[0:TPP, 0:4].rearrange("p (k t) -> p k t", k=2)
        step_rng = bx[0:NB, 8:8 + 2 * NS].rearrange("p (k t) -> p k t", k=2)
        step_no = bx[0:NB, 1000:1000 + NS]
        step_left = bx[0:NB, 1500:1500 + NS]
        flags = bx[0:NB, 2000:2000 + NS]
        thr = bx[0:NB, 2500:2502]
        bounds = bx[0:NB, 2510:2518]
        before = bx[0:NB, 2600:2600 + NB]
        ones25 = bx[0:NB, 2700:2700 + NB]
        bounds_i = bx[0:NB, 2800:2804].bitcast(I32)

        loaded = sem("loaded")
        consts = sem("consts")
        rng_copied = sem("rng_copied")
        rng_out = sem("rng_out")
        rng_in = sem("rng_in")
        count_ready = sem("count_ready")
        base_ready = sem("base_ready")
        bounds_ready = sem("bounds_ready")
        bounds_out = sem("bounds_out")
        bounds_in = sem("bounds_in")
        LOADS1 = 7

        onehot_hi = B1.take([NC, HI], BF16)

        sweep0.place(dst_f, lo_f, onehot_hi, basis.rearrange("p c a b -> p c (a b)"), table0, W1b)

        B2, W2 = regions()
        A = B2.take([NB, NP], F16)
        W2.at = W1_keep
        onehot_src = W2.take([QS, NP], BF16)
        onehot_dst = W2.take([QS, P], BF16)
        counts = W2.take([NP], F16)
        a_loops = sem("a_loops_added")
        a_ready = sem("a_onehots_ready")
        a_used = sem("a_onehots_used")
        a_counts = sem("a_counts_copied")
        a_turned = sem("a_turned")
        a_stored = sem("a_stored")
        TURN = [(g * 8, min(8, NB - g * 8)) for g in range(-(-NB // 8))]

        B3, W3 = regions()
        W3.at = 2 * NB * F * 2
        hn = Region(work, WORK).take([NB, F], F32)
        disB = W3.take([NP], F32, parts=96)
        scaled = [W3.take([BANK], F32, parts=96) for _ in range(3)]
        xT = W3.take([BANK], F32, parts=F1)
        Hin = W3.take([NB, 3, F], BF16)
        Hmid = W3.take([NB, 3, F2], BF16)
        Hout = W3.take([NB, 3, F], BF16)
        dis = W3.take([NB], F32)
        W1s = W3.take([96], F32, parts=3 * F)
        S2 = W3.take([F2], F32, parts=96)
        S3 = W3.take([F], F32, parts=3 * F)
        W2w = W3.take([F2], F32, parts=F1)
        W3w = W3.take([F], F32, parts=F2)
        b1t = W3.take([1], F32, parts=F1)
        b2t = W3.take([1], F32, parts=F2)
        b3t = W3.take([F], F32)
        gtmp = W3.take([4, F2], F32)
        grest = W3.take([4, F2], F32)
        z = W3.take([4, F], F32)
        zs = W3.take([4, 4], F32)
        x3 = lntmp
        ones96 = W3.take([96], BF16)

        l_w = sem("l_weights")
        l_wfree = sem("l_weights_free")
        l_main = sem("l_main")
        l_scaled = sem("l_scaled")
        l_z = sem("l_z")
        l_relu = sem("l_relu")
        l_g = sem("l_g")
        l_h = sem("l_h")
        l_mx = sem("l_softmax_in")
        l_ex = sem("l_softmax_exp")
        d_ones = sem("d_ones")
        d_main = sem("d_main")
        d_deg = sem("d_deg")
        d_sqrt = sem("d_sqrt")
        d_inv = sem("d_inv")
        d_node = sem("d_node")
        h_in = sem("h_in")
        WDMAS = 8

        B4, W4 = regions()
        h2T = B4.take([NP], F32, parts=F)
        aggT = B4.take([NP], F32, parts=F)
        uT = B4.take([NP], F32, parts=F)
        attr8 = B4.take([NC, 8], F32)
        table2 = B4.take([NB, 3, 128], BF16)
        onehot_hi2 = B4.take([NC, HI], BF16)
        src_i2 = B4.take([NC], I32)
        agg_sb = B4.take([LO], F32)
        aggn = B4.take([NB, F], F32)
        u = B4.take([NB, F], F32)
        vprod = B4.take([2, 256], F32)
        wmt = B4.take([128], F32, parts=F)
        wml = B4.take([F], F32, parts=F)
        wut = B4.take([256], F32, parts=F)
        wul = B4.take([F], F32, parts=F)
        h2 = Region(work, WORK).take([NB, F], F32)
        W4.at = 2 * NB * F * 2
        dst_f4 = W4.take([NC], F32)
        lo_f4 = W4.take([NC], F32)
        mark4 = W4.at
        hi_f4 = W4.take([NC], F32)
        tmp_c4 = W4.take([NC], F32)
        rest4 = W4.take([2, 256], F32)
        dst_i4 = W4.take([NC], I32)
        tmp_src4 = W4.take([NC], F32)
        W4b = Region(work, WORK)
        W4b.at = mark4
        sweep2.place(dst_f4, lo_f4, onehot_hi2, attr8, table2, W4b)

        agg_sb0 = Region(big, NB * NP)
        agg_sb0.at = NP * 2
        agg0 = agg_sb0.take([LO], F32)
        aggT0 = agg_sb0.take([NP], F32, parts=F)

        B5, W5 = regions()
        h3T = B5.take([NP], F32, parts=F)
        attr16 = B5.take([NC, F], F32)
        gathered = B5.take([NC, GROW], F32)
        blocks_out = Region(big, NB * NP)
        blocks_out.at = h3T.shape[1] * 2 + NC * F * 2
        rows_sb = [blocks_out.take([NR, GROW], F32) for _ in range(ROWBUFS)]
        row_no = B5.take([NC], I32)
        src_f5 = B5.take([NC], F32)
        att_e = B5.take([NC], F32)
        type_f = B5.take([NC], F32)
        rel = B5.take([256], F32, parts=NR)
        wrel = B5.take([NR, GROW], F32, parts=F)
        wct = B5.take([NR], F32, parts=NBASE)
        wv = B5.take([256], F32, parts=NBASE)
        ws = B5.take([F], F32, parts=F)
        wa = B5.take([3], F32, parts=F)
        wab = B5.take([P], F32, parts=F)
        att = B5.take([3], F32, parts=F)
        a2b = B5.take([F], F32)
        att_d = B5.take([NB], F32)
        h3 = Region(work, WORK).take([NB, F], F32)
        W5.at = 2 * NB * F * 2
        dst_f5 = W5.take([NC], F32)
        zero5 = W5.take([P], F32)
        mark5 = W5.at
        e_chunk = W5.take([101, F], F32)
        W5b = Region(work, WORK)
        W5b.at = mark5
        onehot5 = [W5b.take([QS, P], F32) for _ in range(2)]
        pay5 = [W5b.take([QS, 2, F], F32) for _ in range(2)]
        es5 = W5b.take([QS], F32)
        sum5 = W5b.take([F], F32)
        stage = [W5b.take([GQ, GROW], F32) for _ in range(2)]
        stage_idx = [W5b.take([GQ], I32) for _ in range(2)]
        r_edges = sem("r_edges_ready")
        r_agg = sem("r_agg_done")
        r_out = sem("r_out_added")
        r_gath = [sem(f"r_gather_{i}") for i in range(2)]
        r_kept = sem("r_rows_kept")
        r_idx = sem("r_row_numbers_staged")
        r_started = sem("r_gathers_started")
        t_psum = sem("t_products_ready")
        t_act = sem("t_act_copied")
        t_dve = sem("t_dve_copied")
        t_out = [sem(f"t_rows_out_{i}") for i in range(ROWBUFS)]
        load5 = sem("load5")
        rel_psum = sem("rel_psum")
        rel_sb = sem("rel_sb")
        rel_out = sem("rel_out")
        rel_in = sem("rel_in")
        att_psum = sem("att_psum")
        att_sb = sem("att_sb")
        att_d_psum = sem("att_d_psum")
        load4 = sem("load4")
        upd = sem("upd")
        updv = sem("updv")
        upda = sem("upda")
        out_sem = sem("out_sem")

        block = ctx.enter_context(nc.Block())

        @block.sync
        def _(sp):
            def ld(dst, src, s):
                sp.dma_start(dst, src).then_inc(s, 16)
            ld(dst_rows_i, dstrow_in, loaded)
            ld(x[:], x_in, loaded)
            ld(dst_i, dst_in, loaded)
            ld(src_i, src_in, loaded)
            ld(attr2, attr2_in, loaded)
            ld(w0.rearrange("i (k o) -> i k o", o=F), w0_in.rearrange("k i o -> i k o"), loaded)
            sp.wait_ge(rng_copied, 1)
            ld(range_dram.rearrange("k (p t) -> p k t", t=2), step_mm, rng_out)
            sp.wait_ge(rng_out, 16)
            ld(step_rng, range_dram.partition_broadcast(NB), rng_in)
            sp.wait_ge(bounds_ready, 1)
            ld(table_dram, bounds_i, bounds_out)
            sp.wait_ge(bounds_out, 16)
            ld(steps_row[0:1, :], table_dram.rearrange("(a b) k -> a (b k)", a=1), bounds_in)
            sp.wait_ge(bounds_in, 16)
            phase_end(sp)
            phase_end(sp)
            sync_regroup(sp, agg0, aggT0, 1)
            phase_end(sp)
            phase_end(sp)
            phase_end(sp)
            with sp.Fori(0, LAYERS) as l:
                one = bass.ds(l, 1)
                sp.wait_ge(l_wfree, l + 1)
                for i in range(3):
                    ld(W1s[i * F:(i + 1) * F, 0:F1], w1_in[one, :, :].rearrange("a i o -> (a i) o"), l_w)
                ld(W2w, w2_in[one, :, :].rearrange("a i o -> (a i) o"), l_w)
                ld(W3w, w3_in[one, :, :].rearrange("a i o -> (a i) o"), l_w)
                ld(b1t, b1_in[one, :].rearrange("a (i o) -> (a i) o", o=1), l_w)
                ld(b2t, b2_in[one, :].rearrange("a (i o) -> (a i) o", o=1), l_w)
                ld(b3t, b3_in[one, :].rearrange("a o -> (a o)").partition_broadcast(P), l_w)
            phase_end(sp)
            ld(dst_i4, dst_in, load4)
            ld(src_i2, src_in, load4)
            ld(attr8, attr8_in, load4)
            ld(wmt, wmt_in.rearrange("i j h -> i (j h)"), load4)
            ld(wml, wml_in, load4)
            ld(wut, wut_in.rearrange("i h k -> i (h k)"), load4)
            ld(wul, wul_in, load4)
            phase_end(sp)
            phase_end(sp)
            sync_regroup(sp, agg_sb, aggT, 2)
            phase_end(sp)
            ld(attr16, attr16_in, load5)
            ld(row_no, src_in, load5)
            ld(type_f.bitcast(I32), type_in, load5)
            ld(wct, wct_in, load5)
            ld(wv.rearrange("b (i o) -> b i o", o=F), wv_in.rearrange("i b o -> b i o"), load5)
            ld(ws, ws_in, load5)
            ld(wa, wa_in, load5)
            sp.wait_ge(rel_sb, 1)
            ld(rel_dram.rearrange("(i r o) -> r i o", i=F, r=NR), rel.rearrange("r (i o) -> r i o", o=F), rel_out)
            sp.wait_ge(rel_out, 16)
            ld(wrel[:, :, 0:F], rel_dram.rearrange("(r i o) -> i r o", i=F, r=NR), rel_in)
            for b in range(NB):
                sp.wait_ge(t_act, 2 * b + 2)
                sp.wait_ge(t_dve, b + 1)
                ld(rows_dram[b * P * NR:(b + 1) * P * NR, :].rearrange("(p r) c -> p r c", r=NR),
                   rows_sb[b % ROWBUFS], t_out[b % ROWBUFS])
            for i in range(ROWBUFS):
                sp.wait_ge(t_out[i], 16 * len(range(i, NB, ROWBUFS)))
            phase_end(sp)
            phase_end(sp)
            full = N // P
            ld(out[0:full * P, :].rearrange("(b p) c -> p b c", p=P), x[:, 0:full, :], out_sem)
            ld(out[full * P:N, :], x[0:N - full * P, full, :], out_sem)
            sp.wait_ge(out_sem, 32)

        @block.gpsimd
        def _(g):
            g.iota(iota[:], [[1, NP]], base=-HALF, channel_multiplier=0, allow_small_or_imprecise_dtypes=True)
            g.iota(step_no, [[1, NS]], base=1, channel_multiplier=0, allow_small_or_imprecise_dtypes=True)
            g.iota(step_left, [[-1, NS]], base=NS, channel_multiplier=0, allow_small_or_imprecise_dtypes=True)
            g.iota(thr[:, 0:1], [[1, 1]], base=0, channel_multiplier=P, allow_small_or_imprecise_dtypes=True)
            g.iota(thr[:, 1:2], [[1, 1]], base=P - 1, channel_multiplier=P, allow_small_or_imprecise_dtypes=True)
            g.iota(prev_block[:], [[1, NB]], base=-1, channel_multiplier=0)
            g.drain()
            g.memset(prev_block[0:1, 0:1], NB - 1)
            g.memset(ident[:], 0.0)
            g.memset(before, 1.0)
            g.memset(ones25, 1.0)
            for j in range(4):
                g.memset(centers[:, j:j + 1], -1.0 + 2.0 * j / 3.0)
            g.drain()
            g.affine_select(out=ident[:], in_=ident[:], compare_op=ALU.not_equal, fill=1.0, base=0,
                            pattern=[[-1, P]], channel_multiplier=1)
            g.affine_select(out=before, in_=before, compare_op=ALU.is_gt, fill=0.0, base=0,
                            pattern=[[1, NB]], channel_multiplier=-1)
            g.drain()
            g.tensor_copy(ident_bf[:], ident[:])
            g.tensor_copy(ident_h[:], ident[:])
            g.drain().then_inc(consts, 1)
            phase_end(g)
            sweep0.pool(g)
            phase_end(g)
            phase_end(g)
            phase_end(g)
            phase_end(g)
            phase_end(g)
            phase_end(g)
            sweep2.pool(g)
            phase_end(g)
            phase_end(g)
            g.memset(zero5, 0.0)
            phase_end(g)

            def gather(i, group):
                g.wait_ge(r_kept, group * 2 + 2)
                g.tensor_copy(stage_idx[i], row_no[:, bass.ds(group * GQ, GQ)]).then_inc(r_idx, 1)
                g.wait_ge(r_idx, group + 1)
                g.sem_inc(r_started, 1)
                for q in range(GQ):
                    g.indirect_dma_start(out=stage[i][:, q, :], out_offset=None, in_=rows_dram,
                                         in_offset=bass.IndirectOffsetOnAxis(ap=stage_idx[i][:, q:q + 1], axis=0)
                                         ).then_inc(r_gath[i], 16)

            with g.Fori(0, NG // 2) as k:
                gather(0, k * 2)
                gather(1, k * 2 + 1)
            gather(0, NG - 1)
            phase_end(g)

        @block.scalar
        def _(a):
            act_layernorm(a, 1)
            act_copy_nodes(a, hT, 1)
            phase_end(a)
            sweep0.act(a)
            phase_end(a)
            phase_end(a)
            def store_turned(before, column):
                for g, (s0, sn) in enumerate(TURN):
                    a.wait_ge(a_turned, before + (g + 1))
                    a.activation(A[:, s0:s0 + sn, column], bank(7, [sn, P], F16), ACT.Copy).then_inc(a_stored, 1)

            with a.Fori(0, NB) as b:
                _, count, base = block_table(a, b)
                prev = a.value_load(prev_block[0:1, bass.ds(b, 1)], min_val=0, max_val=NB - 1)
                store_turned(b * len(TURN), bass.ds(prev * P, P))
                a.wait_ge(a_used, (base + count) * QS + QS)
                for j, (c0, cn) in enumerate(CHUNKS):
                    a.activation(counts[:, c0:c0 + cn], bank(j, [cn]), ACT.Copy).then_inc(a_counts, 1)
            store_turned(NB * len(TURN), slice((NB - 1) * P, NB * P))
            phase_end(a)
            for j, (c0, cn) in enumerate(CHUNKS):
                a.wait_ge(d_deg, j + 1)
                a.activation(disB[:, c0:c0 + cn], disB[:, c0:c0 + cn], ACT.Sqrt).then_inc(d_sqrt, 1)
            act_layernorm(a, 2)
            phase_end(a)
            with a.Fori(0, LAYERS) as l:
                a.wait_ge(l_w, l * (16 * WDMAS) + 16 * WDMAS)
                for conv, (width, bias) in enumerate(((F1, b1t), (F2, b2t))):
                    for j, (c0, cn) in enumerate(CHUNKS):
                        k = conv * NCH + j
                        a.wait_ge(l_z, l * (2 * NCH) + (k + 1))
                        a.activation(xT[0:width, 0:cn], bank(3, [cn], parts=width), ACT.Relu,
                                     bias=bias[0:width, :]).then_inc(l_relu, 1)
                for j in range(NCH):
                    a.wait_ge(l_mx, l * NCH + (j + 1))
                    a.activation(z, z, ACT.Exp).then_inc(l_ex, 1)
            phase_end(a)
            act_layernorm(a, 3)
            act_copy_nodes(a, h2T, 2)
            phase_end(a)
            sweep2.act(a)
            phase_end(a)
            a.wait_ge(updv, 1 + len(GROUPS))
            a.activation(u, u, ACT.Silu, scale=1.0 / float(np.sqrt(F * F))).then_inc(upda, 1)
            a.wait_ge(upd, 3 + len(GROUPS))
            a.activation(uT, bank(0, [NP], parts=F, count=7), ACT.Copy).then_inc(upda, 1)
            phase_end(a)
            act_layernorm(a, 4)
            act_copy_nodes(a, h3T, 3)
            for b in range(NB):
                for c in range(2):
                    a.wait_ge(t_psum, 3 * b + c + 1)
                    if b >= ROWBUFS:
                        a.wait_ge(t_out[b % ROWBUFS], 16 * (b // ROWBUFS))
                    a.activation(rows_sb[b % ROWBUFS][:, c * RCHUNK:(c + 1) * RCHUNK, :],
                                 bank((3 * b + c) % 6, [RCHUNK, GROW]), ACT.Copy).then_inc(t_act, 1)
            phase_end(a)
            def keep(i, group, landed):
                a.wait_ge(r_gath[i], landed)
                a.activation(gathered[:, bass.ds(group * GQ, GQ), :], stage[i], ACT.Copy).then_inc(r_kept, 2)

            a.sem_inc(r_kept, 4)
            with a.Fori(0, NG // 2) as k:
                keep(0, k * 2, k * (16 * GQ) + 16 * GQ)
                keep(1, k * 2 + 1, k * (16 * GQ) + 16 * GQ)
            keep(0, NG - 1, 16 * GQ * (NG // 2 + 1))
            phase_end(a)

        @block.tensor
        def _(pe):
            pe.wait_ge(consts, 1)
            pe.wait_ge(count_ready, 1)
            pe.matmul(bank(7, [2])[0:NB, 0:1], before, bounds[:, 1:2], start=True, stop=True)
            pe.matmul(bank(7, [2])[0:NB, 1:2], ones25, bounds[:, 1:2], start=True, stop=True).then_inc(base_ready, 1)
            pe.wait_ge(ln_done, 1)
            pe_transpose_nodes(pe, h0, 1)
            pe_table(pe, hT, w0, 256, 1)
            phase_end(pe)
            sweep0.pe(pe)
            phase_end(pe)
            pe.wait_ge(agg_moved, 16 * HI)
            for b in range(NB):
                mm = pe.matmul(bank(4, [NB, F])[:, b, :], aggT0[:, b * P:(b + 1) * P], ident[0:F, 0:F],
                               start=True, stop=True)
            mm.then_inc(upd, 1)
            phase_end(pe)
            pe.sem_inc(a_used, QS)

            def turn(g, before):
                s0, sn = TURN[g]
                pe.wait_ge(a_stored, before + g)
                for t in range(sn):
                    mm = pe.transpose(bank(7, [sn, P], F16)[:, t, :],
                                      counts[:, (s0 + t) * P:(s0 + t + 1) * P], ident_h[:])
                mm.then_inc(a_turned, 1)

            def count_edges(n, q, first):
                pe.wait_ge(a_ready, n * QS + (q + 1))
                for j, (c0, cn) in enumerate(CHUNKS):
                    if first is not None:
                        pe.wait_ge(a_counts, first + j)
                    mm = pe.matmul(bank(j, [cn]), onehot_dst[:, q, :], onehot_src[:, q, c0:c0 + cn],
                                   start=first is not None, stop=True, skip_group_check=True)
                mm.then_inc(a_used, 1)

            with pe.Fori(0, NB) as b:
                table = block_table(pe, b)
                for q in range(QS):
                    count_edges(table[2], q, b * NCH + 1 if q == 0 else None)
                    if q == 0:
                        pe.wait_ge(a_loops, b + 1)
                    turn(q, b * len(TURN) + 1)
                for s, n in block_steps(pe, table, 1):
                    for q in range(QS):
                        count_edges(n, q, None)
            pe.wait_ge(a_loops, NB + 1)
            for g in range(len(TURN)):
                turn(g, NB * len(TURN) + 1)
            phase_end(pe)
            pe.wait_ge(d_ones, 1)
            for j, (c0, cn) in enumerate(CHUNKS):
                for b in range(NB):
                    mm = pe.matmul(bank(j, [cn], parts=96), ones96, A[:, b, c0:c0 + cn],
                                   start=(b == 0), stop=(b == NB - 1))
                mm.then_inc(d_main, 1)
            pe.wait_ge(d_inv, NCH)
            for b in range(NB):
                mm = pe.matmul(bank(7, [NB])[:, b:b + 1], disB[0:1, b * P:(b + 1) * P], ident[0:1, 0:1],
                               start=True, stop=True)
            mm.then_inc(d_node, 1)
            phase_end(pe)
            with pe.Fori(0, LAYERS) as l:
                pe.wait_ge(l_w, l * (16 * WDMAS) + 16 * WDMAS)
                for conv, (H, width) in enumerate(((Hin, F), (Hmid, F2), (Hout, F))):
                    rows = 3 * width

                    def weigh(j):
                        c0, cn = CHUNKS[j]
                        k = conv * NCH + j
                        pe.wait_ge(l_scaled, l * (3 * NCH) + (k + 1))
                        if conv < 2:
                            w, m = ((W1s, 96), (S2, F2))[conv]
                            pe.matmul(bank(3, [cn], parts=m), w[0:rows, 0:m], scaled[k % 3][0:rows, 0:cn],
                                      start=True, stop=True).then_inc(l_z, 1)

                    def finish(j):
                        c0, cn = CHUNKS[j]
                        k = conv * NCH + j
                        if conv < 2:
                            pe.wait_ge(l_relu, l * (2 * NCH) + (k + 1))
                        pe.wait_ge(l_h, l * (3 * NCH) + (k + 1))
                        for t in range(cn // P):
                            cols = slice(t * P, (t + 1) * P)
                            if conv == 0:
                                mm = pe.matmul(bank(4, [4, F2])[:, t, :], xT[0:F1, cols], W2w, start=True, stop=True)
                            elif conv == 1:
                                mm = pe.matmul(bank(4, [4, F2])[:, t, 0:F], xT[0:F2, cols], W3w, start=True, stop=True)
                            else:
                                mm = pe.matmul(bank(4, [4, F2])[:, t, 0:F], scaled[k % 3][0:rows, cols],
                                               S3, start=True, stop=True)
                        mm.then_inc(l_g, 1)

                    for j, (c0, cn) in enumerate(CHUNKS):
                        k = conv * NCH + j
                        if k >= 3:
                            pe.wait_ge(l_scaled, l * (3 * NCH) + (k - 2))
                        for b in range(NB):
                            if j == 0 and b % 4 == 0:
                                if conv == 0:
                                    pe.wait_ge(l_h, l * (3 * NCH) + 1) if b == 0 else None
                                else:
                                    pe.wait_ge(l_h, l * (3 * NCH) + ((conv - 1) * NCH + b // 4 + 2))
                            mm = pe.matmul(bank(k % 3, [cn], parts=rows), H[:, b, :, :].rearrange("p a f -> p (a f)"),
                                           A[:, b, c0:c0 + cn], start=(b == 0), stop=(b == NB - 1))
                        mm.then_inc(l_main, 1)
                        if j >= 2:
                            finish(j - 2)
                        if j >= 1:
                            weigh(j - 1)
                    finish(NCH - 2)
                    weigh(NCH - 1)
                    finish(NCH - 1)
            phase_end(pe)
            pe.wait_ge(ln_done, 3)
            pe_transpose_nodes(pe, h2, 2)
            pe.wait_ge(load4, 16 * 7)
            pe_table(pe, h2T, wmt, 128, 2)
            phase_end(pe)
            sweep2.pe(pe)
            phase_end(pe)
            pe.wait_ge(agg_moved, 16 * 2 * HI)
            for b in range(NB):
                mm = pe.matmul(bank(7, [NB, F])[:, b, :], aggT[:, b * P:(b + 1) * P], wml, start=True, stop=True)
            mm.then_inc(upd, 1)
            for g, m in GROUPS:
                if g >= 7:
                    pe.wait_ge(updv, 1 + g - 6)
                for t in range(m):
                    b = 2 * g + t
                    mm = pe.matmul(bank(g % 7, [2, 256])[:, t, :], h2T[:, b * P:(b + 1) * P], wut, start=True, stop=True)
                mm.then_inc(upd, 1)
            pe.wait_ge(upda, 1)
            for b in range(NB):
                mm = pe.transpose(bank(0, [NP], parts=F, count=7)[:, b * P:(b + 1) * P], u[:, b, :], ident[:])
            mm.then_inc(upd, 1)
            pe.wait_ge(upda, 2)
            for b in range(NB):
                mm = pe.matmul(bank(7, [NB, F])[:, b, :], uT[:, b * P:(b + 1) * P], wul, start=True, stop=True)
            mm.then_inc(upd, 1)
            phase_end(pe)
            pe.wait_ge(load5, 16 * 7)
            pe.matmul(bank(7, [256], parts=NR), wct, wv, start=True, stop=True).then_inc(rel_psum, 1)
            pe.wait_ge(rel_sb, 1)
            pe.matmul(bank(7, [3], parts=F), ws, wa, start=True, stop=True)
            pe.wait_ge(att_sb, 1)
            pe.matmul(bank(7, [32])[:, 16:32], wab, ws, start=True, stop=True).then_inc(att_psum, 1)
            pe.wait_ge(ln_done, 4)
            pe_transpose_nodes(pe, h3, 3)
            pe.wait_ge(hT_done, 3)
            pe.wait_ge(att_sb, 2)
            for b in range(NB):
                mm = pe.matmul(bank(6, [NB])[:, b:b + 1], h3T[:, b * P:(b + 1) * P], att[:, 2:3],
                               start=True, stop=True)
            mm.then_inc(att_d_psum, 1)
            pe.wait_ge(rel_in, 16)
            pe.wait_ge(att_sb, 3)
            for b in range(NB):
                for c in range(3):
                    if b >= 2 and c < 2:
                        pe.wait_ge(t_act, 2 * (b - 2) + c + 1)
                    elif b >= 2:
                        pe.wait_ge(t_dve, b - 1)
                    pe.matmul(bank((3 * b + c) % 6, [RCHUNK * GROW]), h3T[:, b * P:(b + 1) * P],
                              wrel[:, c * RCHUNK:(c + 1) * RCHUNK, :].rearrange("i r c -> i (r c)"),
                              start=True, stop=True).then_inc(t_psum, 1)
            phase_end(pe)
            pe.sem_inc(r_agg, 2)
            with pe.Fori(0, NB) as b:
                pe.wait_ge(r_out, b + 1)
                table = block_table(pe, b)
                pe.matmul(bank(0, [2 * F]), zero5, zero5[:, 0:2 * F], start=True, stop=True, skip_group_check=True)

                def aggregate(i, n):
                    pe.wait_ge(r_edges, n + 1)
                    for q in range(QS):
                        mm = pe.matmul(bank(0, [2 * F]), onehot5[i][:, q, :],
                                       pay5[i][:, q, :, :].rearrange("p a f -> p (a f)"),
                                       start=False, stop=True, skip_group_check=True)
                    mm.then_inc(r_agg, 1)

                for s, n in block_steps(pe, table):
                    aggregate(0, n)
            phase_end(pe)

        @block.vector
        def _(v):
            v.wait_ge(loaded, 16 * 6)
            v.wait_ge(consts, 1)
            v.tensor_copy(dst_rows, dst_rows_i)
            v.drain()
            rows2 = dst_rows.rearrange("p (t e) -> p t e", t=2)
            v.tensor_reduce(step_mm[:, 0, :], rows2, AX.X, ALU.max)
            v.tensor_reduce(step_mm[:, 1, :], rows2, AX.X, ALU.min)
            v.drain().then_inc(rng_copied, 1)
            dve_layernorm(v, h0, lntmp0, 1)
            v.wait_ge(rng_in, 16)
            v.tensor_scalar(flags, step_rng[:, 0, :], thr[:, 0:1], None, ALU.is_ge)
            v.drain()
            v.tensor_tensor(flags, flags, step_left, ALU.mult)
            v.drain()
            v.tensor_reduce(bounds[:, 0:1], flags, AX.X, ALU.max)
            v.drain()
            v.tensor_scalar(bounds[:, 0:1], bounds[:, 0:1], -1.0, float(NS), ALU.mult, ALU.add)
            v.drain()
            v.tensor_scalar(bounds[:, 0:1], bounds[:, 0:1], float(NS - 2), None, ALU.min)
            v.tensor_scalar(flags, step_rng[:, 1, :], thr[:, 1:2], None, ALU.is_le)
            v.drain()
            v.tensor_tensor(flags, flags, step_no, ALU.mult)
            v.drain()
            v.tensor_reduce(bounds[:, 4:5], flags, AX.X, ALU.max)
            v.drain()
            v.tensor_tensor(bounds[:, 1:2], bounds[:, 4:5], bounds[:, 0:1], ALU.subtract)
            v.drain()
            v.tensor_scalar(bounds[:, 1:2], bounds[:, 1:2], 2.0, None, ALU.max)
            v.drain().then_inc(count_ready, 1)
            v.wait_ge(base_ready, 1)
            v.tensor_copy(bounds[:, 2:4], bank(7, [2])[0:NB, :])
            v.drain()
            v.tensor_copy(bounds_i, bounds[:, 0:4])
            v.drain().then_inc(bounds_ready, 1)
            v.tensor_copy(dst_f, dst_i)
            v.tensor_copy(src_c, src_i)
            v.drain()

            def split_src(src_f, hi, lo, hi_onehot, tmp):
                v.tensor_scalar(hi, src_f, float(LO), None, ALU.is_ge)
                for k in range(2, HI):
                    v.tensor_scalar(tmp, src_f, float(LO * k), None, ALU.is_ge)
                    v.drain()
                    v.tensor_tensor(hi, hi, tmp, ALU.add)
                    v.drain()
                v.tensor_scalar(tmp, hi, -float(LO), None, ALU.mult)
                v.drain()
                v.tensor_tensor(lo, src_f, tmp, ALU.add)
                for k in range(HI):
                    v.tensor_scalar(hi_onehot[:, :, k], hi, float(k), None, ALU.is_equal)
                v.drain()

            split_src(src_c, hi_f, lo_f, onehot_hi, tmp_c)
            v.tensor_scalar(attr2, attr2, -1.0, 1.0, ALU.max, ALU.min)
            v.tensor_tensor(tmp_c, src_c, dst_f, ALU.not_equal)
            v.drain()
            for j in range(4):
                v.tensor_scalar(hats[:, :, :, j], attr2, centers[:, j:j + 1], None, ALU.subtract)
            v.drain()
            rising = basis.rearrange("p c a b -> p (c a b)")[:, 0:NC * 8].rearrange("p (c a b) -> p c a b", a=2, b=4)
            v.tensor_scalar(rising, hats, 1.5, 1.0, ALU.mult, ALU.add)
            v.drain()
            v.tensor_scalar(hats, hats, -1.5, 1.0, ALU.mult, ALU.add)
            v.drain()
            v.tensor_tensor(hats, hats, rising, ALU.min)
            v.drain()
            v.tensor_scalar(hats, hats, 0.0, None, ALU.max)
            v.drain()
            v.tensor_tensor(hats[:, :, 1, :], hats[:, :, 1, :], wide(tmp_c, 4), ALU.mult)
            v.drain()
            v.tensor_tensor(basis, hats[:, :, 0, :].unsqueeze(3).to_broadcast([P, NC, 4, 4]),
                            hats[:, :, 1, :].unsqueeze(2).to_broadcast([P, NC, 4, 4]), ALU.mult)
            v.tensor_scalar(src_c, src_c, -float(HALF), None, ALU.add)
            v.wait_ge(bounds_out, 16)
            dve_table(v, table0, rest, 256, 1)
            phase_end(v)
            sweep0.dve(v)
            phase_end(v)
            v.tensor_copy(agg0, sweep0.agg)
            v.drain().then_inc(agg_copied, 1)
            v.wait_ge(upd, 1)
            v.scalar_tensor_tensor(x[:], bank(4, [NB, F]), 1.0 / 128.0, x[:], ALU.mult, ALU.add)
            v.drain()
            phase_end(v)
            v.memset(counts, 0.0)
            v.drain()
            v.sem_inc(a_counts, NCH)
            v.sem_inc(a_stored, 1)

            def edge_onehots(s, n, q):
                v.wait_ge(a_used, n * QS + (q + 1))
                v.tensor_scalar(onehot_dst[:, q, :], iota128, dst_f[:, bass.ds(s * QS + q, 1)], None,
                                ALU.is_equal)
                v.tensor_scalar(onehot_src[:, q, :], iota[:], src_c[:, bass.ds(s * QS + q, 1)], None,
                                ALU.is_equal).then_inc(a_ready, 1)

            def add_loops(before, column):
                v.wait_ge(a_counts, before)
                own = counts[:, column]
                v.tensor_tensor(own, own, ident_h[:], ALU.add).then_inc(a_loops, 1)

            with v.Fori(0, NB) as b:
                table = block_table(v, b)
                prev = v.value_load(prev_block[0:1, bass.ds(b, 1)], min_val=0, max_val=NB - 1)
                edge_onehots(table[0], table[2], 0)
                edge_onehots(table[0], table[2], 1)
                add_loops(b * NCH + NCH, bass.ds(prev * P, P))
                edge_onehots(table[0], table[2], 2)
                edge_onehots(table[0], table[2], 3)
                for s, n in block_steps(v, table, 1):
                    for q in range(QS):
                        edge_onehots(s, n, q)
                v.drain()
                v.tensor_scalar(dst_f, dst_f, float(P), None, ALU.subtract)
                v.drain()
            add_loops(NB * NCH + NCH, slice((NB - 1) * P, NB * P))
            phase_end(v)
            v.memset(ones96, 1.0).then_inc(d_ones, 1)
            v.memset(W1s, 0.0)
            for j, (c0, cn) in enumerate(CHUNKS):
                v.wait_ge(d_main, j + 1)
                v.tensor_scalar(disB[:, c0:c0 + cn], bank(j, [cn], parts=96), 1.0, None, ALU.max).then_inc(d_deg, 1)
            for j, (c0, cn) in enumerate(CHUNKS):
                v.wait_ge(d_sqrt, j + 1)
                v.reciprocal(disB[:, c0:c0 + cn], disB[:, c0:c0 + cn]).then_inc(d_inv, 1)
            dve_layernorm(v, hn, x3, 2)
            for i in range(3):
                v.tensor_copy(S2[i * F2:(i + 1) * F2, :], ident[i * F2:(i + 1) * F2, i * F2:(i + 1) * F2])
            v.tensor_tensor(S3, ident[0:3 * F, 0:F], ident[0:3 * F, F:2 * F], ALU.add)
            v.drain()
            v.tensor_tensor(S3, S3, ident[0:3 * F, 2 * F:3 * F], ALU.add)
            v.wait_ge(d_node, 1)
            v.tensor_copy(dis, bank(7, [NB]))
            v.drain()

            def parts_of(H, b0, m, src, width):
                t, r = gtmp[:, 0:m, 0:width], grest[:, 0:m, 0:width]
                v.tensor_tensor(t, src, wide(dis[:, b0:b0 + m], width), ALU.mult)
                v.drain()
                return split3(v, [H[:, b0:b0 + m, i, :] for i in range(3)], t, r)

            for j, (c0, cn) in enumerate(CHUNKS):
                b0, m = c0 // P, cn // P
                parts_of(Hin, b0, m, hn[:, b0:b0 + m, :], F)
                v.drain()
            v.sem_inc(l_wfree, 1)
            v.sem_inc(l_h, 1)
            phase_end(v)
            with v.Fori(0, LAYERS) as l:
                for conv, (H, width) in enumerate(((Hmid, F2), (Hout, F), (Hin, F))):
                    rows = 3 * (F, F2, F)[conv]

                    def scale(j):
                        c0, cn = CHUNKS[j]
                        k = conv * NCH + j
                        v.wait_ge(l_main, l * (3 * NCH) + (k + 1))
                        v.tensor_tensor(scaled[k % 3][0:rows, 0:cn], bank(k % 3, [cn], parts=rows),
                                        disB[0:rows, c0:c0 + cn], ALU.mult).then_inc(l_scaled, 1)

                    def store(j):
                        c0, cn = CHUNKS[j]
                        b0, m = c0 // P, cn // P
                        k = conv * NCH + j
                        v.wait_ge(l_g, l * (3 * NCH) + (k + 1))
                        got = bank(4, [4, F2])[:, 0:m, 0:width]
                        if conv < 2:
                            parts_of(H, b0, m, got, width).then_inc(l_h, 1)
                            v.drain()
                            return
                        mx, sm = zs[:, 0:m, 0], zs[:, 0:m, 1]
                        zz = z[:, 0:m, :]
                        v.tensor_tensor(zz, got, b3t.unsqueeze(1).to_broadcast([P, m, F]), ALU.add)
                        v.drain()
                        v.tensor_reduce(mx, zz, AX.X, ALU.max)
                        v.drain()
                        v.tensor_tensor(zz, zz, wide(mx, F), ALU.subtract).then_inc(l_mx, 1)
                        v.wait_ge(l_ex, l * NCH + (j + 1))
                        v.tensor_reduce(sm, zz, AX.X, ALU.add)
                        v.drain()
                        v.reciprocal(sm, sm)
                        v.drain()
                        v.tensor_tensor(x3[:, b0:b0 + m, :], zz, wide(sm, F), ALU.mult)
                        v.drain()
                        parts_of(H, b0, m, x3[:, b0:b0 + m, :], F).then_inc(l_h, 1)
                        v.drain()

                    if conv == 2:
                        v.wait_ge(l_w, l * (16 * WDMAS) + 16 * WDMAS)
                    for j in range(NCH):
                        scale(j)
                        if j >= 2:
                            store(j - 2)
                    store(NCH - 2)
                    store(NCH - 1)
                v.sem_inc(l_wfree, 1)
            v.tensor_tensor(x[:], x[:], x3, ALU.add)
            v.drain()
            phase_end(v)
            dve_layernorm(v, h2, lntmp, 3)
            v.wait_ge(load4, 16 * 7)
            v.tensor_copy(dst_f4, dst_i4)
            v.tensor_copy(tmp_src4, src_i2)
            v.drain()
            split_src(tmp_src4, hi_f4, lo_f4, onehot_hi2, tmp_c4)
            dve_table(v, table2, rest4, 128, 2)
            phase_end(v)
            sweep2.dve(v)
            phase_end(v)
            v.tensor_copy(agg_sb, sweep2.agg)
            v.drain().then_inc(agg_copied, 1)
            v.wait_ge(upd, 2)
            v.tensor_scalar(aggn, bank(7, [NB, F]), 1.0 / float(np.sqrt(F)), None, ALU.mult)
            v.drain().then_inc(updv, 1)
            for g, m in GROUPS:
                v.wait_ge(upd, 3 + g)
                prod = vprod[:, 0:m, :].rearrange("p t (h k) -> p t h k", k=F)
                v.tensor_tensor(prod, bank(g % 7, [2, 256])[:, 0:m, :].rearrange("p t (h k) -> p t h k", k=F),
                                aggn[:, 2 * g:2 * g + m, :].unsqueeze(3).to_broadcast([P, m, F, F]), ALU.mult)
                v.drain()
                v.tensor_reduce(u[:, 2 * g:2 * g + m, :], prod.rearrange("p t h k -> p t k h"), AX.X, ALU.add
                                ).then_inc(updv, 1)
                v.drain()
            v.tensor_tensor(x[:], x[:], h2, ALU.add)
            v.drain()
            v.wait_ge(upd, 4 + len(GROUPS))
            v.scalar_tensor_tensor(x[:], bank(7, [NB, F]), 1.0 / float(np.sqrt(F)), x[:], ALU.mult, ALU.add)
            v.drain()
            phase_end(v)
            dve_layernorm(v, h3, lntmp, 4)
            v.wait_ge(load5, 16 * 7)
            v.tensor_copy(type_f, type_f.bitcast(I32))
            v.tensor_copy(src_f5, row_no)
            v.tensor_copy(wab, wa[:, 1:2].to_broadcast([F, P]))
            v.wait_ge(rel_psum, 1)
            v.tensor_copy(rel, bank(7, [256], parts=NR))
            v.drain().then_inc(rel_sb, 1)
            v.sem_inc(att_sb, 1)
            v.wait_ge(att_psum, 1)
            v.tensor_copy(att, bank(7, [3], parts=F))
            v.tensor_copy(a2b, bank(7, [32])[:, 16:32])
            v.drain().then_inc(att_sb, 1)
            v.tensor_copy(wrel[:, :, F], att[:, 0:1].to_broadcast([F, NR])).then_inc(att_sb, 1)
            v.scalar_tensor_tensor(row_no, src_f5, float(NR), type_f, ALU.mult, ALU.add)
            v.tensor_scalar(dst_f5, dst_f5, -float(HALF), None, ALU.add)
            v.wait_ge(att_d_psum, 1)
            v.tensor_copy(att_d, bank(6, [NB]))
            for b in range(NB):
                if b < NC // 101:
                    cols = slice(b * 101, (b + 1) * 101)
                    v.tensor_tensor(e_chunk, attr16[:, cols, :], a2b.unsqueeze(1).to_broadcast([P, 101, F]), ALU.mult)
                    v.drain()
                    v.tensor_reduce(att_e[:, cols], e_chunk, AX.X, ALU.add)
                    v.drain()
                v.wait_ge(t_psum, 3 * b + 3)
                if b >= ROWBUFS:
                    v.wait_ge(t_out[b % ROWBUFS], 16 * (b // ROWBUFS))
                v.tensor_copy(rows_sb[b % ROWBUFS][:, 2 * RCHUNK:3 * RCHUNK, :],
                              bank((3 * b + 2) % 6, [RCHUNK, GROW])).then_inc(t_dve, 1)
            phase_end(v)
            v.sem_inc(r_out, 1)
            with v.Fori(0, NB) as b:
                table = block_table(v, b)
                for s, n in block_steps(v, table):
                    cols = bass.ds(s * QS, QS)
                    v.wait_ge(r_agg, n + 2)
                    for q in range(QS):
                        v.tensor_scalar(onehot5[0][:, q, :], iota[:, bass.ds(b * P, P)],
                                        dst_f5[:, bass.ds(s * QS + q, 1)], None, ALU.is_equal)
                    v.wait_ge(r_kept, s + 5)
                    v.tensor_tensor(es5, att_e[:, cols], gathered[:, cols, F], ALU.add)
                    v.tensor_copy(pay5[0][:, :, 1, :], gathered[:, cols, 0:F])
                    v.drain()
                    v.tensor_tensor(pay5[0][:, :, 0, :], gathered[:, cols, 0:F], wide(es5, F),
                                    ALU.mult).then_inc(r_edges, 1)
                v.wait_ge(r_agg, table[2] + table[1] + 2)
                xb = x[:, bass.ds(b, 1), :].rearrange("p a f -> p (a f)")
                v.tensor_tensor(xb, bank(0, [2 * F])[:, 0:F], xb, ALU.add)
                v.tensor_scalar(sum5, bank(0, [2 * F])[:, F:2 * F], att_d[:, bass.ds(b, 1)], None,
                                ALU.mult).then_inc(r_out, 1)
                v.drain()
                v.tensor_tensor(xb, xb, sum5, ALU.add)
                v.drain()
            phase_end(v)


_ORDER = ["x", "src", "dst", "dstrow", "type", "attr2", "attr8", "attr16", "w0", "w1", "b1", "w2", "b2",
          "w3", "b3", "wmt", "wml", "wut", "wul", "ws", "wa", "wv", "wct"]


def kernel(**inputs):
    import numpy as _np
    import concourse.bacc as _bacc
    from concourse import mybir as _mybir
    from concourse.bass_utils import run_bass_kernel_spmd as _run

    i = {k: _np.asarray(v) for k, v in inputs.items()}

    def edges(a, pad):
        full = _np.full((NS * STEP,) + a.shape[1:], pad, a.dtype)
        full[:E] = a
        full = full.reshape((NS, P, QS) + a.shape[1:])
        return _np.ascontiguousarray(_np.moveaxis(full, 1, 0).reshape((P, NC) + a.shape[1:]))

    nodes = _np.zeros((NP, F), i["x"].dtype)
    nodes[:N] = i["x"]
    absent = 2 * NP - 1
    dstrow = _np.full((NS * STEP,), absent, i["dst"].dtype)
    dstrow[:E] = i["dst"]
    a = {
        "x": nodes.reshape(NB, P, F).transpose(1, 0, 2), "src": edges(i["src"], 0),
        "dst": edges(i["dst"], absent), "dstrow": dstrow.reshape(TPP, 2 * STEP),
        "type": edges(i["edge_type_90"], 0), "attr2": edges(i["edge_attr_2"], 0),
        "attr8": edges(i["edge_attr_8"], 0), "attr16": edges(i["edge_attr_16"], 0),
        "w0": i["L0_gnn_W"], "w1": i["L1_gnn_W1"], "b1": i["L1_gnn_b1"], "w2": i["L1_gnn_W2"],
        "b2": i["L1_gnn_b2"], "w3": i["L1_gnn_W3"], "b3": i["L1_gnn_b3"], "wmt": i["L2_gnn_W_msg_tp"],
        "wml": i["L2_gnn_W_msg_lin"], "wut": i["L2_gnn_W_upd_tp"], "wul": i["L2_gnn_W_upd_lin"],
        "ws": i["L3_gnn_Ws"], "wa": i["L3_gnn_Wa"].reshape(3, F).T,
        "wv": i["L3_gnn_weight"].reshape(F, NBASE, F), "wct": i["L3_gnn_w_comp"].T,
    }
    a = {f"in_{k}": _np.ascontiguousarray(v) for k, v in a.items()}
    nc = _bacc.Bacc("TRN2", target_bir_lowering=False, num_devices=1)
    args = [nc.dram_tensor(f"in_{k}", a[f"in_{k}"].shape, _mybir.dt.from_np(a[f"in_{k}"].dtype),
                           kind="ExternalInput").ap() for k in _ORDER]
    result = nc.dram_tensor("result", (N, F), _mybir.dt.float32, kind="ExternalOutput").ap()
    gnn(nc, *args, result)
    r = _run(nc, [a], core_ids=[0])
    return r.results[0]["result"]
```

```python
from contextlib import ExitStack

import numpy as np

import concourse.bass as bass
import concourse.mybir as mybir
from concourse.alu_op_type import AluOpType as ALU

ACT = mybir.ActivationFunctionType
AX = mybir.AxisListType
F32, BF16, F16, I32 = mybir.dt.float32, mybir.dt.bfloat16, mybir.dt.float16, mybir.dt.int32
F32R = mybir.dt.float32r
BYTES = {F32: 4, F32R: 4, I32: 4, BF16: 2, F16: 2}

P = 128
N, E, F = 3125, 103125, 16
NB = -(-N // P)
NP = NB * P
QS = 4
PS = 2
NC = -(-E // (P * 2 * QS)) * 2 * QS
MOST = NB * NC
HI, LO = 8, NP // 8
HALF = NP // 2
NR, NBASE = 90, 30
WORK = 14528
SRC_BUFS = 3
LAYERS, F1, F2 = 5, 64, 32
BANK = 512
CHUNKS = [(j * BANK, min(BANK, NP - j * BANK)) for j in range(-(-NP // BANK))]
NCH = len(CHUNKS)
GCHUNKS = CHUNKS[-1:] + CHUNKS[:-1]
GBANKS = [0, 1, 2, 5, 6, 7, 5]
TOGETHER = 3
EPS = 1e-5
GROW = F + 1
RCHUNK = 30
GQ = 2 * QS
NG = NC // GQ
ROWBUFS = 6
ENGINES = 5
RC = 2 * QS
RP = NC // RC
TABLE = 8


def gnn(nc, x_in, src_in, dst_in, dstrow_in, type_in, attr2_in, attr8_in, attr16_in, w0_in,
        w1_in, b1_in, w2_in, b2_in, w3_in, b3_in, wmt_in, wml_in, wut_in, wul_in, ws_in, wa_in,
        wv_in, wct_in, out):
    range_dram = nc.dram_tensor("column_range", (2, NC), F32, kind="Internal").ap()
    table_dram = nc.dram_tensor("block_steps", (NB, TABLE), I32, kind="Internal").ap()
    rel_dram = nc.dram_tensor("relation_weights", (F * NR * F,), F32, kind="Internal").ap()
    rows_dram = nc.dram_tensor("relation_rows", (NP * NR, GROW), F32, kind="Internal").ap()

    with ExitStack() as ctx:
        def sb(name, shape, dt):
            return ctx.enter_context(nc.sbuf_tensor(name, shape, dt))

        def sem(name):
            return ctx.enter_context(nc.semaphore(name))

        def shaped(ap, shape):
            names = "abcd"[:len(shape)]
            if len(shape) == 1:
                return ap
            return ap.rearrange(f"p ({' '.join(names)}) -> p {' '.join(names)}",
                                **{k: d for k, d in zip(names, shape)})

        x = sb("x", [P, NB, F], F32)
        ident = sb("ident", [P, P], F32)
        ident_h = sb("ident_h", [P, P], F16)
        iota = sb("iota", [P, NP], F16)
        iotaLO = iota[:, HALF:HALF + LO]
        steps_row = sb("steps_row", [1, NB * TABLE], I32)
        stat = sb("stat", [P, NB, 2], F32)
        eps_t = sb("eps_t", [P, 1], F32)

        spread = sb("spread", [P, QS, 2, HI * F], F32R)
        onehot_lo = sb("onehot_lo", [P, QS + 2, LO], F32R)

        big = sb("big", [P, NB * NP], F16)
        work = sb("work", [P, WORK], F16)

        class Region:
            def __init__(self, tensor, size):
                self.tensor, self.size, self.at = tensor, size, 0

            def take(self, shape, dt, parts=P):
                n = int(np.prod(shape)) * BYTES[dt] // 2
                ap = self.tensor[0:parts, self.at:self.at + n]
                self.at += n + (-n) % 2
                assert self.at <= self.size, (self.at, self.size)
                return shaped(ap if dt == F16 else ap.bitcast(dt), list(shape))

        def regions():
            return Region(big, NB * NP), Region(work, WORK)

        psum = ctx.enter_context(nc.psum_tensor("psum", [P, 8, BANK], F32))

        def bank(i, shape, dt=F32, parts=P, count=1):
            n = int(np.prod(shape)) * BYTES[dt] // 4
            ap = psum[0:parts, i:i + count, :].rearrange("p a b -> p (a b)")[:, 0:n]
            return shaped(ap if dt == F32 else ap.bitcast(dt), list(shape))

        phase_done = sem("phase_done")
        phase_no = {}

        def phase_end(eng):
            phase_no[eng] = phase_no.get(eng, 0) + 1
            eng.drain().then_inc(phase_done, 1)
            eng.wait_ge(phase_done, ENGINES * phase_no[eng])

        def entry(eng, b, k, least, most):
            return eng.value_load(steps_row[0:1, bass.ds(b * TABLE + k, 1)], min_val=least, max_val=most)

        def block_table(eng, b):
            return entry(eng, b, 0, 0, NC - 2 * QS), entry(eng, b, 1, 1, NC // QS - 1), entry(eng, b, 2, 0, MOST)

        def pair_table(eng, b):
            return entry(eng, b, 4, 0, NC - 3 * PS), entry(eng, b, 5, 2, NC // PS - 1), entry(eng, b, 6, 0, MOST)

        def column(c, most):
            return nc.s_assert_within(c, 0, most, skip_runtime_bounds_check_because="a block's steps end by NC")

        def block_steps(eng, table):
            first, last, base = table
            with eng.Fori(0, last + 1) as i:
                yield column(first + i * QS, NC - QS), base + i

        def split3(v, parts, src, rest):
            v.tensor_copy(parts[0], src)
            v.drain()
            v.tensor_tensor(rest, src, parts[0], ALU.subtract)
            v.drain()
            v.tensor_copy(parts[1], rest)
            v.drain()
            v.tensor_tensor(rest, rest, parts[1], ALU.subtract)
            v.drain()
            return v.tensor_copy(parts[2], rest)

        def wide(ap, n):
            return ap.unsqueeze(2).to_broadcast([ap.shape[0], ap.shape[1], n])

        ln_var = sem("ln_var")
        ln_std = sem("ln_std")
        ln_done = sem("ln_done")

        def dve_layernorm(v, h, tmp, k):
            mean, var, std, rstd = stat[:, :, 0], stat[:, :, 0], stat[:, :, 1], stat[:, :, 0]
            v.tensor_reduce(mean, x[:], AX.X, ALU.add)
            v.drain()
            v.tensor_scalar(mean, mean, 1.0 / F, None, ALU.mult)
            v.drain()
            v.tensor_tensor(h, x[:], wide(mean, F), ALU.subtract)
            v.drain()
            v.tensor_tensor(tmp, h, h, ALU.mult)
            v.drain()
            v.tensor_reduce(var, tmp, AX.X, ALU.add)
            v.drain()
            v.tensor_scalar(var, var, 1.0 / F, EPS, ALU.mult, ALU.add).then_inc(ln_var, 1)
            v.wait_ge(ln_std, k)
            v.reciprocal(rstd, std)
            v.drain()
            v.tensor_tensor(h, h, wide(rstd, F), ALU.mult)
            v.drain()
            v.tensor_scalar(h, h, 0.0, None, ALU.max).then_inc(ln_done, 1)

        def act_layernorm(a, k):
            a.wait_ge(ln_var, k)
            a.activation(stat[:, :, 1], stat[:, :, 0], ACT.Sqrt).then_inc(ln_std, 1)

        hT_psum = sem("hT_psum")
        hT_done = sem("hT_done")

        def pe_transpose_nodes(pe, h, k):
            for b in range(NB):
                mm = pe.transpose(bank(0, [NP], parts=F, count=7)[:, b * P:(b + 1) * P], h[:, b, :], ident[:])
            mm.then_inc(hT_psum, 1)

        def act_copy_nodes(a, hT, k):
            a.wait_ge(hT_psum, k)
            a.activation(hT, bank(0, [NP], parts=F, count=7), ACT.Copy).then_inc(hT_done, 1)

        GROUPS = [(g, min(2, NB - 2 * g)) for g in range(-(-NB // 2))]
        tab_psum = sem("tab_psum")
        tab_free = sem("tab_free")

        def pe_table(pe, hT, w, width, k):
            pe.wait_ge(hT_done, k)
            for g, m in GROUPS:
                if g >= 7:
                    pe.wait_ge(tab_free, len(GROUPS) * (k - 1) + g - 6)
                for t in range(m):
                    b = 2 * g + t
                    mm = pe.matmul(bank(g % 7, [2, 256])[:, t, 0:width], hT[:, b * P:(b + 1) * P], w,
                                   start=True, stop=True)
                mm.then_inc(tab_psum, 1)

        def dve_table(v, table, rest, width, k):
            for g, m in GROUPS:
                v.wait_ge(tab_psum, len(GROUPS) * (k - 1) + g + 1)
                split3(v, [table[:, 2 * g:2 * g + m, i, :] for i in range(3)],
                       bank(g % 7, [2, 256])[:, 0:m, 0:width], rest[:, 0:m, 0:width]).then_inc(tab_free, 1)
                v.drain()

        class Sweep:

            def __init__(self, tag, silu, K):
                self.silu, self.K, self.width = silu, K, K * F
                self.onehot_ready = sem(f"{tag}_onehot_ready")
                self.onehotT_psum = sem(f"{tag}_onehotT_psum")
                self.onehotT_ready = sem(f"{tag}_onehotT_ready")
                self.products_ready = sem(f"{tag}_products_ready")
                self.products_used = sem(f"{tag}_products_used")
                self.sums_ready = sem(f"{tag}_sums_ready")
                self.msg_ready = sem(f"{tag}_msg_ready")
                self.msg_spread = sem(f"{tag}_msg_spread")
                self.lo_ready = sem(f"{tag}_lo_ready")
                self.act_lo_ready = sem(f"{tag}_act_lo_ready")
                self.distance_ready = sem(f"{tag}_distance_ready")
                self.scatter_done = sem(f"{tag}_scatter_done")

            def place(self, dst_c, lo_f, onehot_hi, coef, table, W):
                self.dst_c, self.lo_f, self.onehot_hi, self.coef, self.table = dst_c, lo_f, onehot_hi, coef, table
                self.onehot = W.take([QS, P], F16)
                self.onehotT = W.take([QS, P], BF16)
                self.prod = W.take([QS, 256], F32)
                self.sums = W.take([QS, F], F32)
                self.msg = W.take([QS, F], F32) if self.silu else self.sums
                self.msg_hi = W.take([QS, F], F32R)
                self.msg_lo = W.take([QS, F], F32R)
                self.distance = W.take([LO], F32)
                self.one = W.take([1], F32)
                self.psT = [bank(i, [2, P], F16) for i in (0, 4)]
                self.products = [bank(1 + r, [2, 256])[:, :, 0:self.width] for r in range(2)]
                self.agg = bank(3, [LO])

            def lo_row(self, n, q):
                if q < 2:
                    return onehot_lo[:, q, :]
                return onehot_lo[:, bass.ds((n % 2) * 2 + q, 1), :].rearrange("p a f -> p (a f)")

            def steps_ahead(self, eng, body):
                with eng.Fori(0, NB) as b:
                    first, last, base = block_table(eng, b)
                    with eng.Fori(0, last) as i:
                        s = column(first + i * QS, NC - 2 * QS)
                        body(b, s, base + i, b, s + QS)
                    ahead = (b + 1) % NB
                    body(b, column(first + last * QS, NC - QS), base + last,
                         ahead, entry(eng, ahead, 0, 0, NC - 2 * QS))

            def dve(self, v):
                used = self.msg_ready if self.silu else self.msg_spread

                def onehots(b, s, n):
                    for r in range(2):
                        if n is not None:
                            v.wait_ge(self.onehotT_psum, n * 2 + (r + 1))
                        for q in (2 * r, 2 * r + 1):
                            op = v.tensor_scalar(self.onehot[:, q, :], iota[:, bass.ds(b * P, P)],
                                                 self.dst_c[:, bass.ds(s + q, 1)], None, ALU.is_equal)
                        op.then_inc(self.onehot_ready, 1)

                def body(b, s, n, ahead_b, ahead_s):
                    onehots(ahead_b, ahead_s, n)
                    prods = [self.prod[:, 2 * r:2 * r + 2, 0:self.width].rearrange("p q (k o) -> p q k o", o=F)
                             for r in range(2)]
                    for r in range(2):
                        coef = self.coef[:, bass.ds(s + 2 * r, 2), :]
                        v.wait_ge(self.sums_ready, n * 2 + (r + 1))
                        v.wait_ge(self.products_ready, n * 2 + (r + 1))
                        v.tensor_tensor(prods[r], self.products[r].rearrange("p q (k o) -> p q k o", o=F),
                                        coef.unsqueeze(3).to_broadcast([P, 2, self.K, F]),
                                        ALU.mult).then_inc(self.products_used, 1)
                    for r in range(2):
                        v.wait_ge(self.products_used, n * 2 + (r + 3))
                        v.wait_ge(used, n * 2 + (r + 1))
                        v.tensor_reduce(self.sums[:, 2 * r:2 * r + 2, :], prods[r].rearrange("p q k o -> p q o k"),
                                        AX.X, ALU.add).then_inc(self.sums_ready, 1)
                    for q in (2, 3, 1):
                        v.wait_ge(self.scatter_done, n * 2 + (3 if q == 1 else 2))
                        op = v.tensor_scalar(self.lo_row(n, q), iotaLO, self.lo_f[:, bass.ds(s + q, 1)],
                                             None, ALU.is_equal)
                    op.then_inc(self.lo_ready, 1)

                v.memset(onehot_lo[:].bitcast(F32), 0.0)
                v.memset(self.one, 1.0)
                v.drain()
                v.sem_inc(self.lo_ready, 1)
                v.sem_inc(self.products_used, 2)
                v.sem_inc(self.sums_ready, 2)
                onehots(0, entry(v, 0, 0, 0, NC - 2 * QS), None)
                self.steps_ahead(v, body)

            def act(self, a):
                func, scale = (ACT.Silu, 1.0 / float(np.sqrt(F * self.K))) if self.silu else (ACT.Copy, 1.0)

                def transposed(n):
                    for r in range(2):
                        half = slice(2 * r, 2 * r + 2)
                        if n is None:
                            a.wait_ge(self.onehotT_psum, r + 1)
                        else:
                            a.wait_ge(self.products_ready, n * 2 + (r + 1))
                            a.wait_ge(self.onehotT_psum, n * 2 + (r + 3))
                        a.activation(self.onehotT[:, half, :], self.psT[r], ACT.Copy).then_inc(self.onehotT_ready, 1)

                def message(n, r):
                    half = slice(2 * r, 2 * r + 2)
                    a.wait_ge(self.sums_ready, n * 2 + (r + 3))
                    a.wait_ge(self.msg_spread, n * 2 + (r + 1))
                    if self.silu:
                        a.activation(self.msg[:, half, :], self.sums[:, half, :], func, scale=scale)
                    a.activation(self.msg_hi[:, half, :], self.sums[:, half, :], func,
                                 scale=scale).then_inc(self.msg_ready, 1)

                def body(b, s, n, ahead_b, ahead_s):
                    transposed(n)
                    a.wait_ge(self.act_lo_ready, n + 1)
                    a.activation(self.distance, iotaLO, ACT.Abs, scale=-1.0,
                                 bias=self.lo_f[:, bass.ds(s, 1)]).then_inc(self.distance_ready, 1)
                    message(n, 0)
                    a.wait_ge(self.scatter_done, n * 2 + 3)
                    a.wait_ge(self.distance_ready, n + 1)
                    a.activation(self.lo_row(n, 0), self.distance, ACT.Relu, scale=-1.0,
                                 bias=self.one).then_inc(self.act_lo_ready, 1)
                    message(n, 1)

                a.wait_ge(self.lo_ready, 1)
                a.activation(self.distance[:, 0:1], self.one, func)
                a.sem_inc(self.msg_ready, 2)
                a.sem_inc(self.act_lo_ready, 1)
                transposed(None)
                self.steps_ahead(a, body)

            def pool(self, g):
                g.memset(spread[:].bitcast(F32), 0.0)
                g.drain()
                g.sem_inc(self.msg_spread, 2)
                with g.Fori(0, NB) as b:
                    for s, n in block_steps(g, block_table(g, b)):
                        for r in range(2):
                            half = slice(2 * r, 2 * r + 2)
                            hi = self.onehot_hi[:, bass.ds(s + 2 * r, 2), :].unsqueeze(3)
                            g.wait_ge(self.msg_ready, n * 2 + (r + 3))
                            g.tensor_tensor(self.msg_lo[:, half, :], self.msg[:, half, :],
                                            self.msg_hi[:, half, :], ALU.subtract)
                            g.drain()
                            g.wait_ge(self.scatter_done, n * 2 + (r + 3))
                            for part, msg in enumerate((self.msg_hi, self.msg_lo)):
                                op = g.tensor_tensor(spread[:, half, part, :].rearrange("p q (h o) -> p q h o", o=F),
                                                     msg[:, half, :].unsqueeze(2).to_broadcast([P, 2, HI, F]),
                                                     hi.to_broadcast([P, 2, HI, F]), ALU.mult)
                            op.then_inc(self.msg_spread, 1)

            def scatter(self, pe, n, start=False):
                pe.wait_ge(self.lo_ready, n + 1)
                pe.wait_ge(self.act_lo_ready, n + 1)
                for r in range(2):
                    pe.wait_ge(self.msg_spread, n * 2 + (r + 1))
                    for q in (2 * r, 2 * r + 1):
                        for part in range(2):
                            mm = pe.matmul(self.agg, spread[:, q, part, :], self.lo_row(n + 1, q),
                                           start=False, stop=True, skip_group_check=True)
                    mm.then_inc(self.scatter_done, 1)

            def pe(self, pe):
                pe.wait_ge(self.lo_ready, 1)
                pe.wait_ge(self.msg_spread, 2)
                pe.wait_ge(self.products_used, 2)
                pe.matmul(self.agg, spread[:, 0, 0, :], onehot_lo[:, 0, :], start=True, stop=True,
                          skip_group_check=True).then_inc(self.scatter_done, 2)

                def turn(n):
                    for r in range(2):
                        pe.wait_ge(self.onehot_ready, n * 2 + (r + 1))
                        for q in (2 * r, 2 * r + 1):
                            mm = pe.transpose(self.psT[r][:, q % 2, :], self.onehot[:, q, :], ident_h[:])
                        mm.then_inc(self.onehotT_psum, 1)

                def gather(b, n):
                    for r in range(2):
                        pe.wait_ge(self.onehotT_ready, n * 2 + (r + 1))
                        pe.wait_ge(self.products_used, n * 2 + (r + 1))
                        for t in range(2):
                            for i in range(3):
                                row = self.table[:, bass.ds(b, 1), i, :].rearrange("p a w -> p (a w)")
                                mm = pe.matmul(self.products[r][:, t, :], self.onehotT[:, 2 * r + t, :],
                                               row, start=(i == 0), stop=(i == 2))
                        mm.then_inc(self.products_ready, 1)

                def body(b, s, n, ahead_b, ahead_s):
                    turn(n + 1)
                    self.scatter(pe, n)
                    gather(ahead_b, n + 1)

                turn(0)
                gather(0, 0)
                self.steps_ahead(pe, body)
                _, last, base = block_table(pe, NB - 1)
                self.scatter(pe, base + last + 1)

        sweep0 = Sweep("spline", False, 16)
        sweep2 = Sweep("tensor", True, 8)

        agg_copied = sem("agg_copied")
        agg_moved = sem("agg_moved")

        def sync_regroup(sp, agg_sb, aggT, k):
            sp.wait_ge(agg_copied, k)
            for h in range(HI):
                sp.dma_start(aggT[0:F, h * LO:(h + 1) * LO], agg_sb[h * F:(h + 1) * F, :]).then_inc(agg_moved, 16)

        B1, W1 = regions()
        hT = B1.take([NP], F32, parts=F)
        attr2 = B1.take([NC, 2], F32)
        hats = B1.take([NC, 2, 4], F32)
        basis = B1.take([NC, 4, 4], F32)
        table0_at = B1.at
        table0 = B1.take([NB, 3, 256], BF16)
        dst_i = B1.take([NC], I32)
        src_i = B1.take([NC], I32)
        dst_f = W1.take([NC], F32)
        src_c = W1.take([NC], F32)
        W1_keep = W1.at
        h0 = B1.take([NB, F], F32)
        lntmp0 = B1.take([NB, F], F32)
        lnwork = Region(work, WORK)
        lnwork.at = 2 * NB * F
        lntmp = lnwork.take([NB, F], F32)
        lo_f = W1.take([NC], F32)
        mark = W1.at
        rest = W1.take([2, 256], F32)
        hi_f = W1.take([NC], F32)
        tmp_c = W1.take([NC], F32)
        w0 = W1.take([256], F32, parts=F)
        centers = W1.take([4], F32)
        W1b = Region(work, WORK)
        W1b.at = mark
        dst_rows = hats.rearrange("p a b c -> p (a b c)")[0:RP, 0:RC * P]
        dst_rows_i = basis.rearrange("p a b c -> p (a b c)").bitcast(I32)[0:RP, 0:RC * P]
        bounds_place = Region(big, NB * NP)
        bounds_place.at = table0_at

        def small(shape, parts=NB, dt=F32):
            return bounds_place.take(shape, dt, parts)

        col_mm = small([2, RC], RP)
        col_rng = small([2, NC])
        col_no = small([NC])
        col_left = small([NC])
        flags = small([NC])
        thr = small([2])
        bounds = small([TABLE])
        found = small([4])
        before = small([NB])
        bounds_i = small([TABLE], dt=I32)

        loaded = sem("loaded")
        consts = sem("consts")
        rng_copied = sem("rng_copied")
        rng_out = sem("rng_out")
        rng_in = sem("rng_in")
        count_ready = sem("count_ready")
        base_ready = sem("base_ready")
        bounds_ready = sem("bounds_ready")
        bounds_out = sem("bounds_out")
        bounds_in = sem("bounds_in")
        LOADS1 = 7

        onehot_hi = B1.take([NC, HI], BF16)

        sweep0.place(dst_f, lo_f, onehot_hi, basis.rearrange("p c a b -> p c (a b)"), table0, W1b)

        B2, W2 = regions()
        A = B2.take([NB, NP], F16)
        W2.at = W1_keep
        onehot_src = W2.take([SRC_BUFS, NP], BF16)
        onehot_dst = W2.take([SRC_BUFS, P], BF16)
        counts = A[:, :, (NB - 1) * P:NB * P]

        def edge_buffers(m):
            slot = bass.ds(m % SRC_BUFS, 1)
            return [t[:, slot, :].rearrange("p a c -> p (a c)") for t in (onehot_dst, onehot_src)]

        a_loops = sem("a_loops_added")
        a_ready = sem("a_onehots_ready")
        a_used = sem("a_onehots_used")
        a_counts = sem("a_counts_copied")
        a_turned = sem("a_turned")
        a_stored = sem("a_stored")
        TURN = [(g * 8, min(8, NB - g * 8)) for g in range(-(-NB // 8))]

        B3, W3 = regions()
        W3.at = NB * F * 2
        hn = Region(work, WORK).take([NB, F], F32)
        disB = W3.take([NP], F32, parts=96)
        scaled = [iota[0:96, i * 2 * BANK:(i + 1) * 2 * BANK].bitcast(F32) for i in range(3)]
        xT = W3.take([BANK], F32, parts=F1)
        Hin = W3.take([NB, 3, F], BF16)
        Hmid = W3.take([NB, 3, F2], BF16)
        Hout = W3.take([NB, 3, F], BF16)
        dis = W3.take([NB], F32)
        W1s = W3.take([96], F32, parts=3 * F)
        S2 = W3.take([F2], F32, parts=96)
        S3 = W3.take([F], F32, parts=3 * F)
        W2w = W3.take([F2], F32, parts=F1)
        W3w = W3.take([F], F32, parts=F2)
        b1t = W3.take([1], F32, parts=F1)
        b2t = W3.take([1], F32, parts=F2)
        b3all = W3.take([LAYERS, F], F32)
        gtmp = W3.take([4, F2], F32)
        grest = W3.take([4, F2], F32)
        z = W3.take([4, F], F32)
        zs = W3.take([4, 4], F32)
        x3 = hn
        lntmp3 = Hmid.rearrange("p b i f -> p (b i f)").bitcast(F32)[:, 0:NB * F].rearrange("p (b f) -> p b f", f=F)
        ones96 = W3.take([96], BF16)

        l_w = sem("l_weights")
        l_wfree = sem("l_weights_free")
        l_main = sem("l_main")
        l_scaled = sem("l_scaled")
        l_z = sem("l_z")
        l_relu = sem("l_relu")
        l_g = sem("l_g")
        l_gfree = sem("l_g_bank_free")
        l_h = sem("l_h")
        l_b3 = sem("l_b3")
        l_mx = sem("l_softmax_in")
        l_ex = sem("l_softmax_exp")
        d_ones = sem("d_ones")
        d_main = sem("d_main")
        d_deg = sem("d_deg")
        d_sqrt = sem("d_sqrt")
        d_inv = sem("d_inv")
        d_node = sem("d_node")
        h_in = sem("h_in")
        WDMAS = 7

        B4, W4 = regions()
        h2T = B4.take([NP], F32, parts=F)
        aggT = B4.take([NP], F32, parts=F)
        uT = B4.take([NP], F32, parts=F)
        attr8 = B4.take([NC, 8], F32)
        table2 = B4.take([NB, 3, 128], BF16)
        onehot_hi2 = B4.take([NC, HI], BF16)
        src_i2 = B4.take([NC], I32)
        agg_sb = B4.take([LO], F32)
        aggn = B4.take([NB, F], F32)
        u = B4.take([NB, F], F32)
        vprod = B4.take([2, 256], F32)
        wmt = B4.take([128], F32, parts=F)
        wml = B4.take([F], F32, parts=F)
        wut = B4.take([256], F32, parts=F)
        wul = B4.take([F], F32, parts=F)
        h2 = Region(work, WORK).take([NB, F], F32)
        W4.at = 2 * NB * F * 2
        dst_f4 = W4.take([NC], F32)
        lo_f4 = W4.take([NC], F32)
        mark4 = W4.at
        hi_f4 = W4.take([NC], F32)
        tmp_c4 = W4.take([NC], F32)
        rest4 = W4.take([2, 256], F32)
        dst_i4 = W4.take([NC], I32)
        tmp_src4 = W4.take([NC], F32)
        W4b = Region(work, WORK)
        W4b.at = mark4
        sweep2.place(dst_f4, lo_f4, onehot_hi2, attr8, table2, W4b)

        agg_sb0 = Region(big, NB * NP)
        agg_sb0.at = NP * 2
        agg0 = agg_sb0.take([LO], F32)
        aggT0 = agg_sb0.take([NP], F32, parts=F)

        B5, W5 = regions()
        ident_bf = B5.take([P], BF16)
        h3_parts = B5.take([NB, 3, F], BF16)
        h3T_parts = B5.take([NP], BF16, parts=3 * F)
        attr16 = B5.take([NC, F], F32)
        gathered_at = B5.at
        gathered = B5.take([NC, GROW], F32)
        blocks_out = Region(big, NB * NP)
        blocks_out.at = gathered_at
        rows_sb = [blocks_out.take([NR, GROW], F32) for _ in range(ROWBUFS)]
        row_no = B5.take([NC], I32)
        src_f5 = B5.take([NC], F32)
        att_e = B5.take([NC], F32)
        type_f = B5.take([NC], F32)
        rel = B5.take([256], F32, parts=NR)
        wrel = B5.take([NR, GROW], F32, parts=3 * F)
        wrel_parts = [B5.take([NR, GROW], BF16, parts=3 * F) for _ in range(3)]
        wrel_rest = rows_sb[-1][0:3 * F]
        wct = B5.take([NR], F32, parts=NBASE)
        wv = B5.take([256], F32, parts=NBASE)
        ws = B5.take([F], F32, parts=F)
        wa = B5.take([3], F32, parts=F)
        wab = B5.take([2, P], F32, parts=F)
        ws3 = B5.take([3, F], F32, parts=F)
        a2b = B5.take([F], F32)
        a3b = B5.take([F], F32)
        att_d = B5.take([NB], F32)
        h3 = Region(work, WORK).take([NB, F], F32)
        W5.at = 2 * NB * F * 2
        dst_f5 = W5.take([NC], F32)
        zero5 = W5.take([P], F32)
        mark5 = W5.at
        e_chunk = W5.take([101, F], F32)
        W5b = Region(work, WORK)
        W5b.at = mark5
        onehot5 = W5b.take([QS, P], F32)
        pay5 = W5b.take([QS, 2, F], F32)
        es5 = W5b.take([QS], F32)
        sum5 = W5b.take([F], F32)
        stage = [W5b.take([GQ, GROW], F32) for _ in range(2)]
        stage_idx = [W5b.take([GQ], I32) for _ in range(2)]
        r_edges = sem("r_edges_ready")
        r_agg = sem("r_agg_done")
        r_out = sem("r_out_added")
        r_gath = [sem(f"r_gather_{i}") for i in range(2)]
        r_kept = sem("r_rows_kept")
        r_idx = sem("r_row_numbers_staged")
        r_started = sem("r_gathers_started")
        t_psum = sem("t_products_ready")
        t_act = sem("t_act_copied")
        t_dve = sem("t_dve_copied")
        t_out = [sem(f"t_rows_out_{i}") for i in range(ROWBUFS)]
        load5 = sem("load5")
        rel_psum = sem("rel_psum")
        rel_sb = sem("rel_sb")
        rel_out = sem("rel_out")
        rel_in = sem("rel_in")
        att_psum = sem("att_psum")
        att_sb = sem("att_sb")
        h3_split = sem("h3_split")
        wrel_split = sem("wrel_split")
        load5w = sem("load5_weights")
        load4 = sem("load4")
        upd = sem("upd")
        updv = sem("updv")
        upda = sem("upda")
        out_sem = sem("out_sem")

        block = ctx.enter_context(nc.Block())

        @block.sync
        def _(sp):
            def ld(dst, src, s):
                sp.dma_start(dst, src).then_inc(s, 16)
            ld(dst_rows_i, dstrow_in, loaded)
            ld(x[:], x_in, loaded)
            ld(dst_i, dst_in, loaded)
            ld(src_i, src_in, loaded)
            ld(attr2, attr2_in, loaded)
            ld(w0.rearrange("i (k o) -> i k o", o=F), w0_in.rearrange("k i o -> i k o"), loaded)
            sp.wait_ge(rng_copied, 1)
            ld(range_dram.rearrange("k (p t) -> p k t", t=RC), col_mm, rng_out)
            sp.wait_ge(rng_out, 16)
            ld(col_rng, range_dram.partition_broadcast(NB), rng_in)
            sp.wait_ge(bounds_ready, 1)
            ld(table_dram, bounds_i, bounds_out)
            sp.wait_ge(bounds_out, 16)
            ld(steps_row[0:1, :], table_dram.rearrange("(a b) k -> a (b k)", a=1), bounds_in)
            sp.wait_ge(bounds_in, 16)
            phase_end(sp)
            phase_end(sp)
            sync_regroup(sp, agg0, aggT0, 1)
            phase_end(sp)
            phase_end(sp)
            phase_end(sp)
            ld(b3all, b3_in.partition_broadcast(P), l_b3)
            with sp.Fori(0, LAYERS) as l:
                one = bass.ds(l, 1)
                sp.wait_ge(l_wfree, l + 1)
                for i in range(3):
                    ld(W1s[i * F:(i + 1) * F, 0:F1], w1_in[one, :, :].rearrange("a i o -> (a i) o"), l_w)
                ld(W2w, w2_in[one, :, :].rearrange("a i o -> (a i) o"), l_w)
                ld(W3w, w3_in[one, :, :].rearrange("a i o -> (a i) o"), l_w)
                ld(b1t, b1_in[one, :].rearrange("a (i o) -> (a i) o", o=1), l_w)
                ld(b2t, b2_in[one, :].rearrange("a (i o) -> (a i) o", o=1), l_w)
            phase_end(sp)
            ld(dst_i4, dst_in, load4)
            ld(src_i2, src_in, load4)
            ld(attr8, attr8_in, load4)
            ld(wmt, wmt_in.rearrange("i j h -> i (j h)"), load4)
            ld(wml, wml_in, load4)
            ld(wut, wut_in.rearrange("i h k -> i (h k)"), load4)
            ld(wul, wul_in, load4)
            phase_end(sp)
            phase_end(sp)
            sync_regroup(sp, agg_sb, aggT, 2)
            phase_end(sp)
            ld(wct, wct_in, load5w)
            ld(wv.rearrange("b (i o) -> b i o", o=F), wv_in.rearrange("i b o -> b i o"), load5w)
            ld(ws, ws_in, load5w)
            ld(wa, wa_in, load5w)
            ld(row_no, src_in, load5)
            ld(type_f.bitcast(I32), type_in, load5)
            ld(attr16, attr16_in, load5)
            sp.wait_ge(rel_sb, 1)
            ld(rel_dram.rearrange("(i r o) -> r i o", i=F, r=NR), rel.rearrange("r (i o) -> r i o", o=F), rel_out)
            sp.wait_ge(rel_out, 16)
            for k in range(3):
                ld(wrel[k * F:(k + 1) * F, :, 0:F], rel_dram.rearrange("(r i o) -> i r o", i=F, r=NR), rel_in)
            for b in range(NB):
                sp.wait_ge(t_act, 2 * b + 2)
                sp.wait_ge(t_dve, b + 1)
                ld(rows_dram[b * P * NR:(b + 1) * P * NR, :].rearrange("(p r) c -> p r c", r=NR),
                   rows_sb[b % ROWBUFS], t_out[b % ROWBUFS])
            for i in range(ROWBUFS):
                sp.wait_ge(t_out[i], 16 * len(range(i, NB, ROWBUFS)))
            phase_end(sp)
            phase_end(sp)
            full = N // P
            ld(out[0:full * P, :].rearrange("(b p) c -> p b c", p=P), x[:, 0:full, :], out_sem)
            ld(out[full * P:N, :], x[0:N - full * P, full, :], out_sem)
            sp.wait_ge(out_sem, 32)

        @block.gpsimd
        def _(g):
            g.iota(iota[:], [[1, NP]], base=-HALF, channel_multiplier=0, allow_small_or_imprecise_dtypes=True)
            g.iota(col_no, [[1, NC]], base=1, channel_multiplier=0, allow_small_or_imprecise_dtypes=True)
            g.iota(col_left, [[-1, NC]], base=NC, channel_multiplier=0, allow_small_or_imprecise_dtypes=True)
            g.iota(thr[:, 0:1], [[1, 1]], base=0, channel_multiplier=P, allow_small_or_imprecise_dtypes=True)
            g.iota(thr[:, 1:2], [[1, 1]], base=P - 1, channel_multiplier=P, allow_small_or_imprecise_dtypes=True)
            g.drain()
            g.memset(ident[:], 0.0)
            g.memset(before, 1.0)
            for j in range(4):
                g.memset(centers[:, j:j + 1], -1.0 + 2.0 * j / 3.0)
            g.drain()
            g.affine_select(out=ident[:], in_=ident[:], compare_op=ALU.not_equal, fill=1.0, base=0,
                            pattern=[[-1, P]], channel_multiplier=1)
            g.affine_select(out=before, in_=before, compare_op=ALU.is_gt, fill=0.0, base=0,
                            pattern=[[1, NB]], channel_multiplier=-1)
            g.drain()
            g.tensor_copy(ident_h[:], ident[:])
            g.drain().then_inc(consts, 1)
            phase_end(g)
            sweep0.pool(g)
            phase_end(g)
            phase_end(g)
            phase_end(g)
            phase_end(g)
            phase_end(g)
            g.iota(iota[:], [[1, NP]], base=-HALF, channel_multiplier=0, allow_small_or_imprecise_dtypes=True)
            phase_end(g)
            sweep2.pool(g)
            phase_end(g)
            phase_end(g)
            g.memset(zero5, 0.0)
            phase_end(g)

            def gather(i, group):
                g.wait_ge(r_kept, (group + 1) * GQ)
                g.tensor_copy(stage_idx[i], row_no[:, bass.ds(group * GQ, GQ)]).then_inc(r_idx, 1)
                g.wait_ge(r_idx, group + 1)
                g.sem_inc(r_started, 1)
                for q in range(GQ):
                    g.indirect_dma_start(out=stage[i][:, q, :], out_offset=None, in_=rows_dram,
                                         in_offset=bass.IndirectOffsetOnAxis(ap=stage_idx[i][:, q:q + 1], axis=0)
                                         ).then_inc(r_gath[i], 16)

            with g.Fori(0, NG // 2) as k:
                gather(0, k * 2)
                gather(1, k * 2 + 1)
            gather(0, NG - 1)
            phase_end(g)

        @block.scalar
        def _(a):
            act_layernorm(a, 1)
            act_copy_nodes(a, hT, 1)
            phase_end(a)
            sweep0.act(a)
            phase_end(a)
            phase_end(a)
            def store_turned(before, column):
                for g, (s0, sn) in enumerate(TURN):
                    a.wait_ge(a_turned, before + (g + 1))
                    a.activation(A[:, s0:s0 + sn, column], bank(7, [sn, P], F16), ACT.Copy).then_inc(a_stored, 1)

            with a.Fori(0, NB) as b:
                _, last, base = pair_table(a, b)
                prev = (b + (NB - 1)) % NB
                store_turned(b * len(TURN), bass.ds(prev * P, P))
                a.drain()
                a.wait_ge(a_used, (base + last) * PS + PS + SRC_BUFS)
                for j, (c0, cn) in enumerate(CHUNKS):
                    a.activation(counts[:, c0 // P:(c0 + cn) // P, :], bank(j, [cn // P, P]), ACT.Copy).then_inc(a_counts, 1)
            store_turned(NB * len(TURN), slice((NB - 1) * P, NB * P))
            phase_end(a)
            for j, (c0, cn) in enumerate(CHUNKS):
                a.wait_ge(d_deg, j + 1)
                a.activation(disB[:, c0:c0 + cn], disB[:, c0:c0 + cn], ACT.Sqrt).then_inc(d_sqrt, 1)
            act_layernorm(a, 2)
            phase_end(a)
            with a.Fori(0, LAYERS) as l:
                a.wait_ge(l_w, l * (16 * WDMAS) + 16 * WDMAS)
                for conv, (width, bias) in enumerate(((F1, b1t), (F2, b2t))):
                    for j, (c0, cn) in enumerate(GCHUNKS):
                        k = conv * NCH + j
                        a.wait_ge(l_z, l * (2 * NCH) + (k + 1))
                        a.activation(xT[0:width, 0:cn], bank(3, [cn], parts=width), ACT.Relu,
                                     bias=bias[0:width, :]).then_inc(l_relu, 1)
                for j, (c0, cn) in enumerate(GCHUNKS):
                    a.wait_ge(l_mx, l * NCH + (j + 1))
                    a.activation(z[:, 0:cn // P, :], z[:, 0:cn // P, :], ACT.Exp).then_inc(l_ex, 1)
            phase_end(a)
            act_layernorm(a, 3)
            act_copy_nodes(a, h2T, 2)
            phase_end(a)
            sweep2.act(a)
            phase_end(a)
            a.wait_ge(updv, 1 + len(GROUPS))
            a.activation(u, u, ACT.Silu, scale=1.0 / float(np.sqrt(F * F))).then_inc(upda, 1)
            a.wait_ge(upd, 3 + len(GROUPS))
            a.activation(uT, bank(0, [NP], parts=F, count=7), ACT.Copy).then_inc(upda, 1)
            phase_end(a)
            act_layernorm(a, 4)
            a.wait_ge(hT_psum, 3)
            a.activation(h3T_parts, bank(0, [NP], BF16, parts=3 * F, count=4), ACT.Copy).then_inc(hT_done, 1)
            for b in range(NB):
                for c in range(2):
                    a.wait_ge(t_psum, 3 * b + c + 1)
                    if b >= ROWBUFS:
                        a.wait_ge(t_out[b % ROWBUFS], 16 * (b // ROWBUFS))
                    a.activation(rows_sb[b % ROWBUFS][:, c * RCHUNK:(c + 1) * RCHUNK, :],
                                 bank((3 * b + c) % 6, [RCHUNK, GROW]), ACT.Copy).then_inc(t_act, 1)
            phase_end(a)
            def keep(i, group, landed):
                a.wait_ge(r_gath[i], landed)
                a.activation(gathered[:, bass.ds(group * GQ, GQ), :], stage[i], ACT.Copy).then_inc(r_kept, GQ)

            a.sem_inc(r_kept, 2 * GQ)
            with a.Fori(0, NG // 2) as k:
                keep(0, k * 2, k * (16 * GQ) + 16 * GQ)
                keep(1, k * 2 + 1, k * (16 * GQ) + 16 * GQ)
            keep(0, NG - 1, 16 * GQ * (NG // 2 + 1))
            phase_end(a)

        @block.tensor
        def _(pe):
            pe.wait_ge(consts, 1)
            pe.wait_ge(count_ready, 1)
            pe.matmul(bank(7, [2])[0:NB, 0:1], before, bounds[:, 3:4], start=True, stop=True)
            pe.matmul(bank(7, [2])[0:NB, 1:2], before, bounds[:, 7:8], start=True, stop=True).then_inc(base_ready, 1)
            pe.wait_ge(ln_done, 1)
            pe_transpose_nodes(pe, h0, 1)
            pe_table(pe, hT, w0, 256, 1)
            phase_end(pe)
            sweep0.pe(pe)
            phase_end(pe)
            pe.wait_ge(agg_moved, 16 * HI)
            for b in range(NB):
                mm = pe.matmul(bank(4, [NB, F])[:, b, :], aggT0[:, b * P:(b + 1) * P], ident[0:F, 0:F],
                               start=True, stop=True)
            mm.then_inc(upd, 1)
            phase_end(pe)
            pe.sem_inc(a_used, SRC_BUFS)

            def turn(g, before):
                s0, sn = TURN[g]
                pe.wait_ge(a_stored, before + g)
                for t in range(sn):
                    mm = pe.transpose(bank(7, [sn, P], F16)[:, t, :],
                                      counts[:, s0 + t, :], ident_h[:])
                mm.then_inc(a_turned, 1)

            def count_edges(m, first=None):
                pe.wait_ge(a_ready, m + 1)
                of_dst, of_src = edge_buffers(m)
                for j, (c0, cn) in enumerate(CHUNKS):
                    if first is not None:
                        pe.wait_ge(a_counts, first + j)
                    mm = pe.matmul(bank(j, [cn]), of_dst, of_src[:, c0:c0 + cn],
                                   start=first is not None, stop=True, skip_group_check=True)
                mm.then_inc(a_used, 1)

            with pe.Fori(0, NB) as b:
                _, last, base = pair_table(pe, b)
                for q in range(2 * PS):
                    count_edges(base * PS + q, b * NCH + 1 if q == 0 else None)
                    if q == 0:
                        pe.wait_ge(a_loops, b + 1)
                    turn(q, b * len(TURN) + 1)
                with pe.Fori(2, last + 1) as i:
                    for q in range(PS):
                        count_edges((base + i) * PS + q)
            pe.wait_ge(a_loops, NB + 1)
            for g in range(len(TURN)):
                turn(g, NB * len(TURN) + 1)
            phase_end(pe)
            pe.wait_ge(d_ones, 1)
            for j, (c0, cn) in enumerate(CHUNKS):
                for b in range(NB):
                    mm = pe.matmul(bank(j, [cn], parts=96), ones96, A[:, b, c0:c0 + cn],
                                   start=(b == 0), stop=(b == NB - 1))
                mm.then_inc(d_main, 1)
            pe.wait_ge(d_inv, NCH)
            for b in range(NB):
                mm = pe.matmul(bank(7, [NB])[:, b:b + 1], disB[0:1, b * P:(b + 1) * P], ident[0:1, 0:1],
                               start=True, stop=True)
            mm.then_inc(d_node, 1)
            phase_end(pe)
            with pe.Fori(0, LAYERS) as l:
                for conv, (H, width) in enumerate(((Hin, F), (Hmid, F2), (Hout, F))):
                    rows = 3 * width

                    def weigh(j):
                        c0, cn = GCHUNKS[j]
                        k = conv * NCH + j
                        pe.wait_ge(l_scaled, l * (3 * NCH) + (k + 1))
                        if k == 0:
                            pe.wait_ge(l_w, l * (16 * WDMAS) + 16 * WDMAS)
                        if conv < 2:
                            w, m = ((W1s, 96), (S2, F2))[conv]
                            pe.matmul(bank(3, [cn], parts=m), w[0:rows, 0:m], scaled[k % 3][0:rows, 0:cn],
                                      start=True, stop=True).then_inc(l_z, 1)

                    def finish(j):
                        c0, cn = GCHUNKS[j]
                        k = conv * NCH + j
                        if conv < 2:
                            pe.wait_ge(l_relu, l * (2 * NCH) + (k + 1))
                        pe.wait_ge(l_gfree, l * (3 * NCH) + (k + 1))
                        for t in range(cn // P):
                            cols = slice(t * P, (t + 1) * P)
                            if conv == 0:
                                mm = pe.matmul(bank(4, [4, F2])[:, t, :], xT[0:F1, cols], W2w, start=True, stop=True)
                            elif conv == 1:
                                mm = pe.matmul(bank(4, [4, F2])[:, t, 0:F], xT[0:F2, cols], W3w, start=True, stop=True)
                            else:
                                mm = pe.matmul(bank(4, [4, F2])[:, t, 0:F], scaled[k % 3][0:rows, cols],
                                               S3, start=True, stop=True)
                        mm.then_inc(l_g, 1)

                    def accumulate(j, blocks):
                        c0, cn = GCHUNKS[j]
                        for b in blocks:
                            mm = pe.matmul(bank(GBANKS[j], [cn], parts=rows),
                                           H[:, b, :, :].rearrange("p a f -> p (a f)"),
                                           A[:, b, c0:c0 + cn], start=(b == NB - 1), stop=(b == NB - 2))
                        return mm

                    def written(j):
                        pe.wait_ge(l_h, l * (3 * NCH) + (conv * NCH + j + 2))

                    for j, (c0, cn) in enumerate(GCHUNKS[:-1]):
                        written(j)
                        for chunk in range(TOGETHER):
                            accumulate(chunk, range(c0 // P, (c0 + cn) // P))
                    written(NCH - 1)
                    late = range(GCHUNKS[-1][0] // P, NB - 1)
                    for j in range(NCH):
                        if j == NCH - 1:
                            pe.wait_ge(l_scaled, l * (3 * NCH) + (conv * NCH + 4))
                        blocks = late if j < TOGETHER else [NB - 1, *range(NB - 1)]
                        accumulate(j, blocks).then_inc(l_main, 1)
                        if j >= 2:
                            finish(j - 2)
                        if j >= 1:
                            weigh(j - 1)
                    finish(NCH - 2)
                    weigh(NCH - 1)
                    finish(NCH - 1)
            phase_end(pe)
            pe.wait_ge(ln_done, 3)
            pe_transpose_nodes(pe, h2, 2)
            pe.wait_ge(load4, 16 * 7)
            pe_table(pe, h2T, wmt, 128, 2)
            phase_end(pe)
            sweep2.pe(pe)
            phase_end(pe)
            pe.wait_ge(agg_moved, 16 * 2 * HI)
            for b in range(NB):
                mm = pe.matmul(bank(7, [NB, F])[:, b, :], aggT[:, b * P:(b + 1) * P], wml, start=True, stop=True)
            mm.then_inc(upd, 1)
            for g, m in GROUPS:
                if g >= 7:
                    pe.wait_ge(updv, 1 + g - 6)
                for t in range(m):
                    b = 2 * g + t
                    mm = pe.matmul(bank(g % 7, [2, 256])[:, t, :], h2T[:, b * P:(b + 1) * P], wut, start=True, stop=True)
                mm.then_inc(upd, 1)
            pe.wait_ge(upda, 1)
            for b in range(NB):
                mm = pe.transpose(bank(0, [NP], parts=F, count=7)[:, b * P:(b + 1) * P], u[:, b, :], ident[:])
            mm.then_inc(upd, 1)
            pe.wait_ge(upda, 2)
            for b in range(NB):
                mm = pe.matmul(bank(7, [NB, F])[:, b, :], uT[:, b * P:(b + 1) * P], wul, start=True, stop=True)
            mm.then_inc(upd, 1)
            phase_end(pe)
            pe.wait_ge(load5w, 16 * 4)
            pe.matmul(bank(7, [256], parts=NR), wct, wv, start=True, stop=True).then_inc(rel_psum, 1)
            pe.wait_ge(rel_sb, 1)
            pe.wait_ge(att_sb, 1)
            pe.matmul(bank(7, [1], parts=3 * F), ws3.rearrange("o k i -> o (k i)"), wa[:, 0:1], start=True, stop=True)
            pe.matmul(bank(7, [32])[:, 16:32], wab[:, 0, :], ws, start=True, stop=True)
            pe.matmul(bank(7, [48])[:, 32:48], wab[:, 1, :], ws, start=True, stop=True).then_inc(att_psum, 1)
            pe.wait_ge(h3_split, 1)
            for b in range(NB):
                mm = pe.transpose(bank(0, [NP], BF16, parts=3 * F, count=4)[:, b * P:(b + 1) * P],
                                  h3_parts[:, b, :, :].rearrange("p i f -> p (i f)"), ident_bf)
            mm.then_inc(hT_psum, 1)
            pe.wait_ge(hT_done, 3)
            pe.wait_ge(wrel_split, 1)
            for b in range(NB):
                for c in range(3):
                    if b >= 2 and c < 2:
                        pe.wait_ge(t_act, 2 * (b - 2) + c + 1)
                    elif b >= 2:
                        pe.wait_ge(t_dve, b - 1)
                    for k in range(3):
                        mm = pe.matmul(bank((3 * b + c) % 6, [RCHUNK * GROW]), h3T_parts[:, b * P:(b + 1) * P],
                                       wrel_parts[k][:, c * RCHUNK:(c + 1) * RCHUNK, :].rearrange("i r c -> i (r c)"),
                                       start=(k == 0), stop=(k == 2))
                    mm.then_inc(t_psum, 1)
            phase_end(pe)
            pe.sem_inc(r_agg, 2)
            with pe.Fori(0, NB) as b:
                pe.wait_ge(r_out, b + 1)
                table = block_table(pe, b)
                pe.matmul(bank(0, [2 * F]), zero5, zero5[:, 0:2 * F], start=True, stop=True, skip_group_check=True)

                for s, n in block_steps(pe, table):
                    for r in range(2):
                        pe.wait_ge(r_edges, n * 2 + (r + 1))
                        for q in (2 * r, 2 * r + 1):
                            mm = pe.matmul(bank(0, [2 * F]), onehot5[:, q, :],
                                           pay5[:, q, :, :].rearrange("p a f -> p (a f)"),
                                           start=False, stop=True, skip_group_check=True)
                        mm.then_inc(r_agg, 1)
            phase_end(pe)

        @block.vector
        def _(v):
            v.wait_ge(loaded, 16 * 6)
            v.wait_ge(consts, 1)
            v.tensor_copy(dst_rows, dst_rows_i)
            v.drain()
            rows = dst_rows.rearrange("p (t e) -> p t e", t=RC)
            v.tensor_reduce(col_mm[:, 0, :], rows, AX.X, ALU.max)
            v.tensor_reduce(col_mm[:, 1, :], rows, AX.X, ALU.min)
            v.drain().then_inc(rng_copied, 1)
            dve_layernorm(v, h0, lntmp0, 1)
            v.wait_ge(rng_in, 16)
            first, end, cols = (found[:, k:k + 1] for k in range(3))
            v.tensor_scalar(flags, col_rng[:, 0, :], thr[:, 0:1], None, ALU.is_ge)
            v.drain()
            v.tensor_tensor(flags, flags, col_left, ALU.mult)
            v.drain()
            v.tensor_reduce(first, flags, AX.X, ALU.max)
            v.drain()
            v.tensor_scalar(first, first, -1.0, float(NC), ALU.mult, ALU.add)
            v.drain()
            v.tensor_scalar(flags, col_rng[:, 1, :], thr[:, 1:2], None, ALU.is_le)
            v.drain()
            v.tensor_tensor(flags, flags, col_no, ALU.mult)
            v.drain()
            v.tensor_reduce(end, flags, AX.X, ALU.max)
            v.drain()
            v.tensor_tensor(cols, end, first, ALU.subtract)
            v.drain()
            for at, unit, least in ((0, QS, 2), (4, PS, 3)):
                start, count = bounds[:, at:at + 1], bounds[:, at + 3:at + 4]
                v.tensor_scalar(count, cols, 1.0 / unit, (unit - 1) / unit - 0.375, ALU.mult, ALU.add)
                v.drain()
                v.tensor_scalar(count, count, float(2 ** 23), None, ALU.add)
                v.drain()
                v.tensor_scalar(count, count, -float(2 ** 23), float(least), ALU.add, ALU.max)
                v.drain()
                v.tensor_scalar(start, count, -float(unit), float(NC), ALU.mult, ALU.add)
                v.drain()
                v.tensor_tensor(start, start, first, ALU.min)
            v.drain().then_inc(count_ready, 1)
            v.wait_ge(base_ready, 1)
            for k, at in enumerate((0, 4)):
                v.tensor_copy(bounds[:, at + 2:at + 3], bank(7, [2])[0:NB, k:k + 1])
                v.tensor_scalar(bounds[:, at + 1:at + 2], bounds[:, at + 3:at + 4], -1.0, None, ALU.add)
            v.drain()
            v.tensor_copy(bounds_i, bounds)
            v.drain().then_inc(bounds_ready, 1)
            v.tensor_copy(dst_f, dst_i)
            v.tensor_copy(src_c, src_i)
            v.drain()

            def split_src(src_f, hi, lo, hi_onehot, tmp):
                v.tensor_scalar(hi, src_f, float(LO), None, ALU.is_ge)
                for k in range(2, HI):
                    v.tensor_scalar(tmp, src_f, float(LO * k), None, ALU.is_ge)
                    v.drain()
                    v.tensor_tensor(hi, hi, tmp, ALU.add)
                    v.drain()
                v.tensor_scalar(tmp, hi, -float(LO), None, ALU.mult)
                v.drain()
                v.tensor_tensor(lo, src_f, tmp, ALU.add)
                for k in range(HI):
                    v.tensor_scalar(hi_onehot[:, :, k], hi, float(k), None, ALU.is_equal)
                v.drain()

            split_src(src_c, hi_f, lo_f, onehot_hi, tmp_c)
            v.tensor_scalar(attr2, attr2, -1.0, 1.0, ALU.max, ALU.min)
            v.tensor_tensor(tmp_c, src_c, dst_f, ALU.not_equal)
            v.drain()
            for j in range(4):
                v.tensor_scalar(hats[:, :, :, j], attr2, centers[:, j:j + 1], None, ALU.subtract)
            v.drain()
            rising = basis.rearrange("p c a b -> p (c a b)")[:, 0:NC * 8].rearrange("p (c a b) -> p c a b", a=2, b=4)
            v.tensor_scalar(rising, hats, 1.5, 1.0, ALU.mult, ALU.add)
            v.drain()
            v.tensor_scalar(hats, hats, -1.5, 1.0, ALU.mult, ALU.add)
            v.drain()
            v.tensor_tensor(hats, hats, rising, ALU.min)
            v.drain()
            v.tensor_scalar(hats, hats, 0.0, None, ALU.max)
            v.drain()
            v.tensor_tensor(hats[:, :, 1, :], hats[:, :, 1, :], wide(tmp_c, 4), ALU.mult)
            v.drain()
            v.tensor_tensor(basis, hats[:, :, 0, :].unsqueeze(3).to_broadcast([P, NC, 4, 4]),
                            hats[:, :, 1, :].unsqueeze(2).to_broadcast([P, NC, 4, 4]), ALU.mult)
            v.tensor_scalar(src_c, src_c, -float(HALF), None, ALU.add)
            v.tensor_scalar(dst_f, dst_f, -float(HALF), None, ALU.add)
            v.wait_ge(bounds_out, 16)
            dve_table(v, table0, rest, 256, 1)
            phase_end(v)
            sweep0.dve(v)
            phase_end(v)
            v.tensor_copy(agg0, sweep0.agg)
            v.drain().then_inc(agg_copied, 1)
            v.wait_ge(upd, 1)
            v.scalar_tensor_tensor(x[:], bank(4, [NB, F]), 1.0 / 128.0, x[:], ALU.mult, ALU.add)
            v.drain()
            phase_end(v)
            v.memset(counts, 0.0)
            v.drain()
            v.sem_inc(a_counts, NCH)
            v.sem_inc(a_stored, 1)

            def edge_onehots(b, c, m):
                of_dst, of_src = edge_buffers(m)
                v.wait_ge(a_used, m + 1)
                v.tensor_scalar(of_dst, iota[:, bass.ds(b * P, P)], dst_f[:, bass.ds(c, 1)], None, ALU.is_equal)
                v.tensor_scalar(of_src, iota[:], src_c[:, bass.ds(c, 1)], None, ALU.is_equal).then_inc(a_ready, 1)

            def add_loops(before, block):
                v.wait_ge(a_counts, before)
                own = counts[:, block, :]
                v.tensor_tensor(own, own, ident_h[:].unsqueeze(1), ALU.add).then_inc(a_loops, 1)

            with v.Fori(0, NB) as b:
                first, last, base = pair_table(v, b)
                prev = (b + (NB - 1)) % NB
                for q in range(2 * PS):
                    edge_onehots(b, first + q, base * PS + q)
                    if q == 1:
                        add_loops(b * NCH + NCH, bass.ds(prev, 1))
                with v.Fori(2, last + 1) as i:
                    c = column(first + i * PS, NC - PS)
                    for q in range(PS):
                        edge_onehots(b, c + q, (base + i) * PS + q)
            add_loops(NB * NCH + NCH, slice(NB - 1, NB))
            phase_end(v)
            v.memset(ones96, 1.0).then_inc(d_ones, 1)
            v.memset(W1s, 0.0)
            for j, (c0, cn) in enumerate(CHUNKS):
                v.wait_ge(d_main, j + 1)
                v.tensor_scalar(disB[:, c0:c0 + cn], bank(j, [cn], parts=96), 1.0, None, ALU.max).then_inc(d_deg, 1)
            for j, (c0, cn) in enumerate(CHUNKS):
                v.wait_ge(d_sqrt, j + 1)
                v.reciprocal(disB[:, c0:c0 + cn], disB[:, c0:c0 + cn]).then_inc(d_inv, 1)
            dve_layernorm(v, hn, lntmp3, 2)
            for i in range(3):
                v.tensor_copy(S2[i * F2:(i + 1) * F2, :], ident[i * F2:(i + 1) * F2, i * F2:(i + 1) * F2])
            v.tensor_tensor(S3, ident[0:3 * F, 0:F], ident[0:3 * F, F:2 * F], ALU.add)
            v.drain()
            v.tensor_tensor(S3, S3, ident[0:3 * F, 2 * F:3 * F], ALU.add)
            v.wait_ge(d_node, 1)
            v.tensor_copy(dis, bank(7, [NB]))
            v.drain()

            def parts_of(H, b0, m, src, width, emptied=None):
                t, r = gtmp[:, 0:m, 0:width], grest[:, 0:m, 0:width]
                op = v.tensor_tensor(t, src, wide(dis[:, b0:b0 + m], width), ALU.mult)
                if emptied is not None:
                    op.then_inc(emptied, 1)
                v.drain()
                return split3(v, [H[:, b0:b0 + m, i, :] for i in range(3)], t, r)

            for j, (c0, cn) in enumerate(CHUNKS):
                b0, m = c0 // P, cn // P
                parts_of(Hin, b0, m, hn[:, b0:b0 + m, :], F)
                v.drain()
            v.sem_inc(l_wfree, 1)
            v.sem_inc(l_h, NCH + 1)
            v.sem_inc(l_gfree, 1)
            phase_end(v)
            v.wait_ge(l_b3, 16)
            with v.Fori(0, LAYERS) as l:
                for conv, (H, width) in enumerate(((Hmid, F2), (Hout, F), (Hin, F))):
                    rows = 3 * (F, F2, F)[conv]

                    def scale(j):
                        c0, cn = GCHUNKS[j]
                        k = conv * NCH + j
                        v.wait_ge(l_main, l * (3 * NCH) + (k + 1))
                        v.tensor_tensor(scaled[k % 3][0:rows, 0:cn], bank(GBANKS[j], [cn], parts=rows),
                                        disB[0:rows, c0:c0 + cn], ALU.mult).then_inc(l_scaled, 1)

                    def store(j):
                        c0, cn = GCHUNKS[j]
                        b0, m = c0 // P, cn // P
                        k = conv * NCH + j
                        v.wait_ge(l_g, l * (3 * NCH) + (k + 1))
                        got = bank(4, [4, F2])[:, 0:m, 0:width]
                        if conv < 2:
                            parts_of(H, b0, m, got, width, l_gfree).then_inc(l_h, 1)
                            v.drain()
                            return
                        mx, sm = zs[:, 0:m, 0], zs[:, 0:m, 1]
                        zz = z[:, 0:m, :]
                        b3 = b3all[:, bass.ds(l, 1), :].to_broadcast([P, m, F])
                        v.tensor_tensor(zz, got, b3, ALU.add).then_inc(l_gfree, 1)
                        v.drain()
                        v.tensor_reduce(mx, zz, AX.X, ALU.max)
                        v.drain()
                        v.tensor_tensor(zz, zz, wide(mx, F), ALU.subtract).then_inc(l_mx, 1)
                        v.wait_ge(l_ex, l * NCH + (j + 1))
                        v.tensor_reduce(sm, zz, AX.X, ALU.add)
                        v.drain()
                        v.reciprocal(sm, sm)
                        v.drain()
                        v.tensor_tensor(x3[:, b0:b0 + m, :], zz, wide(sm, F), ALU.mult)
                        v.drain()
                        parts_of(H, b0, m, x3[:, b0:b0 + m, :], F).then_inc(l_h, 1)
                        v.drain()

                    for j in range(NCH):
                        scale(j)
                        if j >= 2:
                            store(j - 2)
                    store(NCH - 2)
                    store(NCH - 1)
                    if conv == 1:
                        v.sem_inc(l_wfree, 1)
            v.tensor_tensor(x[:], x[:], x3, ALU.add)
            v.drain()
            phase_end(v)
            dve_layernorm(v, h2, lntmp, 3)
            v.wait_ge(load4, 16 * 7)
            v.tensor_copy(dst_f4, dst_i4)
            v.tensor_copy(tmp_src4, src_i2)
            v.drain()
            v.tensor_scalar(dst_f4, dst_f4, -float(HALF), None, ALU.add)
            split_src(tmp_src4, hi_f4, lo_f4, onehot_hi2, tmp_c4)
            dve_table(v, table2, rest4, 128, 2)
            phase_end(v)
            sweep2.dve(v)
            phase_end(v)
            v.tensor_copy(agg_sb, sweep2.agg)
            v.drain().then_inc(agg_copied, 1)
            v.wait_ge(upd, 2)
            v.tensor_scalar(aggn, bank(7, [NB, F]), 1.0 / float(np.sqrt(F)), None, ALU.mult)
            v.drain().then_inc(updv, 1)
            for g, m in GROUPS:
                v.wait_ge(upd, 3 + g)
                prod = vprod[:, 0:m, :].rearrange("p t (h k) -> p t h k", k=F)
                v.tensor_tensor(prod, bank(g % 7, [2, 256])[:, 0:m, :].rearrange("p t (h k) -> p t h k", k=F),
                                aggn[:, 2 * g:2 * g + m, :].unsqueeze(3).to_broadcast([P, m, F, F]), ALU.mult)
                v.drain()
                v.tensor_reduce(u[:, 2 * g:2 * g + m, :], prod.rearrange("p t h k -> p t k h"), AX.X, ALU.add
                                ).then_inc(updv, 1)
                v.drain()
            v.tensor_tensor(x[:], x[:], h2, ALU.add)
            v.drain()
            v.wait_ge(upd, 4 + len(GROUPS))
            v.scalar_tensor_tensor(x[:], bank(7, [NB, F]), 1.0 / float(np.sqrt(F)), x[:], ALU.mult, ALU.add)
            v.drain()
            phase_end(v)
            v.tensor_copy(ident_bf, ident[:])
            v.wait_ge(load5w, 16 * 4)
            for k in range(2):
                v.tensor_copy(wab[:, k, :], wa[:, k + 1:k + 2].to_broadcast([F, P]))
            v.tensor_copy(ws3, ws.unsqueeze(1).to_broadcast([F, 3, F]))
            v.drain().then_inc(att_sb, 1)
            v.wait_ge(rel_psum, 1)
            v.tensor_copy(rel, bank(7, [256], parts=NR))
            v.drain().then_inc(rel_sb, 1)
            dve_layernorm(v, h3, lntmp, 4)
            v.drain()
            split3(v, [h3_parts[:, :, i, :] for i in range(3)], h3, lntmp).then_inc(h3_split, 1)
            v.wait_ge(att_psum, 1)
            v.tensor_copy(wrel[:, :, F], bank(7, [1], parts=3 * F).to_broadcast([3 * F, NR]))
            v.tensor_copy(a2b, bank(7, [32])[:, 16:32])
            v.tensor_copy(a3b, bank(7, [48])[:, 32:48])
            v.drain()
            v.wait_ge(rel_in, 16 * 3)
            split3(v, wrel_parts, wrel, wrel_rest).then_inc(wrel_split, 1)
            v.tensor_tensor(lntmp, h3, a3b.unsqueeze(1).to_broadcast([P, NB, F]), ALU.mult)
            v.drain()
            v.tensor_reduce(att_d, lntmp, AX.X, ALU.add)
            v.wait_ge(load5, 16 * 3)
            v.tensor_copy(type_f, type_f.bitcast(I32))
            v.tensor_copy(src_f5, row_no)
            v.drain()
            v.scalar_tensor_tensor(row_no, src_f5, float(NR), type_f, ALU.mult, ALU.add)
            for b in range(NB):
                if b < NC // 101:
                    cols = slice(b * 101, (b + 1) * 101)
                    v.tensor_tensor(e_chunk, attr16[:, cols, :], a2b.unsqueeze(1).to_broadcast([P, 101, F]), ALU.mult)
                    v.drain()
                    v.tensor_reduce(att_e[:, cols], e_chunk, AX.X, ALU.add)
                    v.drain()
                v.wait_ge(t_psum, 3 * b + 3)
                if b >= ROWBUFS:
                    v.wait_ge(t_out[b % ROWBUFS], 16 * (b // ROWBUFS))
                v.tensor_copy(rows_sb[b % ROWBUFS][:, 2 * RCHUNK:3 * RCHUNK, :],
                              bank((3 * b + 2) % 6, [RCHUNK, GROW])).then_inc(t_dve, 1)
            phase_end(v)
            v.sem_inc(r_out, 1)
            with v.Fori(0, NB) as b:
                table = block_table(v, b)
                for s, n in block_steps(v, table):
                    cols = bass.ds(s, QS)
                    v.wait_ge(r_kept, s + (2 * GQ + QS))
                    v.tensor_tensor(es5, att_e[:, cols], gathered[:, cols, F], ALU.add)
                    for r in range(2):
                        half, cols = slice(2 * r, 2 * r + 2), bass.ds(s + 2 * r, 2)
                        v.wait_ge(r_agg, n * 2 + (r + 1))
                        for q in (2 * r, 2 * r + 1):
                            v.tensor_scalar(onehot5[:, q, :], iota[:, bass.ds(b * P, P)],
                                            dst_f5[:, bass.ds(s + q, 1)], None, ALU.is_equal)
                        v.tensor_copy(pay5[:, half, 1, :], gathered[:, cols, 0:F])
                        if r == 0:
                            v.drain()
                        v.tensor_tensor(pay5[:, half, 0, :], gathered[:, cols, 0:F], wide(es5[:, half], F),
                                        ALU.mult).then_inc(r_edges, 1)
                    v.drain()
                v.wait_ge(r_agg, (table[2] + table[1]) * 2 + 4)
                xb = x[:, bass.ds(b, 1), :].rearrange("p a f -> p (a f)")
                v.tensor_tensor(xb, bank(0, [2 * F])[:, 0:F], xb, ALU.add)
                v.tensor_scalar(sum5, bank(0, [2 * F])[:, F:2 * F], att_d[:, bass.ds(b, 1)], None,
                                ALU.mult).then_inc(r_out, 1)
                v.drain()
                v.tensor_tensor(xb, xb, sum5, ALU.add)
                v.drain()
            phase_end(v)


_ORDER = ["x", "src", "dst", "dstrow", "type", "attr2", "attr8", "attr16", "w0", "w1", "b1", "w2", "b2",
          "w3", "b3", "wmt", "wml", "wut", "wul", "ws", "wa", "wv", "wct"]


def kernel(**inputs):
    import numpy as _np
    import concourse.bacc as _bacc
    from concourse import mybir as _mybir
    from concourse.bass_utils import run_bass_kernel_spmd as _run

    i = {k: _np.asarray(v) for k, v in inputs.items()}

    def edges(a, pad):
        full = _np.full((NC * P,) + a.shape[1:], pad, a.dtype)
        full[:E] = a
        return _np.ascontiguousarray(_np.moveaxis(full.reshape((NC, P) + a.shape[1:]), 1, 0))

    nodes = _np.zeros((NP, F), i["x"].dtype)
    nodes[:N] = i["x"]
    absent = 2 * NP - 1
    dstrow = _np.full((NC * P,), absent, i["dst"].dtype)
    dstrow[:E] = i["dst"]
    a = {
        "x": nodes.reshape(NB, P, F).transpose(1, 0, 2), "src": edges(i["src"], 0),
        "dst": edges(i["dst"], absent), "dstrow": dstrow.reshape(RP, RC * P),
        "type": edges(i["edge_type_90"], 0), "attr2": edges(i["edge_attr_2"], 0),
        "attr8": edges(i["edge_attr_8"], 0), "attr16": edges(i["edge_attr_16"], 0),
        "w0": i["L0_gnn_W"], "w1": i["L1_gnn_W1"], "b1": i["L1_gnn_b1"], "w2": i["L1_gnn_W2"],
        "b2": i["L1_gnn_b2"], "w3": i["L1_gnn_W3"], "b3": i["L1_gnn_b3"], "wmt": i["L2_gnn_W_msg_tp"],
        "wml": i["L2_gnn_W_msg_lin"], "wut": i["L2_gnn_W_upd_tp"], "wul": i["L2_gnn_W_upd_lin"],
        "ws": i["L3_gnn_Ws"], "wa": i["L3_gnn_Wa"].reshape(3, F).T,
        "wv": i["L3_gnn_weight"].reshape(F, NBASE, F), "wct": i["L3_gnn_w_comp"].T,
    }
    a = {f"in_{k}": _np.ascontiguousarray(v) for k, v in a.items()}
    nc = _bacc.Bacc("TRN2", target_bir_lowering=False, num_devices=1)
    args = [nc.dram_tensor(f"in_{k}", a[f"in_{k}"].shape, _mybir.dt.from_np(a[f"in_{k}"].dtype),
                           kind="ExternalInput").ap() for k in _ORDER]
    result = nc.dram_tensor("result", (N, F), _mybir.dt.float32, kind="ExternalOutput").ap()
    gnn(nc, *args, result)
    r = _run(nc, [a], core_ids=[0])
    return r.results[0]["result"]
```
